# Optimizing a Trainium2 kernel written in Bass

```python
import numpy as np
import jax
import jax.numpy as jnp

def _softmax(x, axis=-1):
    return jax.nn.softmax(x, axis=axis)

def _gelu(x):
    return jax.nn.gelu(x, approximate=True)

def _silu(x):
    return jax.nn.silu(x)

def _sigmoid(x):
    return jax.nn.sigmoid(x)

def _layernorm(x, axis=-1, eps=1e-05):
    m = jnp.mean(x, axis=axis, keepdims=True)
    v = jnp.var(x, axis=axis, keepdims=True)
    return (x - m) / jnp.sqrt(v + eps)

def _scatter_add(tgt, idx, src, axis=0):
    return tgt.at[idx].add(src)

def _segment_sum(src, seg, n):
    return jax.ops.segment_sum(src, seg, n)
kernel_name = 'mk_seq_preln_d1_jaxref_r8_07338f'

def setup_inputs(seed: int=0):
    np.random.seed(seed)
    _w = jnp.asarray

    def _L0_attn_setup():
        import math
        import jax, jax.numpy as jnp
        import numpy as np
        D_MODEL = 128
        N_HEADS = 16
        D_HEAD = D_MODEL // N_HEADS
        BLOCK = 256
        BATCH = 2
        SEQ = 256

        def _rotate(t, cos, sin):
            t1 = t[..., 0::2]
            t2 = t[..., 1::2]
            r1 = t1 * cos - t2 * sin
            r2 = t1 * sin + t2 * cos
            return jnp.stack([r1, r2], axis=-1).reshape(t.shape)
        key = jax.random.key(seed)
        k1, k2, k3 = jax.random.split(key, 3)
        x = jax.random.normal(k1, (BATCH, SEQ, D_MODEL), dtype=jnp.float32)
        Wqkv = jax.random.normal(k2, (3 * D_MODEL, D_MODEL), dtype=jnp.float32) * 0.02
        Wo = jax.random.normal(k3, (D_MODEL, D_MODEL), dtype=jnp.float32) * 0.02
        log_xi = jnp.full((N_HEADS,), math.log(BLOCK / 2.0), dtype=jnp.float32)
        pi_gate_logit = jnp.full((N_HEADS,), 2.0, dtype=jnp.float32)
        e_gate_logit = jnp.full((N_HEADS,), 2.0, dtype=jnp.float32)
        return {'x': x, 'Wqkv': Wqkv, 'Wo': Wo, 'log_xi': log_xi, 'pi_gate_logit': pi_gate_logit, 'e_gate_logit': e_gate_logit}
    _L0_attn_in = _L0_attn_setup()

    def _L0_ffn_setup():
        import jax, jax.numpy as jnp
        import numpy as np
        DIM = 128
        DEPTH = 2
        HEADS = 8
        DIM_HEAD = 64
        WINDOW = 64
        INNER = HEADS * DIM_HEAD
        HID = int(DIM * 4 * 2 / 3)
        B, N = (2, 1024)
        QK_SCALE = 8.0

        def shift_token(t):
            t1, t2 = jnp.split(t, 2, axis=-1)
            t2 = jnp.pad(t2, ((0, 0), (1, 0), (0, 0)))[:, :-1]
            return jnp.concatenate([t1, t2], axis=-1)

        def l2norm(t):
            return t / jnp.clip(jnp.linalg.norm(t, axis=-1, keepdims=True), 1e-12)

        def rotate_half(x):
            x1, x2 = jnp.split(x, 2, axis=-1)
            return jnp.concatenate([-x2, x1], axis=-1)

        def rotary_xpos(q, k):
            n = q.shape[-2]
            half_idx = jnp.arange(0, DIM_HEAD, 2, dtype=jnp.float32)
            inv_freq = 1.0 / 10000.0 ** (half_idx / DIM_HEAD)
            t = jnp.arange(n, dtype=jnp.float32)
            freqs = t[:, None] * inv_freq[None, :]
            freqs = jnp.concatenate([freqs, freqs], axis=-1)
            base = (half_idx + 0.4 * DIM_HEAD) / (1.4 * DIM_HEAD)
            power = (t - n // 2) / float(WINDOW // 2)
            scale = base[None, :] ** power[:, None]
            scale = jnp.concatenate([scale, scale], axis=-1)
            cos, sin = (jnp.cos(freqs), jnp.sin(freqs))
            q = q * cos * scale + rotate_half(q) * sin * scale
            k = k * cos / scale + rotate_half(k) * sin / scale
            return (q, k)

        def local_attention(q, k, v):
            b, h, n, d = q.shape
            w = n // WINDOW
            bq = q.reshape(b, h, w, WINDOW, d) * QK_SCALE
            bk = k.reshape(b, h, w, WINDOW, d)
            bv = v.reshape(b, h, w, WINDOW, d)

            def look_around(t):
                p = jnp.pad(t, ((0, 0), (0, 0), (1, 0), (0, 0), (0, 0)))
                return jnp.concatenate([p[:, :, :w], p[:, :, 1:]], axis=3)
            bk, bv = (look_around(bk), look_around(bv))
            bt = jnp.arange(n).reshape(w, WINDOW)
            btp = jnp.pad(bt, ((1, 0), (0, 0)), constant_values=-1)
            btk = jnp.concatenate([btp[:w], btp[1:]], axis=1)
            sim = jnp.einsum('bhwid,bhwjd->bhwij', bq, bk)
            i = bt[:, :, None]
            j = btk[:, None, :]
            mask = (i < j) | (i > j + WINDOW) | (j == -1)
            sim = jnp.where(mask, -jnp.finfo(sim.dtype).max, sim)
            attn = jax.nn.softmax(sim, axis=-1)
            out = jnp.einsum('bhwij,bhwjd->bhwid', attn, bv)
            return out.reshape(b, h, n, d)

        def _layer(x, wqkv, qs, ksc, wo, lg, lb, w1, b1, w2, b2):
            b, n, _ = x.shape
            h = shift_token(x)
            qkv = h @ wqkv
            q, k, v = jnp.split(qkv, 3, axis=-1)
            to_heads = lambda t: t.reshape(b, n, HEADS, DIM_HEAD).transpose(0, 2, 1, 3)
            q, k, v = (to_heads(q), to_heads(k), to_heads(v))
            q = l2norm(q) * qs
            k = l2norm(k) * ksc
            q, k = rotary_xpos(q, k)
            o = local_attention(q, k, v)
            o = o.transpose(0, 2, 1, 3).reshape(b, n, INNER)
            x = x + o @ wo
            h = shift_token(x)
            mu = h.mean(-1, keepdims=True)
            var = h.var(-1, keepdims=True)
            h = (h - mu) / jnp.sqrt(var + 1e-05) * lg + lb
            h = h @ w1 + b1
            a, g = jnp.split(h, 2, axis=-1)
            h = a * jax.nn.gelu(g, approximate=False)
            x = x + h @ w2 + b2
            return x
        key = jax.random.key(seed)
        ks = jax.random.split(key, 6)
        return {'x': jax.random.normal(ks[0], (B, N, DIM), jnp.float32), 'wqkv': jax.random.normal(ks[1], (DEPTH, DIM, 3 * INNER), jnp.float32) * 0.02, 'q_scale': jnp.ones((DEPTH, DIM_HEAD), jnp.float32), 'k_scale': jnp.ones((DEPTH, DIM_HEAD), jnp.float32), 'wo': jax.random.normal(ks[2], (DEPTH, INNER, DIM), jnp.float32) * 0.02, 'ln_g': jnp.ones((DEPTH, DIM), jnp.float32), 'ln_b': jnp.zeros((DEPTH, DIM), jnp.float32), 'w1': jax.random.normal(ks[3], (DEPTH, DIM, 2 * HID), jnp.float32) * 0.02, 'b1': jnp.zeros((DEPTH, 2 * HID), jnp.float32), 'w2': jax.random.normal(ks[4], (DEPTH, HID, DIM), jnp.float32) * 0.02, 'b2': jnp.zeros((DEPTH, DIM), jnp.float32)}
    _L0_ffn_in = _L0_ffn_setup()
    _d = {'L0_attn_x': _L0_attn_in['x'], 'L0_attn_Wqkv': _L0_attn_in['Wqkv'], 'L0_attn_Wo': _L0_attn_in['Wo'], 'L0_attn_log_xi': _L0_attn_in['log_xi'], 'L0_attn_pi_gate_logit': _L0_attn_in['pi_gate_logit'], 'L0_attn_e_gate_logit': _L0_attn_in['e_gate_logit'], 'L0_ffn_wqkv': _L0_ffn_in['wqkv'], 'L0_ffn_q_scale': _L0_ffn_in['q_scale'], 'L0_ffn_k_scale': _L0_ffn_in['k_scale'], 'L0_ffn_wo': _L0_ffn_in['wo'], 'L0_ffn_ln_g': _L0_ffn_in['ln_g'], 'L0_ffn_ln_b': _L0_ffn_in['ln_b'], 'L0_ffn_w1': _L0_ffn_in['w1'], 'L0_ffn_b1': _L0_ffn_in['b1'], 'L0_ffn_w2': _L0_ffn_in['w2'], 'L0_ffn_b2': _L0_ffn_in['b2']}
    _x0 = _d['L0_attn_x']
    _d['L0_attn_x'] = jax.random.normal(jax.random.fold_in(jax.random.key(seed), 1), (8, 512, 128), dtype=_x0.dtype)
    del _x0
    return _d

def reference(L0_attn_x, L0_attn_Wqkv, L0_attn_Wo, L0_attn_log_xi, L0_attn_pi_gate_logit, L0_attn_e_gate_logit, L0_ffn_wqkv, L0_ffn_q_scale, L0_ffn_k_scale, L0_ffn_wo, L0_ffn_ln_g, L0_ffn_ln_b, L0_ffn_w1, L0_ffn_b1, L0_ffn_w2, L0_ffn_b2):

    def _L0_attn_ref(x, Wqkv, Wo, log_xi, pi_gate_logit, e_gate_logit):
        import math
        import jax, jax.numpy as jnp
        import numpy as np
        D_MODEL = 128
        N_HEADS = 16
        D_HEAD = D_MODEL // N_HEADS
        BLOCK = 256
        BATCH = 2
        SEQ = 256

        def _rotate(t, cos, sin):
            t1 = t[..., 0::2]
            t2 = t[..., 1::2]
            r1 = t1 * cos - t2 * sin
            r2 = t1 * sin + t2 * cos
            return jnp.stack([r1, r2], axis=-1).reshape(t.shape)
        b, n, d = x.shape
        H, dh = (N_HEADS, D_HEAD)
        qkv = (x @ Wqkv.T).reshape(b, n, 3, H, dh)
        q = jnp.transpose(qkv[:, :, 0], (0, 2, 1, 3))
        k = jnp.transpose(qkv[:, :, 1], (0, 2, 1, 3))
        v = jnp.transpose(qkv[:, :, 2], (0, 2, 1, 3))
        pi_g = jax.nn.sigmoid(pi_gate_logit)
        e_g = jax.nn.sigmoid(e_gate_logit)
        kfrac = jnp.arange(0, dh, 2, dtype=jnp.float32) / dh
        pi_inv_freq = jnp.float32(math.pi) ** (1.0 - kfrac)
        pos = jnp.arange(n, dtype=jnp.float32)
        theta = pos[:, None] * pi_inv_freq[None, :]
        theta = theta[None, :, :] * pi_g[:, None, None]
        cos, sin = (jnp.cos(theta), jnp.sin(theta))
        q_rot = _rotate(q, cos, sin)
        k_rot = _rotate(k, cos, sin)
        scores = jnp.einsum('bhqd,bhkd->bhqk', q_rot, k_rot) / jnp.float32(math.sqrt(dh))
        xi = jnp.exp(log_xi)
        i = jnp.arange(n, dtype=jnp.float32)
        d_mat = jnp.abs(i[:, None] - i[None, :])
        decay_bias = -(d_mat[None, :, :] / xi[:, None, None]) * e_g[:, None, None]
        scores = scores + decay_bias[None]
        causal = jnp.tril(jnp.ones((n, n), dtype=bool))
        scores = jnp.where(causal[None, None], scores, jnp.float32(-jnp.inf))
        attn = jax.nn.softmax(scores, axis=-1)
        out = jnp.einsum('bhqk,bhkd->bhqd', attn, v)
        out = jnp.transpose(out, (0, 2, 1, 3)).reshape(b, n, d)
        return out @ Wo.T

    def _L0_ffn_ref(x, wqkv, q_scale, k_scale, wo, ln_g, ln_b, w1, b1, w2, b2):
        import jax, jax.numpy as jnp
        import numpy as np
        DIM = 128
        DEPTH = 2
        HEADS = 8
        DIM_HEAD = 64
        WINDOW = 64
        INNER = HEADS * DIM_HEAD
        HID = int(DIM * 4 * 2 / 3)
        B, N = (2, 1024)
        QK_SCALE = 8.0

        def shift_token(t):
            t1, t2 = jnp.split(t, 2, axis=-1)
            t2 = jnp.pad(t2, ((0, 0), (1, 0), (0, 0)))[:, :-1]
            return jnp.concatenate([t1, t2], axis=-1)

        def l2norm(t):
            return t / jnp.clip(jnp.linalg.norm(t, axis=-1, keepdims=True), 1e-12)

        def rotate_half(x):
            x1, x2 = jnp.split(x, 2, axis=-1)
            return jnp.concatenate([-x2, x1], axis=-1)

        def rotary_xpos(q, k):
            n = q.shape[-2]
            half_idx = jnp.arange(0, DIM_HEAD, 2, dtype=jnp.float32)
            inv_freq = 1.0 / 10000.0 ** (half_idx / DIM_HEAD)
            t = jnp.arange(n, dtype=jnp.float32)
            freqs = t[:, None] * inv_freq[None, :]
            freqs = jnp.concatenate([freqs, freqs], axis=-1)
            base = (half_idx + 0.4 * DIM_HEAD) / (1.4 * DIM_HEAD)
            power = (t - n // 2) / float(WINDOW // 2)
            scale = base[None, :] ** power[:, None]
            scale = jnp.concatenate([scale, scale], axis=-1)
            cos, sin = (jnp.cos(freqs), jnp.sin(freqs))
            q = q * cos * scale + rotate_half(q) * sin * scale
            k = k * cos / scale + rotate_half(k) * sin / scale
            return (q, k)

        def local_attention(q, k, v):
            b, h, n, d = q.shape
            w = n // WINDOW
            bq = q.reshape(b, h, w, WINDOW, d) * QK_SCALE
            bk = k.reshape(b, h, w, WINDOW, d)
            bv = v.reshape(b, h, w, WINDOW, d)

            def look_around(t):
                p = jnp.pad(t, ((0, 0), (0, 0), (1, 0), (0, 0), (0, 0)))
                return jnp.concatenate([p[:, :, :w], p[:, :, 1:]], axis=3)
            bk, bv = (look_around(bk), look_around(bv))
            bt = jnp.arange(n).reshape(w, WINDOW)
            btp = jnp.pad(bt, ((1, 0), (0, 0)), constant_values=-1)
            btk = jnp.concatenate([btp[:w], btp[1:]], axis=1)
            sim = jnp.einsum('bhwid,bhwjd->bhwij', bq, bk)
            i = bt[:, :, None]
            j = btk[:, None, :]
            mask = (i < j) | (i > j + WINDOW) | (j == -1)
            sim = jnp.where(mask, -jnp.finfo(sim.dtype).max, sim)
            attn = jax.nn.softmax(sim, axis=-1)
            out = jnp.einsum('bhwij,bhwjd->bhwid', attn, bv)
            return out.reshape(b, h, n, d)

        def _layer(x, wqkv, qs, ksc, wo, lg, lb, w1, b1, w2, b2):
            b, n, _ = x.shape
            h = shift_token(x)
            qkv = h @ wqkv
            q, k, v = jnp.split(qkv, 3, axis=-1)
            to_heads = lambda t: t.reshape(b, n, HEADS, DIM_HEAD).transpose(0, 2, 1, 3)
            q, k, v = (to_heads(q), to_heads(k), to_heads(v))
            q = l2norm(q) * qs
            k = l2norm(k) * ksc
            q, k = rotary_xpos(q, k)
            o = local_attention(q, k, v)
            o = o.transpose(0, 2, 1, 3).reshape(b, n, INNER)
            x = x + o @ wo
            h = shift_token(x)
            mu = h.mean(-1, keepdims=True)
            var = h.var(-1, keepdims=True)
            h = (h - mu) / jnp.sqrt(var + 1e-05) * lg + lb
            h = h @ w1 + b1
            a, g = jnp.split(h, 2, axis=-1)
            h = a * jax.nn.gelu(g, approximate=False)
            x = x + h @ w2 + b2
            return x
        for l in range(DEPTH):
            x = _layer(x, wqkv[l], q_scale[l], k_scale[l], wo[l], ln_g[l], ln_b[l], w1[l], b1[l], w2[l], b2[l])
        return x
    x = L0_attn_x
    x = x + _L0_attn_ref(_layernorm(x, axis=-1), L0_attn_Wqkv, L0_attn_Wo, L0_attn_log_xi, L0_attn_pi_gate_logit, L0_attn_e_gate_logit)
    x = x + _L0_ffn_ref(_layernorm(x, axis=-1), L0_ffn_wqkv, L0_ffn_q_scale, L0_ffn_k_scale, L0_ffn_wo, L0_ffn_ln_g, L0_ffn_ln_b, L0_ffn_w1, L0_ffn_b1, L0_ffn_w2, L0_ffn_b2)
    return x

_drawn_inputs = setup_inputs


def setup_inputs(seed=0):
    import zlib

    import numpy as np

    out = dict(_drawn_inputs(seed))
    spreads = {'L0_attn_log_xi': (4.852030277252197, 0.6),
     'L0_attn_pi_gate_logit': (2.0, 0.6),
     'L0_attn_e_gate_logit': (2.0, 0.6),
     'L0_ffn_q_scale': (1.0, 0.6),
     'L0_ffn_k_scale': (1.0, 0.6),
     'L0_ffn_ln_g': (1.0, 0.6),
     'L0_ffn_ln_b': (0.0, 0.8),
     'L0_ffn_b1': (0.0, 0.8),
     'L0_ffn_b2': (0.0, 0.446)}
    factors = {'L0_attn_Wqkv': 8.0,
     'L0_attn_Wo': 8.0,
     'L0_ffn_wqkv': 3.745,
     'L0_ffn_wo': 3.741,
     'L0_ffn_w1': 6.153,
     'L0_ffn_w2': 6.064}
    for name, (base, spread) in spreads.items():
        noise = np.random.default_rng([zlib.crc32(name.encode()), seed]).standard_normal(out[name].shape)
        drawn = base * np.exp(spread * noise) if base else spread * noise
        out[name] = jnp.asarray(drawn.astype(out[name].dtype))
    for name, factor in factors.items():
        out[name] = (out[name] * factor).astype(out[name].dtype)
    return out
```

```python
from contextlib import ExitStack

import concourse.bass as bass
from concourse import mybir

F32 = mybir.dt.float32
BF16 = mybir.dt.bfloat16
I32 = mybir.dt.int32
ALU = mybir.AluOpType
ACT = mybir.ActivationFunctionType
AX = mybir.AxisListType

P = 128
SEQS, TOK, DM = 8, 512, 128
NT = TOK // P
AH, AD = 16, 8
PAIRS = AH // 2
LAYERS, FH, FD = 2, 8, 64
CH = FH // 2
WIN = 64
HID = int(DM * 4 * 2 / 3)
HCH = [(j * P, min(P, HID - j * P)) for j in range((HID + P - 1) // P)]
LNS = 2 + LAYERS
Q_PARTS, K_PARTS = (0, 0, 1, 1, 0, 2), (0, 1, 0, 1, 2, 0)
DECAY_ROW = len(Q_PARTS) * AD
MAX_ROW = DECAY_ROW + 6
K_SCORE, K_SHIFTED = MAX_ROW, MAX_ROW + 3
RSQRT_MAGIC = 0x5F3759DF
NEWTON = 3
RSQRT_STEPS = 2 + 3 * NEWTON
SECTION = {0: (0, 512), 1: (512, 384), 3: (896, 128), 2: (1024, 256)}
PT_COLS = 1280
UNITS_ST = [((0,), 0, 512), ((1, 3), 512, 512), ((2,), 1024, 256)]


def build(nc, x, consts, a_w, a_vec, f_w, f_vec, out):
    (ident_d, causal_d, band_d, posfreq_d, pos_d, sign_d, rope_d) = consts
    (awqk_d, awv_d, awo_d) = a_w
    (pi_gate_d, log_xi_d, e_gate_d) = a_vec
    (wqkv_d, wo_d, w1_d, w2_d) = f_w
    (qkscale_d, ln_gb_d, b1_d, b2_d) = f_vec

    with ExitStack() as ctx:
        def sb(name, shape, dt=F32):
            return ctx.enter_context(nc.sbuf_tensor(name, shape, dt))

        ident = sb("ident", [P, P])
        ident_b = sb("ident_b", [P, P], BF16)
        causal = sb("causal", [P, 2, P], BF16)
        band = sb("band", [P, 2, P], BF16)
        mean_w = sb("mean_w", [P, P])
        awqk = sb("awqk", [P, 4, P])
        awv = sb("awv", [P, P])
        awo = sb("awo", [P, P])
        wqkv = sb("wqkv", [P, LAYERS, 3 * CH * P])
        wo = sb("wo", [P, LAYERS, CH, P])
        w1 = sb("w1", [P, LAYERS, 2 * HID])
        w2 = sb("w2", [P, LAYERS, len(HCH), P])
        ln_gb = sb("ln_gb", [P, LAYERS, 2])
        b1 = sb("b1", [P, LAYERS, 2, len(HCH)])
        b2 = sb("b2", [P, LAYERS])
        a_rot = sb("a_rot", [P, 4, TOK])
        f_rot = sb("f_rot", [P, LAYERS, 4, NT, FD])
        qkscale = sb("qkscale", [P, LAYERS, 2, FD])
        gate = sb("gate", [P, 4])
        sign = sb("sign", [P, 1])
        dec = sb("dec", [AH, 8])

        x_in = sb("x_in", [P, NT, DM])
        xT = sb("xT", [P, TOK])
        cent = sb("cent", [P, TOK])
        sq = sb("sq", [P, TOK])
        rstd = sb("rstd", [P, 3, NT])
        xn = sb("xn", [P, TOK])
        prod = sb("prod", [P, 4, TOK])
        rot = sb("rot", [P, 2, TOK])
        part = sb("part", [P, 2, 3, TOK], BF16)
        qP = sb("qP", [P, PAIRS, TOK], BF16)
        kP = sb("kP", [P, PAIRS, TOK], BF16)
        negm = sb("negm", [P, NT, 2, PAIRS])
        negm_r = sb("negm_r", [P, NT, 2, PAIRS])
        negm_p = sb("negm_p", [P, NT, 2, 3, PAIRS], BF16)
        mT = sb("mT", [2 * 3 * PAIRS, TOK], BF16)
        vA = sb("vA", [P, NT, AH, 32])
        pT = sb("pT", [P, 2, 2, PT_COLS])
        oP = sb("oP", [P, 2, TOK])
        rl = sb("rl", [P, 2, NT, 4])
        oN = sb("oN", [P, NT, AH, AD])
        oA = sb("oA", [P, TOK])
        x1T = sb("x1T", [P, TOK])

        cur = sb("cur", [P, TOK])
        hT = sb("hT", [P, TOK])
        sqf = sb("sqf", [P, 2, CH * P])
        t1 = sb("t1", [P, 2, CH * P])
        t2 = sb("t2", [P, 2, CH * P])
        ss = sb("ss", [P, 3, 2 * NT, FH])
        r = sb("r", [P, 2 * NT, CH * P])
        rope = r[:, 0:2, :].rearrange("p a (b t d) -> p (a b) t d", t=NT, d=FD)
        causal_f = r[:, 2, 0:2 * P].rearrange("p (a k) -> p a k", a=2)
        band_f = r[:, 3, 0:2 * P].rearrange("p (a k) -> p a k", a=2)
        qT = sb("qT", [P, CH, TOK])
        kT = sb("kT", [P, CH, WIN + TOK])
        v_own = sb("v_own", [P, NT, FH, FD + 1])
        v_cross = sb("v_cross", [P, NT, FH, FD + 1])
        nm = sb("nm", [P, 2, CH])
        rlf = sb("rlf", [P, 2, CH])
        mid = sb("mid", [P, TOK])
        nT = sb("nT", [P, TOK])
        gel = r[:, 0:len(HCH), :]
        oT = r[:, 0:CH, :]
        ex = t1[:].rearrange("p b (c k) -> p b c k", c=CH)
        pTf = t2[:].rearrange("p b (c k) -> p b c k", c=CH)
        oS = sqf[:].rearrange("p b (h d) -> p b h d", h=FH)
        hid = r[:, len(HCH):2 * len(HCH), :]
        ob = sb("ob", [P, NT, DM])

        ps = ctx.enter_context(nc.psum_tensor("ps", [P, 8, 512], F32))

        per_round = {}

        def sem(name, per):
            s = ctx.enter_context(nc.semaphore(name))
            per_round[id(s)] = per
            return s

        def after(s, rnd, n):
            return rnd * per_round[id(s)] + n

        const_in = sem("const_in", 0)
        const_ready = sem("const_ready", 0)
        pre_dve = sem("pre_dve", 0)
        pre_act = sem("pre_act", 0)
        decay_in = sem("decay_in", 0)
        seq_done = sem("seq_done", 1)
        x_loaded = sem("x_loaded", 16)
        xT_ps = sem("xT_ps", 1)
        xT_sb = sem("xT_sb", 1)
        ln_mean = sem("ln_mean", 1)
        ln_cent = sem("ln_cent", 1)
        ln_sq = sem("ln_sq", 1)
        ln_var = sem("ln_var", 1)
        ln_rsqrt = sem("ln_rsqrt", RSQRT_STEPS)
        ln_spread = sem("ln_spread", 1)
        ln_out = sem("ln_out", 1)
        a_proj = sem("a_proj", 5)
        a_prod = sem("a_prod", 4)
        a_rot_sum = sem("a_rot_sum", 2)
        a_hi = sem("a_hi", 2)
        a_rest = sem("a_rest", 2)
        a_mid = sem("a_mid", 2)
        a_lo = sem("a_lo", 2)
        a_packed = sem("a_packed", 16 * 4 * len(Q_PARTS))
        a_v = sem("a_v", 1)
        a_s = sem("a_s", PAIRS * NT)
        a_max = sem("a_max", PAIRS * NT)
        a_maxparts = sem("a_maxparts", 5)
        a_maxT = sem("a_maxT", 1)
        a_maxT_sb = sem("a_maxT_sb", 1)
        a_max_in = sem("a_max_in", 32)
        a_st = sem("a_st", PAIRS * 3)
        a_exp = sem("a_exp", PAIRS * 3)
        a_pv = sem("a_pv", 4)
        a_o_sb = sem("a_o_sb", 4)
        a_oT = sem("a_oT", 4)
        a_rl = sem("a_rl", 4)
        a_norm = sem("a_norm", 4)
        a_oN_T = sem("a_oN_T", 1)
        a_oA = sem("a_oA", 1)
        a_y = sem("a_y", 1)
        a_x1 = sem("a_x1", 1)
        f_shift = sem("f_shift", 4)
        f_proj = sem("f_proj", 3 * NT)
        f_sq = sem("f_sq", 2 * NT)
        f_ss = sem("f_ss", 2 * NT)
        f_cos = sem("f_cos", 2 * NT)
        f_sin = sem("f_sin", 4 * NT)
        f_rope = sem("f_rope", 2 * NT)
        f_rsqrt = sem("f_rsqrt", RSQRT_STEPS)
        f_unit_v = sem("f_unit_v", NT)
        f_unit_p = sem("f_unit_p", NT)
        f_qkT = sem("f_qkT", 2 * NT)
        f_qkT_sb = sem("f_qkT_sb", 2 * NT)
        f_v = sem("f_v", NT)
        f_v_cross = sem("f_v_cross", 32)
        f_s = sem("f_s", 2 * NT)
        f_max = sem("f_max", 2 * NT)
        f_shifted = sem("f_shifted", 2 * NT)
        f_exp = sem("f_exp", 2 * NT)
        f_pT = sem("f_pT", 2 * NT)
        f_pT_sb = sem("f_pT_sb", 2 * NT)
        f_o = sem("f_o", 2 * NT)
        f_rl = sem("f_rl", 2 * NT)
        f_norm = sem("f_norm", 2 * NT)
        f_oT = sem("f_oT", NT)
        f_oT_sb = sem("f_oT_sb", NT)
        f_wo = sem("f_wo", 1)
        f_mid = sem("f_mid", 1)
        f_ln_gb = sem("f_ln_gb", 1)
        f_w1 = sem("f_w1", 2 * len(HCH))
        f_gelu = sem("f_gelu", len(HCH))
        f_hid = sem("f_hid", len(HCH))
        f_w2 = sem("f_w2", 1)
        f_next = sem("f_next", 1)
        y_sum = sem("y_sum", 1)
        y_ps = sem("y_ps", 1)
        y_out = sem("y_out", 16)

        def rsqrt(eng, y, s, a, steps, rnd):
            n = 1
            eng.wait_ge(steps, after(steps, rnd, n))
            eng.tensor_scalar(y.bitcast(I32), s.bitcast(I32), -0.5, float(RSQRT_MAGIC),
                              ALU.mult, ALU.add).then_inc(steps, 1)
            for _ in range(NEWTON):
                n += 1
                eng.wait_ge(steps, after(steps, rnd, n))
                eng.tensor_tensor(a, y, y, ALU.mult).then_inc(steps, 1)
                n += 1
                eng.wait_ge(steps, after(steps, rnd, n))
                eng.scalar_tensor_tensor(a, a, -0.5, s, ALU.mult, ALU.mult).then_inc(steps, 1)
                n += 1
                eng.wait_ge(steps, after(steps, rnd, n))
                eng.scalar_tensor_tensor(y, a, 1.5, y, ALU.add, ALU.mult).then_inc(steps, 1)
            assert n + 1 == RSQRT_STEPS

        N_CONST = 16 * (16 + 6 * LAYERS)
        block = ctx.enter_context(nc.Block())

        @block.sync
        def _(sp):
            loads = [(ident[:], ident_d), (causal_f, causal_d), (band_f, band_d), (sign[:], sign_d),
                     (prod[:, 0, :], posfreq_d), (gate[:, 0:1], pi_gate_d),
                     (dec[:, 0:1], log_xi_d), (dec[:, 1:2], e_gate_d), (prod[0:AH, 1, :], pos_d),
                     (awqk[:], awqk_d), (awv[:], awv_d), (awo[:], awo_d), (rope, rope_d),
                     (qkscale[:], qkscale_d), (b2[:], b2_d), (ln_gb[:], ln_gb_d)]
            for dst, src in loads:
                sp.dma_start(dst, src).then_inc(const_in, 16)
            for l in range(LAYERS):
                sp.dma_start(wqkv[:, l, :], wqkv_d[l]).then_inc(const_in, 16)
                sp.dma_start(wo[:, l], wo_d[l].rearrange("(c p) d -> p c d", p=P)).then_inc(const_in, 16)
                sp.dma_start(w1[:, l, :], w1_d[l]).then_inc(const_in, 16)
                full = (HID // P) * P
                sp.dma_start(w2[:, l, 0:HID // P, :],
                             w2_d[l, 0:full].rearrange("(c p) d -> p c d", p=P)).then_inc(const_in, 16)
                sp.dma_start(w2[0:HID - full, l, HID // P, :], w2_d[l, full:HID]).then_inc(const_in, 16)
                sp.dma_start(b1[:, l], b1_d[l]).then_inc(const_in, 16)

            sp.wait_ge(pre_dve, 1000)
            n_dec = 0
            for side, (dst, row0) in enumerate(((qP, DECAY_ROW), (kP, DECAY_ROW + 3))):
                for par in range(2):
                    for p3 in range(3):
                        row = 64 * par + row0 + p3
                        sp.dma_start(dst[row:row + 1, :, :],
                                     part[PAIRS * par:PAIRS * par + PAIRS, side, p3, :]).then_inc(decay_in, 16)
                        n_dec += 16
            sp.wait_ge(decay_in, n_dec)

            sp.sem_inc(y_out, 16)
            sp.sem_inc(seq_done, 1)
            with sp.Fori(0, SEQS) as i:
                sp.wait_ge(seq_done, after(seq_done, i, 1))
                sp.dma_start(x_in[:], x[i].rearrange("(t p) d -> p t d", p=P)).then_inc(x_loaded, 16)
                for side, (dst, order) in enumerate(((qP, Q_PARTS), (kP, K_PARTS))):
                    sp.wait_ge(a_lo, after(a_lo, i, side + 1))
                    if side == 0:
                        sp.wait_ge(a_mid, after(a_mid, i, 1))
                        sp.wait_ge(a_hi, after(a_hi, i, 1))
                    else:
                        sp.wait_ge(a_mid, after(a_mid, i, 2))
                        sp.wait_ge(a_hi, after(a_hi, i, 2))
                    for par in range(2):
                        for seg, p3 in enumerate(order):
                            row = 64 * par + AD * seg
                            sp.dma_start(dst[row:row + AD, :, :],
                                         part[64 * par:64 * par + 64, side, p3, :]).then_inc(a_packed, 16)
                sp.wait_ge(a_maxT_sb, after(a_maxT_sb, i, 1))
                for par in range(2):
                    row = 64 * par + MAX_ROW
                    sp.dma_start(qP[row:row + 3, :, :], mT[3 * PAIRS * par:3 * PAIRS * (par + 1), :]).then_inc(a_max_in, 16)
                for l in range(LAYERS):
                    lay = i * LAYERS + l
                    sp.wait_ge(f_v, after(f_v, lay, NT))
                    sp.dma_start(v_cross[0:WIN, :, :, :], v_own[0:WIN, :, :, :]).then_inc(f_v_cross, 16)
                    sp.dma_start(v_cross[WIN:P, 1:NT, :, :], v_own[WIN:P, 0:NT - 1, :, :]).then_inc(f_v_cross, 16)
                sp.wait_ge(seq_done, after(seq_done, i, 2))
                sp.dma_start(out[i].rearrange("(t p) d -> p t d", p=P), ob[:]).then_inc(y_out, 16)
            sp.wait_ge(y_out, 16 * (SEQS + 1))

        @block.gpsimd
        def _(pool):
            fills = [(qP[:], 1.0), (kP[:], 1.0), (vA[:], 0.0), (mean_w[:], 1.0 / DM), (kT[:], 0.0),
                     (hT[:], 0.0), (v_own[:], 1.0), (v_cross[:], 0.0)]
            for dst, val in fills:
                pool.memset(dst, val).then_inc(const_ready, 1)
            pool.wait_ge(const_ready, 3)
            pool.memset(vA[:, :, :, AD:AD + 1], 1.0).then_inc(const_ready, 1)
            with pool.Fori(0, SEQS) as i:
                for l in range(LAYERS):
                    lay = i * LAYERS + l
                    for u in range(2 * NT):
                        pool.wait_ge(f_cos, after(f_cos, lay, u + 1))
                        pool.wait_ge(f_sin, after(f_sin, lay, 2 * u + 2))
                        pool.tensor_tensor(r[:, u, :], t1[:, u % 2, :], t2[:, u % 2, :], ALU.add).then_inc(f_rope, 1)
                    pool.wait_ge(f_rsqrt, after(f_rsqrt, lay, RSQRT_STEPS))
                    for u in range(1, 2 * NT, 2):
                        pool.wait_ge(f_rope, after(f_rope, lay, u + 1))
                        rv = r[:, u, :].rearrange("p (h d) -> p h d", h=FH)
                        pool.tensor_tensor(rv, rv, ss[:, 1, u, :].unsqueeze(2).broadcast_to([P, FH, FD]),
                                           ALU.mult).then_inc(f_unit_p, 1)

        @block.scalar
        def _(act):
            act.wait_ge(const_in, N_CONST)
            act.activation(gate[:, 1:2], gate[:, 0:1], ACT.Exp, scale=-1.0).then_inc(pre_act, 1)
            act.activation(dec[:, 2:4], dec[:, 0:2], ACT.Exp, scale=-1.0).then_inc(pre_act, 1)
            act.wait_ge(pre_dve, 100)
            act.activation(a_rot[:, 0, :], a_rot[:, 2, :], ACT.Sin).then_inc(pre_act, 1)
            act.activation(a_rot[:, 1, :], a_rot[:, 3, :], ACT.Sin).then_inc(pre_act, 1)
            act.wait_ge(pre_dve, 1000)

            with act.Fori(0, SEQS) as i:

                def ln_square(n):
                    norm = i * LNS + n
                    act.wait_ge(ln_cent, after(ln_cent, norm, 1))
                    act.activation(sq[:], cent[:], ACT.Square).then_inc(ln_sq, 1)

                act.wait_ge(seq_done, after(seq_done, i, 1))
                act.wait_ge(xT_ps, after(xT_ps, i, 1))
                act.copy(xT[:], ps[:, 0, :]).then_inc(xT_sb, 1)
                ln_square(0)
                act.wait_ge(a_proj, after(a_proj, i, 5))
                act.copy(vA[:, :, :, 0:AD], ps[:, 7, :].rearrange("p (t h d) -> p t h d", t=NT, h=AH)).then_inc(a_v, 1)
                for side in range(2):
                    act.wait_ge(a_rot_sum, after(a_rot_sum, i, side + 1))
                    act.copy(part[:, side, 0, :], rot[:, side, :]).then_inc(a_hi, 1)
                for side in range(2):
                    act.wait_ge(a_rest, after(a_rest, i, side + 1))
                    act.copy(part[:, side, 1, :], rot[:, side, :]).then_inc(a_mid, 1)
                act.wait_ge(a_maxT, after(a_maxT, i, 1))
                act.copy(mT[:], ps[0:6 * PAIRS, 4, :]).then_inc(a_maxT_sb, 1)
                for pr in range(PAIRS):
                    for n, (_, col, w) in enumerate(UNITS_ST):
                        u = 3 * pr + n
                        act.wait_ge(a_st, after(a_st, i, u + 1))
                        if pr >= 2:
                            act.wait_ge(a_pv, after(a_pv, i, (pr - 2) // 2 + 1))
                        act.activation(pT[:, pr % 2, :, col:col + w],
                                       ps[:, 2 * (u % 2):2 * (u % 2) + 2, 0:w], ACT.Exp).then_inc(a_exp, 1)
                    if pr % 2:
                        g = pr // 2
                        act.wait_ge(a_pv, after(a_pv, i, g + 1))
                        if g >= 2:
                            act.wait_ge(a_oT, after(a_oT, i, g - 1))
                        act.copy(oP[:, g % 2, :], ps[:, 4 + g % 2, :]).then_inc(a_o_sb, 1)
                act.wait_ge(a_oN_T, after(a_oN_T, i, 1))
                act.copy(oA[:], ps[:, 0, :]).then_inc(a_oA, 1)
                ln_square(1)

                for l in range(LAYERS):
                    lay = i * LAYERS + l
                    for u in range(2 * NT):
                        act.wait_ge(f_proj, after(f_proj, lay, u + 1))
                        if u >= 2:
                            act.wait_ge(f_ss, after(f_ss, lay, u - 1))
                        act.activation(sqf[:, u % 2, :], ps[:, u % 8, :], ACT.Square).then_inc(f_sq, 1)
                    for t in range(NT):
                        act.wait_ge(f_proj, after(f_proj, lay, 2 * NT + t + 1))
                        act.copy(v_own[:, t, :, 0:FD], ps[:, t, :].rearrange("p (h d) -> p h d", h=FH)).then_inc(f_v, 1)
                    for u in range(2 * NT):
                        act.wait_ge(f_qkT, after(f_qkT, lay, u + 1))
                        t = u % NT
                        dst = qT[:, :, P * t:P * t + P] if u < NT else kT[:, :, WIN + P * t:WIN + P * t + P]
                        act.copy(dst, ps[:, 4 + u % 4, :].rearrange("p (c q) -> p c q", c=CH)).then_inc(f_qkT_sb, 1)
                    for v in range(2 * NT + 1):
                        if v < 2 * NT:
                            act.wait_ge(f_shifted, after(f_shifted, lay, v + 1))
                            act.activation(ex[:, v % 2], ex[:, v % 2], ACT.Exp).then_inc(f_exp, 1)
                            act.wait_ge(f_pT, after(f_pT, lay, v + 1))
                            if v >= 2:
                                act.wait_ge(f_o, after(f_o, lay, v - 1))
                            act.copy(pTf[:, v % 2], ps[:, 2 + v % 2, :].rearrange("p (c q) -> p c q", c=CH)).then_inc(f_pT_sb, 1)
                        if v >= 2 and v % 2 == 0:
                            t = v // 2 - 1
                            act.wait_ge(f_oT, after(f_oT, lay, t + 1))
                            act.copy(oT[:, :, P * t:P * t + P], ps[:, 6 + t % 2, :].rearrange("p (c q) -> p c q", c=CH)).then_inc(f_oT_sb, 1)
                    ln_square(2 + l)
                    for j, (_, w) in enumerate(HCH):
                        act.wait_ge(f_w1, after(f_w1, lay, j + 1))
                        act.activation(gel[0:w, j, :], ps[0:w, j, :], ACT.Gelu, bias=b1[0:w, l, 1, j:j + 1]).then_inc(f_gelu, 1)
                act.wait_ge(y_ps, after(y_ps, i, 1))
                act.wait_ge(y_out, after(y_out, i, 16))
                act.copy(ob[:], ps[:, 7, :].rearrange("p (t d) -> p t d", t=NT)).then_inc(seq_done, 1)

        @block.vector
        def _(dve):
            pd = pre_dve
            cnt = [0]

            def link(ins):
                cnt[0] += 1
                ins.then_inc(pd, 1)
                dve.wait_ge(pd, cnt[0])

            dve.wait_ge(const_in, N_CONST)
            dve.wait_ge(const_ready, 9)
            link(dve.tensor_copy(ident_b[:], ident[:]))
            link(dve.tensor_copy(causal[:], causal_f))
            link(dve.tensor_copy(band[:], band_f))
            for l in range(LAYERS):
                for k in range(2):
                    sc = qkscale[:, l, k, :].unsqueeze(1).broadcast_to([P, NT, FD])
                    link(dve.tensor_tensor(f_rot[:, l, 2 * k], rope[:, 2 * k], sc, ALU.mult))
                    for h in range(2):
                        a, b = slice(32 * h, 32 * h + 32), slice(32 - 32 * h, 64 - 32 * h)
                        link(dve.tensor_tensor(f_rot[:, l, 2 * k + 1, :, a], rope[:, 2 * k + 1, :, a],
                                               sc[:, :, b], ALU.mult))
            dve.wait_ge(pre_act, 2)
            link(dve.tensor_scalar(gate[:, 2:3], gate[:, 1:2], 1.0, None, ALU.add))
            link(dve.reciprocal(gate[:, 3:4], gate[:, 2:3]))
            theta = prod[:, 2, :]
            link(dve.tensor_scalar(theta, prod[:, 0, :], gate[:, 3:4], None, ALU.mult))
            TWO_PI = 6.283185307179586
            c1 = 6.28125
            c2 = 0.0019350051879882812
            c3 = TWO_PI - c1 - c2
            big = 12582912.0
            turns = prod[:, 3, :]
            for dst, quarter in ((a_rot[:, 2, :], 0.25), (a_rot[:, 3, :], 0.0)):
                link(dve.tensor_scalar(turns, theta, 1.0 / TWO_PI, quarter, ALU.mult, ALU.add))
                link(dve.tensor_scalar(turns, turns, big, None, ALU.add))
                link(dve.tensor_scalar(turns, turns, big, None, ALU.subtract))
                link(dve.scalar_tensor_tensor(dst, turns, -c1, theta, ALU.mult, ALU.add))
                link(dve.scalar_tensor_tensor(dst, turns, -c2, dst, ALU.mult, ALU.add))
                link(dve.scalar_tensor_tensor(dst, turns, -c3, dst, ALU.mult, ALU.add))
                if quarter:
                    link(dve.tensor_scalar(dst, dst, TWO_PI / 4, None, ALU.add))
                link(dve.tensor_scalar(dst, dst, 3.1415925, -3.1415925, ALU.min, ALU.max))
            assert cnt[0] < 100
            dve.sem_inc(pd, 100 - cnt[0])
            cnt[0] = 100
            link(dve.tensor_scalar(dec[:, 4:5], dec[:, 3:4], 1.0, None, ALU.add))
            link(dve.reciprocal(dec[:, 5:6], dec[:, 4:5]))
            link(dve.tensor_tensor(dec[:, 6:7], dec[:, 5:6], dec[:, 2:3], ALU.mult))
            cpos, rest = prod[0:AH, 2, :], prod[0:AH, 3, :]
            for side, sgn in ((0, -1.0), (1, 1.0)):
                link(dve.tensor_scalar(cpos, prod[0:AH, 1, :], dec[:, 6:7], sgn, ALU.mult, ALU.mult))
                link(dve.tensor_copy(part[0:AH, side, 0, :], cpos))
                link(dve.tensor_tensor(rest, cpos, part[0:AH, side, 0, :], ALU.subtract))
                link(dve.tensor_copy(part[0:AH, side, 1, :], rest))
                link(dve.tensor_tensor(part[0:AH, side, 2, :], rest, part[0:AH, side, 1, :], ALU.subtract))
            dve.wait_ge(pre_act, 4)
            link(dve.tensor_copy(a_rot[:, 2, :], a_rot[:, 0, :]))
            link(dve.tensor_scalar(a_rot[:, 3, :], a_rot[:, 1, :], sign[:, 0:1], None, ALU.mult))
            link(dve.tensor_scalar(a_rot[:, 0:2, :], a_rot[:, 2:4, :], AD ** -0.5, None, ALU.mult))
            dve.sem_inc(pd, 1000 - cnt[0])
            cnt[0] = 1000
            dve.wait_ge(pd, 1000)
            dve.wait_ge(decay_in, 16 * 12)

            with dve.Fori(0, SEQS) as i:

                def layer_norm(n, src, dst):
                    norm = i * LNS + n
                    dve.wait_ge(ln_mean, after(ln_mean, norm, 1))
                    dve.tensor_tensor(cent[:], src, ps[:, 0, :], ALU.subtract).then_inc(ln_cent, 1)
                    dve.wait_ge(ln_var, after(ln_var, norm, 1))
                    dve.tensor_scalar(rstd[:, 0, :], ps[:, 1, 0:NT], 1e-5, None, ALU.add).then_inc(ln_rsqrt, 1)
                    rsqrt(dve, rstd[:, 1, :], rstd[:, 0, :], rstd[:, 2, :], ln_rsqrt, norm)
                    dve.wait_ge(ln_spread, after(ln_spread, norm, 1))
                    dve.wait_ge(ln_cent, after(ln_cent, norm, 1))
                    dve.tensor_tensor(dst, cent[:], ps[:, 2, :], ALU.mult).then_inc(ln_out, 1)

                dve.wait_ge(seq_done, after(seq_done, i, 1))
                dve.wait_ge(xT_sb, after(xT_sb, i, 1))
                layer_norm(0, xT[:], xn[:])
                for side in range(2):
                    for n in range(2):
                        u = 2 * side + n
                        dve.wait_ge(a_proj, after(a_proj, i, u + 1))
                        dve.tensor_tensor(prod[:, u, :], ps[:, 3 + u, :], a_rot[:, u, :], ALU.mult).then_inc(a_prod, 1)
                    dve.wait_ge(a_prod, after(a_prod, i, 2 * side + 2))
                    dve.tensor_tensor(rot[:, side, :], prod[:, 2 * side, :], prod[:, 2 * side + 1, :], ALU.add).then_inc(a_rot_sum, 1)
                for side in range(2):
                    dve.wait_ge(a_hi, after(a_hi, i, side + 1))
                    dve.tensor_tensor(rot[:, side, :], rot[:, side, :], part[:, side, 0, :], ALU.subtract).then_inc(a_rest, 1)
                for side in range(2):
                    dve.wait_ge(a_mid, after(a_mid, i, side + 1))
                    dve.tensor_tensor(part[:, side, 2, :], rot[:, side, :], part[:, side, 1, :], ALU.subtract).then_inc(a_lo, 1)
                for pr in range(PAIRS):
                    for t in range(NT):
                        u = NT * pr + t
                        dve.wait_ge(a_s, after(a_s, i, u + 1))
                        b = 2 * (u % 2)
                        dve.tensor_reduce(negm[:, t, :, pr], ps[:, b:b + 2, 0:P * (t + 1)], AX.X, ALU.max,
                                          negate=True).then_inc(a_max, 1)
                dve.wait_ge(a_max, after(a_max, i, PAIRS * NT))
                mp = a_maxparts
                dve.tensor_copy(negm_p[:, :, :, 0, :], negm[:]).then_inc(mp, 1)
                dve.wait_ge(a_maxparts, after(a_maxparts, i, 1))
                dve.tensor_tensor(negm_r[:], negm[:], negm_p[:, :, :, 0, :], ALU.subtract).then_inc(mp, 1)
                dve.wait_ge(a_maxparts, after(a_maxparts, i, 2))
                dve.tensor_copy(negm_p[:, :, :, 1, :], negm_r[:]).then_inc(mp, 1)
                dve.wait_ge(a_maxparts, after(a_maxparts, i, 3))
                dve.tensor_tensor(negm_p[:, :, :, 2, :], negm_r[:], negm_p[:, :, :, 1, :], ALU.subtract).then_inc(mp, 2)
                for g in range(4):
                    dve.wait_ge(a_oT, after(a_oT, i, g + 1))
                    acc = ps[:, 6 + g % 2, :].rearrange("p (t h d) -> p t h d", t=NT, h=4)
                    dve.reciprocal(rl[:, g % 2], acc[:, :, :, AD]).then_inc(a_rl, 1)
                    dve.wait_ge(a_rl, after(a_rl, i, g + 1))
                    dve.tensor_tensor(oN[:, :, 4 * g:4 * g + 4, :], acc[:, :, :, 0:AD],
                                      rl[:, g % 2].unsqueeze(3).broadcast_to([P, NT, 4, AD]), ALU.mult).then_inc(a_norm, 1)
                dve.wait_ge(a_y, after(a_y, i, 1))
                dve.tensor_tensor(x1T[:], xT[:], ps[:, 3, :], ALU.add).then_inc(a_x1, 1)
                dve.wait_ge(a_x1, after(a_x1, i, 1))
                layer_norm(1, x1T[:], cur[:])

                for l in range(LAYERS):
                    lay = i * LAYERS + l

                    def shift(src, n):
                        dve.tensor_copy(hT[0:64, :], src[0:64, :]).then_inc(f_shift, 1)
                        dve.tensor_copy(hT[64:P, 1:TOK], src[64:P, 0:TOK - 1]).then_inc(f_shift, 1)

                    if l == 0:
                        dve.wait_ge(ln_out, after(ln_out, i * LNS + 1, 1))
                    else:
                        dve.wait_ge(f_next, after(f_next, i * LAYERS, 1))
                    shift(cur, 0)
                    for u in range(2 * NT):
                        kind, t = divmod(u, NT)
                        dve.wait_ge(f_proj, after(f_proj, lay, u + 1))
                        dve.wait_ge(f_sq, after(f_sq, lay, u + 1))
                        bank = ps[:, u % 8, :]
                        dve.tensor_reduce(ss[:, 0, u, :], sqf[:, u % 2, :].rearrange("p (h d) -> p h d", h=FH),
                                          AX.X, ALU.add).then_inc(f_ss, 1)
                        if u >= 2:
                            dve.wait_ge(f_rope, after(f_rope, lay, u - 1))
                        cosb = f_rot[:, l, 2 * kind, t, :].unsqueeze(1).broadcast_to([P, FH, FD])
                        sinb = f_rot[:, l, 2 * kind + 1, t, :].unsqueeze(1).broadcast_to([P, FH, FD])
                        heads = bank.rearrange("p (h d) -> p h d", h=FH)
                        dve.tensor_tensor(t1[:, u % 2, :].rearrange("p (h d) -> p h d", h=FH), heads, cosb,
                                          ALU.mult).then_inc(f_cos, 1)
                        tv = t2[:, u % 2, :].rearrange("p (h d) -> p h d", h=FH)
                        for h in range(2):
                            a, b = slice(32 * h, 32 * h + 32), slice(32 - 32 * h, 64 - 32 * h)
                            dve.tensor_tensor(tv[:, :, a], heads[:, :, b], sinb[:, :, a], ALU.mult).then_inc(f_sin, 1)
                    dve.wait_ge(f_ss, after(f_ss, lay, 2 * NT))
                    flat = [ss[:, n].rearrange("p u h -> p (u h)") for n in range(3)]
                    dve.tensor_scalar(flat[0], flat[0], 1e-24, None, ALU.max).then_inc(f_rsqrt, 1)
                    rsqrt(dve, flat[1], flat[0], flat[2], f_rsqrt, lay)
                    dve.wait_ge(f_rsqrt, after(f_rsqrt, lay, RSQRT_STEPS))
                    for u in range(0, 2 * NT, 2):
                        dve.wait_ge(f_rope, after(f_rope, lay, u + 1))
                        rv = r[:, u, :].rearrange("p (h d) -> p h d", h=FH)
                        dve.tensor_tensor(rv, rv, ss[:, 1, u, :].unsqueeze(2).broadcast_to([P, FH, FD]),
                                          ALU.mult).then_inc(f_unit_v, 1)
                    for v in range(2 * NT + 2):
                        if v < 2 * NT:
                            dve.wait_ge(f_s, after(f_s, lay, v + 1))
                            sc = ps[:, v % 2, :].rearrange("p (c k) -> p c k", c=CH)
                            if v >= 2:
                                dve.wait_ge(f_shifted, after(f_shifted, lay, v - 1))
                            dve.tensor_reduce(nm[:, v % 2], sc, AX.X, ALU.max, negate=True).then_inc(f_max, 1)
                            dve.wait_ge(f_max, after(f_max, lay, v + 1))
                            if v >= 2:
                                dve.wait_ge(f_pT, after(f_pT, lay, v - 1))
                            dve.tensor_tensor(ex[:, v % 2], sc, nm[:, v % 2].unsqueeze(2).broadcast_to([P, CH, P]),
                                              ALU.add).then_inc(f_shifted, 1)
                        if v >= 2:
                            w = v - 2
                            t, par = divmod(w, 2)
                            dve.wait_ge(f_o, after(f_o, lay, w + 1))
                            acc = ps[:, 4 + w % 2, 0:CH * (FD + 1)].rearrange("p (c d) -> p c d", c=CH)
                            dve.reciprocal(rlf[:, w % 2], acc[:, :, FD]).then_inc(f_rl, 1)
                            dve.wait_ge(f_rl, after(f_rl, lay, w + 1))
                            if t >= 2:
                                dve.wait_ge(f_oT, after(f_oT, lay, t - 1))
                            ov = oS[:, t % 2].rearrange("p (c s) d -> p c s d", s=2)
                            dve.tensor_tensor(ov[:, :, par, :], acc[:, :, 0:FD],
                                              rlf[:, w % 2].unsqueeze(2).broadcast_to([P, CH, FD]),
                                              ALU.mult).then_inc(f_norm, 1)
                    dve.wait_ge(f_wo, after(f_wo, lay, 1))
                    dve.tensor_tensor(mid[:], cur[:], ps[:, 0, :], ALU.add).then_inc(f_mid, 1)
                    dve.wait_ge(f_mid, after(f_mid, lay, 1))
                    shift(mid, 1)
                    dve.wait_ge(f_shift, after(f_shift, lay, 4))
                    layer_norm(2 + l, hT[:], nT[:])
                    dve.wait_ge(ln_out, after(ln_out, i * LNS + 2 + l, 1))
                    dve.tensor_scalar(nT[:], nT[:], ln_gb[:, l, 0:1], ln_gb[:, l, 1:2], ALU.mult, ALU.add).then_inc(f_ln_gb, 1)
                    for j, (_, w) in enumerate(HCH):
                        dve.wait_ge(f_w1, after(f_w1, lay, len(HCH) + j + 1))
                        dve.wait_ge(f_gelu, after(f_gelu, lay, j + 1))
                        dve.scalar_tensor_tensor(hid[0:w, j, :], ps[0:w, 3 + j, :], b1[0:w, l, 0, j:j + 1],
                                                 gel[0:w, j, :], ALU.add, ALU.mult).then_inc(f_hid, 1)
                    dve.wait_ge(f_w2, after(f_w2, lay, 1))
                    dve.scalar_tensor_tensor(cur[:], ps[:, 6, :], b2[:, l:l + 1], mid[:], ALU.add, ALU.add).then_inc(f_next, 1)
                dve.wait_ge(f_next, after(f_next, i * LAYERS + 1, 1))
                dve.tensor_tensor(mid[:], cur[:], x1T[:], ALU.add).then_inc(y_sum, 1)

        @block.tensor
        def _(pe):
            def transpose4(bank, src):
                for t in range(4):
                    last = pe.transpose(ps[:, bank, P * t:P * t + P], src(t), ident[:])
                return last

            pe.wait_ge(pre_dve, 1000)
            pe.wait_ge(const_ready, 9)
            pe.wait_ge(decay_in, 16 * 12)

            with pe.Fori(0, SEQS) as i:

                def layer_norm(n, src):
                    norm = i * LNS + n
                    pe.matmul(ps[:, 0, :], mean_w[:], src, start=True, stop=True).then_inc(ln_mean, 1)
                    pe.wait_ge(ln_sq, after(ln_sq, norm, 1))
                    for t in range(NT):
                        last = pe.matmul(ps[:, 1, t:t + 1], sq[:, P * t:P * t + P], mean_w[:, 0:1], start=True, stop=True)
                    last.then_inc(ln_var, 1)
                    pe.wait_ge(ln_rsqrt, after(ln_rsqrt, norm, RSQRT_STEPS))
                    for t in range(NT):
                        last = pe.matmul(ps[:, 2, P * t:P * t + P], rstd[:, 1, t:t + 1].broadcast_to([P, P]), ident[:],
                                         start=True, stop=True)
                    last.then_inc(ln_spread, 1)

                pe.wait_ge(seq_done, after(seq_done, i, 1))
                pe.wait_ge(x_loaded, after(x_loaded, i, 16))
                transpose4(0, lambda t: x_in[:, t, :]).then_inc(xT_ps, 1)
                pe.wait_ge(xT_sb, after(xT_sb, i, 1))
                layer_norm(0, xT[:])
                pe.wait_ge(ln_out, after(ln_out, i * LNS + 0, 1))
                for u in range(4):
                    pe.matmul(ps[:, 3 + u, :], awqk[:, u, :], xn[:], start=True, stop=True).then_inc(a_proj, 1)
                for t in range(NT):
                    last = pe.matmul(ps[:, 7, P * t:P * t + P], xn[:, P * t:P * t + P], awv[:], start=True, stop=True)
                last.then_inc(a_proj, 1)
                pe.wait_ge(a_packed, after(a_packed, i, 16 * 4 * len(Q_PARTS)))
                for pr in range(PAIRS):
                    for t in range(NT):
                        u = NT * pr + t
                        if u >= 2:
                            pe.wait_ge(a_max, after(a_max, i, u - 1))
                        for h in range(2):
                            o = ps[:, 2 * (u % 2) + h, :]
                            rows = slice(64 * h, 64 * h + K_SCORE)
                            pe.matmul(o[:, 0:P * (t + 1)], qP[rows, pr, P * t:P * t + P], kP[rows, pr, 0:P * (t + 1)],
                                      start=True, stop=False)
                        for h in range(2):
                            o = ps[:, 2 * (u % 2) + h, :]
                            last = pe.matmul(o[:, P * t:P * t + P], ident_b[:], causal[:, 0, :], start=False, stop=True)
                        last.then_inc(a_s, 1)
                pe.wait_ge(a_maxparts, after(a_maxparts, i, 5))
                pe.wait_ge(a_proj, after(a_proj, i, 5))
                for t in range(NT):
                    last = pe.matmul(ps[0:6 * PAIRS, 4, P * t:P * t + P], negm_p[:, t].rearrange("p a m h -> p (a m h)"),
                                     ident_b[:], start=True, stop=True)
                last.then_inc(a_maxT, 1)
                pe.wait_ge(a_max_in, after(a_max_in, i, 32))

                def values(g):
                    pe.wait_ge(a_exp, after(a_exp, i, 6 * (g + 1)))
                    for j in range(NT):
                        col, w = SECTION[j]
                        for hh in range(4):
                            last = pe.matmul(ps[32 * hh:32 * hh + 32, 4 + g % 2, P * j:TOK], vA[:, j, 4 * g + hh, :],
                                             pT[:, hh // 2, hh % 2, col:col + w], start=(j == 0), stop=(j == NT - 1))
                    last.then_inc(a_pv, 1)

                def values_T(g):
                    pe.wait_ge(a_o_sb, after(a_o_sb, i, g + 1))
                    if g >= 2:
                        pe.wait_ge(a_norm, after(a_norm, i, g - 1))
                    transpose4(6 + g % 2, lambda t: oP[:, g % 2, P * t:P * t + P]).then_inc(a_oT, 1)

                pe.wait_ge(a_v, after(a_v, i, 1))
                for pr in range(PAIRS):
                    for n, (tiles, _, _) in enumerate(UNITS_ST):
                        u = 3 * pr + n
                        if u >= 2:
                            pe.wait_ge(a_exp, after(a_exp, i, u - 1))
                        else:
                            pe.wait_ge(a_max, after(a_max, i, PAIRS * NT))
                        off = 0
                        for k, j in enumerate(tiles):
                            w = SECTION[j][1]
                            for h in range(2):
                                rows = slice(64 * h, 64 * h + K_SHIFTED)
                                o = ps[:, 2 * (u % 2) + h, off:off + w]
                                pe.matmul(o, kP[rows, pr, P * j:P * j + P], qP[rows, pr, P * j:TOK],
                                          start=(k == 0), stop=False, skip_group_check=True)
                            for h in range(2):
                                o = ps[:, 2 * (u % 2) + h, off:off + P]
                                last = pe.matmul(o, ident_b[:], causal[:, 1, :], start=False, stop=True,
                                                 skip_group_check=True)
                            off += w
                        last.then_inc(a_st, 1)
                    if pr % 2:
                        values(pr // 2)
                        if pr >= 3:
                            values_T(pr // 2 - 1)
                values_T(3)
                pe.wait_ge(a_norm, after(a_norm, i, 4))
                transpose4(0, lambda t: oN[:, t].rearrange("p h d -> p (h d)")).then_inc(a_oN_T, 1)
                pe.wait_ge(a_oA, after(a_oA, i, 1))
                pe.matmul(ps[:, 3, :], awo[:], oA[:], start=True, stop=True).then_inc(a_y, 1)
                pe.wait_ge(a_x1, after(a_x1, i, 1))
                layer_norm(1, x1T[:])

                for l in range(LAYERS):
                    lay = i * LAYERS + l
                    pe.wait_ge(f_shift, after(f_shift, lay, 2))
                    for u in range(3 * NT):
                        kind, t = divmod(u, NT)
                        if kind == 2:
                            pe.wait_ge(f_sin, after(f_sin, lay, 2 * t + 2))
                        pe.matmul(ps[:, u % 8, :], hT[:, P * t:P * t + P],
                                  wqkv[:, l, CH * P * kind:CH * P * (kind + 1)], start=True, stop=True).then_inc(f_proj, 1)
                    pe.wait_ge(f_sin, after(f_sin, lay, 4 * NT))
                    for u in range(2 * NT):
                        if u % 2:
                            pe.wait_ge(f_unit_p, after(f_unit_p, lay, u // 2 + 1))
                        else:
                            pe.wait_ge(f_unit_v, after(f_unit_v, lay, u // 2 + 1))
                        if u >= 4:
                            pe.wait_ge(f_qkT_sb, after(f_qkT_sb, lay, u - 3))
                        transpose4(4 + u % 4, lambda c: r[:, u, P * c:P * c + P]).then_inc(f_qkT, 1)

                    def local_values(v):
                        t, par = divmod(v, 2)
                        pe.wait_ge(f_pT_sb, after(f_pT_sb, lay, v + 1))
                        if v >= 2:
                            pe.wait_ge(f_norm, after(f_norm, lay, v - 1))
                        for c in range(CH):
                            h = 2 * c + par
                            cols = slice((FD + 1) * c, (FD + 1) * (c + 1))
                            pe.matmul(ps[0:64, 4 + v % 2, cols], pTf[:, v % 2, c, 0:64], v_cross[:, t, h, :],
                                      start=True, stop=True, skip_group_check=True)
                            last = pe.matmul(ps[64:P, 4 + v % 2, cols], pTf[:, v % 2, c, 64:P], v_own[:, t, h, :],
                                             start=True, stop=True, skip_group_check=True)
                        last.then_inc(f_o, 1)

                    pe.wait_ge(f_qkT_sb, after(f_qkT_sb, lay, 2 * NT))
                    pe.wait_ge(f_v, after(f_v, lay, NT))
                    pe.wait_ge(f_v_cross, after(f_v_cross, lay, 32))
                    for v in range(2 * NT + 2):
                        if v < 2 * NT:
                            t, par = divmod(v, 2)
                            if v >= 2:
                                pe.wait_ge(f_shifted, after(f_shifted, lay, v - 1))
                            rows = slice(64 * par, 64 * par + 64)
                            pe.matmul(ps[:, v % 2, :].rearrange("p (c k) -> p c k", c=CH), ident_b[:],
                                      band[:, 0 if t else 1, :].unsqueeze(1).broadcast_to([P, CH, P]),
                                      start=True, stop=False, skip_group_check=True)
                            for c in range(CH):
                                q0 = P * t
                                even, odd = ps[0:64, v % 2, P * c:P * c + P], ps[64:P, v % 2, P * c:P * c + P]
                                pe.matmul(even[:, 0:64], qT[rows, c, q0:q0 + 64], kT[rows, c, q0 + 64:q0 + 128],
                                          start=False, stop=True, skip_group_check=True)
                                pe.matmul(even[:, 64:128], qT[rows, c, q0:q0 + 64], kT[rows, c, q0:q0 + 64],
                                          start=False, stop=True, skip_group_check=True)
                                last = pe.matmul(odd, qT[rows, c, q0 + 64:q0 + 128], kT[rows, c, q0 + 64:q0 + 192],
                                                 start=False, stop=True, skip_group_check=True)
                            last.then_inc(f_s, 1)
                        if 1 <= v <= 2 * NT:
                            w = v - 1
                            pe.wait_ge(f_exp, after(f_exp, lay, w + 1))
                            if w >= 2:
                                pe.wait_ge(f_pT_sb, after(f_pT_sb, lay, w - 1))
                            transpose4(2 + w % 2, lambda c: ex[:, w % 2, c, :]).then_inc(f_pT, 1)
                            local_values(w)
                        if v >= 3 and v % 2 == 1:
                            t = (v - 3) // 2
                            pe.wait_ge(f_norm, after(f_norm, lay, 2 * t + 2))
                            if t >= 2:
                                pe.wait_ge(f_oT_sb, after(f_oT_sb, lay, t - 1))
                            transpose4(6 + t % 2, lambda c: oS[:, t % 2, 2 * c:2 * c + 2, :].rearrange("p h d -> p (h d)")).then_inc(f_oT, 1)
                    pe.wait_ge(f_oT_sb, after(f_oT_sb, lay, NT))
                    for c in range(CH):
                        last = pe.matmul(ps[:, 0, :], wo[:, l, c, :], oT[:, c, :], start=(c == 0), stop=(c == CH - 1))
                    last.then_inc(f_wo, 1)
                    pe.wait_ge(f_shift, after(f_shift, lay, 4))
                    layer_norm(2 + l, hT[:])
                    pe.wait_ge(f_ln_gb, after(f_ln_gb, lay, 1))
                    for n, half in ((0, 1), (1, 0)):
                        for j, (j0, w) in enumerate(HCH):
                            pe.matmul(ps[0:w, 3 * n + j, :], w1[:, l, HID * half + j0:HID * half + j0 + w], nT[:],
                                      start=True, stop=True).then_inc(f_w1, 1)
                    pe.wait_ge(f_hid, after(f_hid, lay, len(HCH)))
                    for j, (j0, w) in enumerate(HCH):
                        last = pe.matmul(ps[:, 6, :], w2[0:w, l, j, :], hid[0:w, j, :], start=(j == 0), stop=(j == len(HCH) - 1))
                    last.then_inc(f_w2, 1)
                pe.wait_ge(y_sum, after(y_sum, i, 1))
                transpose4(7, lambda t: mid[:, P * t:P * t + P]).then_inc(y_ps, 1)


def kernel(L0_attn_x, L0_attn_Wqkv, L0_attn_Wo, L0_attn_log_xi, L0_attn_pi_gate_logit,
           L0_attn_e_gate_logit, L0_ffn_wqkv, L0_ffn_q_scale, L0_ffn_k_scale, L0_ffn_wo,
           L0_ffn_ln_g, L0_ffn_ln_b, L0_ffn_w1, L0_ffn_b1, L0_ffn_w2, L0_ffn_b2):
    import math

    import numpy as np
    import concourse.bacc as bacc
    from concourse.bass_utils import run_bass_kernel_spmd

    f32 = np.float32
    rows = np.arange(P)
    par, dim, pair = rows // 64, (rows % 64) // PAIRS, rows % PAIRS
    head = 2 * pair + par
    order = np.array([2 * p + a for a in range(2) for p in range(PAIRS)])

    neg = f32(-1e30)
    q_, k_ = np.arange(P)[:, None], np.arange(P)[None, :]
    causal = np.stack([np.where(k_ <= q_, f32(0), neg), np.where(k_ >= q_, f32(0), neg)], 1).astype(f32)
    a, b = np.arange(WIN)[:, None], np.arange(WIN)[None, :]
    own, before = np.where(b <= a, f32(0), neg), np.where(b >= a, f32(0), neg)
    none = np.full((WIN, WIN), neg)
    band = np.stack([np.block([[own, before], [before, own]]), np.block([[own, none], [before, own]])], 1).astype(f32)
    kfrac = np.arange(0, AD, 2, dtype=f32) / f32(AD)
    inv = (f32(math.pi) ** (f32(1.0) - kfrac)).astype(f32)
    pos = np.arange(TOK, dtype=f32)
    posfreq = (pos[None, :] * inv[dim // 2][:, None]).astype(f32)
    sign = np.where(dim % 2 == 0, f32(-1), f32(1)).astype(f32)[:, None]
    half = np.arange(0, FD, 2, dtype=f32)
    inv_freq = (f32(1.0) / (f32(10000.0) ** (half / f32(FD)))).astype(f32)
    freqs = (pos[:, None] * inv_freq[None, :]).astype(f32)
    freqs = np.concatenate([freqs, freqs], -1).astype(np.float64)
    base = (half + f32(0.4 * FD)) / f32(1.4 * FD)
    power = (pos - f32(TOK // 2)) / f32(WIN // 2)
    scale = (base[None, :] ** power[:, None]).astype(f32)
    scale = np.concatenate([scale, scale], -1).astype(np.float64)
    rsign = np.where(np.arange(FD) < FD // 2, -1.0, 1.0)
    cos, sin = np.cos(freqs), np.sin(freqs) * rsign
    rope = np.stack([8.0 * cos * scale, 8.0 * sin * scale, cos / scale, sin / scale]).astype(f32)
    rope = rope.reshape(4, NT, P, FD).transpose(2, 0, 1, 3)

    W = np.asarray(L0_attn_Wqkv)
    at = head * AD + dim
    swapped = head * AD + (dim ^ 1)
    awqk = np.stack([W[at].T, W[swapped].T, W[DM + at].T, W[DM + swapped].T], 1)
    b1 = np.zeros((LAYERS, P, 2, len(HCH)), f32)
    for j, (j0, w) in enumerate(HCH):
        for s in range(2):
            b1[:, :w, s, j] = np.asarray(L0_ffn_b1)[:, HID * s + j0:HID * s + j0 + w]
    qk = np.stack([np.asarray(L0_ffn_q_scale), np.asarray(L0_ffn_k_scale)], 1)
    arrays = {
        "x": np.asarray(L0_attn_x),
        "ident": np.eye(P, dtype=f32), "causal": causal, "band": band, "posfreq": posfreq,
        "pos": np.broadcast_to(pos, (AH, TOK)), "sign": sign, "rope": rope,
        "awqk": awqk, "awv": W[2 * DM:].T, "awo": np.asarray(L0_attn_Wo).T,
        "pi_gate": np.asarray(L0_attn_pi_gate_logit)[head][:, None],
        "log_xi": np.asarray(L0_attn_log_xi)[order][:, None],
        "e_gate": np.asarray(L0_attn_e_gate_logit)[order][:, None],
        "wqkv": np.asarray(L0_ffn_wqkv), "wo": np.asarray(L0_ffn_wo), "w1": np.asarray(L0_ffn_w1),
        "w2": np.asarray(L0_ffn_w2), "qkscale": np.broadcast_to(qk[None], (P,) + qk.shape),
        "ln_gb": np.stack([np.asarray(L0_ffn_ln_g).T, np.asarray(L0_ffn_ln_b).T], 2), "b1": b1,
        "b2": np.asarray(L0_ffn_b2).T,
    }
    arrays = {f"in_{k}": np.ascontiguousarray(v) for k, v in arrays.items()}
    nc = bacc.Bacc("TRN2", target_bir_lowering=False, num_devices=1)
    d = {k[3:]: nc.dram_tensor(k, v.shape, mybir.dt.from_np(v.dtype), kind="ExternalInput").ap()
         for k, v in arrays.items()}
    out = nc.dram_tensor("out", (SEQS, TOK, DM), F32, kind="ExternalOutput").ap()
    build(nc, d["x"],
          [d[k] for k in ("ident", "causal", "band", "posfreq", "pos", "sign", "rope")],
          [d[k] for k in ("awqk", "awv", "awo")], [d[k] for k in ("pi_gate", "log_xi", "e_gate")],
          [d[k] for k in ("wqkv", "wo", "w1", "w2")],
          [d[k] for k in ("qkscale", "ln_gb", "b1", "b2")], out)
    r = run_bass_kernel_spmd(nc, [arrays], core_ids=[0])
    return r.results[0]["out"]
```

```python
from contextlib import ExitStack

import concourse.bass as bass
from concourse import mybir

F32 = mybir.dt.float32
BF16 = mybir.dt.bfloat16
I32 = mybir.dt.int32
ALU = mybir.AluOpType
ACT = mybir.ActivationFunctionType
AX = mybir.AxisListType

P = 128
SEQS, TOK, DM = 8, 512, 128
NT = TOK // P
AH, AD = 16, 8
PAIRS = AH // 2
LAYERS, FH, FD = 2, 8, 64
CH = FH // 2
WIN = 64
HID = int(DM * 4 * 2 / 3)
HCH = [(j * P, min(P, HID - j * P)) for j in range((HID + P - 1) // P)]
LNS = 2 + LAYERS
Q_PARTS, K_PARTS = (0, 0, 1, 1, 0, 2), (0, 1, 0, 1, 2, 0)
DECAY_ROW = len(Q_PARTS) * AD
MAX_ROW = DECAY_ROW + 6
K_SCORE, K_SHIFTED = MAX_ROW, MAX_ROW + 3
RSQRT_MAGIC = 0x5F3759DF
NEWTON = 3
RSQRT_STEPS = 2 + 3 * NEWTON
SECTION = {0: (0, 512), 1: (512, 384), 3: (896, 128), 2: (1024, 256)}
PT_COLS = 1280
PASS = [((0,), 0, 512), ((1, 3), 512, 512), ((2,), 1024, 256)]
GROUP = 4
GROUPS = AH // GROUP
ST_UNITS = len(PASS) * GROUP

A_SPREAD = 7
A_PROJ = 9
A_S = A_PROJ + 13
S_SLOTS = [slot for h in (0, 1, 4, 5, 8, 9, 12, 13)
           for slot in (((h, 3, 0),), ((h, 2, 0), (h, 0, 384)), ((h + 2, 3, 0),),
                        ((h + 2, 2, 0), (h + 2, 0, 384)), ((h, 1, 0), (h + 2, 1, 256)))]
SLOTS_PAIR = len(S_SLOTS) // PAIRS
S_MAXIMA = [7 * (n // SLOTS_PAIR) + (1, 3, 4, 6, 7)[n % SLOTS_PAIR] for n in range(len(S_SLOTS))]
A_MAXT = A_S + len(S_SLOTS) + 1
A_ST = A_MAXT + 5
A_TAIL = A_ST + GROUPS * ST_UNITS
A_TICKS = A_TAIL + 17
F_RSQRT, F_QKT, F_ATT = 11, 13, 18
F_WO = F_ATT + 13
F_LN = F_WO + 2
F_MLP = F_LN + 7
F_LAYER = F_MLP + 7
F_TICKS = LAYERS * F_LAYER + 3
W_A, W_PACK, W_S, W_MAXT, W_ST = 0.98, 2.77, 0.8, 1.0, 1.18
W_F, W_PROJ, W_ATT, W_MLP = 1.22, 1.82, 2.55, 1.95
A_UNTIL = 0.94


def merged():
    a = [W_A] * A_TICKS
    for k in range(A_PROJ + 7, A_S + 1):
        a[k] = W_PACK
    for k in range(len(S_SLOTS)):
        a[A_S + 1 + k] = W_S
    for k in range(A_MAXT, A_ST + 1):
        a[k] = W_MAXT
    for k in range(GROUPS * ST_UNITS):
        a[A_ST + 1 + k] = W_ST
    f = [W_F] * F_TICKS
    for l in range(LAYERS):
        for k in range(1, 13):
            f[F_LAYER * l + k] = W_PROJ
        for k in range(13):
            f[F_LAYER * l + F_ATT + k] = W_ATT
        for k in (F_WO, F_MLP, F_MLP + 1, F_MLP + 5):
            f[F_LAYER * l + k] = W_MLP
    at = []
    for who, cost, until in (("A", a, A_UNTIL), ("F", f, 1.0)):
        done, total = 0.0, sum(cost)
        for k, c in enumerate(cost):
            at.append((until * done / total, who, k))
            done += c
    return [(who, k) for _, who, k in sorted(at)]




def build(nc, x, consts, a_w, a_vec, f_w, f_vec, out):
    (ident_d, causal_d, band_d, posfreq_d, pos_d, sign_d, rope_d) = consts
    (awqk_d, awv_d, awo_d) = a_w
    (pi_gate_d, log_xi_d, e_gate_d) = a_vec
    (wqkv_d, wo_d, w1_d, w2_d) = f_w
    (qkscale_d, ln_gb_d, b1_d, b2_d) = f_vec

    with ExitStack() as ctx:
        def sb(name, shape, dt=F32):
            return ctx.enter_context(nc.sbuf_tensor(name, shape, dt))

        ident = sb("ident", [P, P])
        ident_b = sb("ident_b", [P, P], BF16)
        causal = sb("causal", [P, 2, P], BF16)
        band = sb("band", [P, 2, P], BF16)
        mean_w = sb("mean_w", [P, P])
        awqk = sb("awqk", [P, 4, P])
        awv = sb("awv", [P, P])
        awo = sb("awo", [P, P])
        wqkv = sb("wqkv", [P, LAYERS, 3 * CH * P])
        wo = sb("wo", [P, LAYERS, CH, P])
        w1 = sb("w1", [P, LAYERS, 2 * HID])
        w2 = sb("w2", [P, LAYERS, len(HCH), P])
        ln_gb = sb("ln_gb", [P, LAYERS, 2])
        b1 = sb("b1", [P, LAYERS, 2, len(HCH)])
        b2 = sb("b2", [P, LAYERS])
        a_rot = sb("a_rot", [P, 4, TOK])
        f_rot = sb("f_rot", [P, LAYERS, 4, NT, FD])
        qkscale = sb("qkscale", [P, LAYERS, 2, FD])
        gate = sb("gate", [P, 4])
        sign = sb("sign", [P, 1])
        dec = sb("dec", [AH, 8])

        x_in = sb("x_in", [P, NT, DM])
        xT = sb("xT", [P, TOK])
        sq = sb("sq", [P, TOK])
        rstd = sb("rstd", [P, 3, NT])
        xn = sb("xn", [P, TOK])
        prod = sb("prod", [P, 4, TOK])
        rot = sb("rot", [P, 2, TOK])
        part = sb("part", [P, 2, 3, TOK], BF16)
        qP = sb("qP", [P, PAIRS, TOK], BF16)
        kP = sb("kP", [P, PAIRS, TOK], BF16)
        negm = sb("negm", [P, NT, 2, PAIRS])
        negm_r = sb("negm_r", [P, NT, 2, PAIRS])
        negm_p = sb("negm_p", [P, NT, 2, 3, PAIRS], BF16)
        mT = sb("mT", [2 * 3 * PAIRS, TOK], BF16)
        vA = sb("vA", [P, NT, AH, 32])
        pT = sb("pT", [P, GROUP, PT_COLS])
        oP = sb("oP", [P, TOK])
        rl = sb("rl", [P, 2, NT, GROUP])
        oN = sb("oN", [P, NT, AH, AD])
        oA = sb("oA", [P, TOK])
        x1T = sb("x1T", [P, TOK])
        xf = sb("xf", [P, TOK])

        res = sb("res", [P, TOK])
        cur = sb("cur", [P, TOK])
        hT = sb("hT", [P, TOK])
        rstd_f = sb("rstd_f", [P, 3, NT])
        sqf = sb("sqf", [P, 2, CH * P])
        t1 = sb("t1", [P, 2, CH * P])
        t2 = sb("t2", [P, 2, CH * P])
        ss = sb("ss", [P, 3, 2 * NT, FH])
        r = sb("r", [P, 2 * NT, CH * P])
        ex = t1[:].rearrange("p b (c k) -> p b c k", c=CH)
        pTf = t2[:].rearrange("p b (c k) -> p b c k", c=CH)
        oS = sqf[:].rearrange("p b (h d) -> p b h d", h=FH)
        oT = r[:, 0:CH, :]
        gel = r[:, 0:len(HCH), :]
        hid = r[:, len(HCH):2 * len(HCH), :]
        rope = r[:, 0:2, :].rearrange("p a (b t d) -> p (a b) t d", t=NT, d=FD)
        causal_f = r[:, 2, 0:2 * P].rearrange("p (a k) -> p a k", a=2)
        band_f = r[:, 3, 0:2 * P].rearrange("p (a k) -> p a k", a=2)
        qT = sb("qT", [P, CH, TOK])
        kT = sb("kT", [P, CH, WIN + TOK])
        v_own = sb("v_own", [P, NT, FH, FD + 1])
        v_cross = sb("v_cross", [P, NT, FH, FD + 1])
        nm = sb("nm", [P, 2, CH])
        rlf = sb("rlf", [P, 2, CH])
        mid = sb("mid", [P, TOK])
        nT = sb("nT", [P, TOK])
        ob = sb("ob", [P, NT, DM])

        ps = ctx.enter_context(nc.psum_tensor("ps", [P, 8, 512], F32))
        F_BANKS = 5

        def fbank(n):
            return ps[:, 3 + n % F_BANKS, :]

        per_round = {}

        def sem(name, per):
            s = ctx.enter_context(nc.semaphore(name))
            per_round[id(s)] = per
            return s

        def after(s, rnd, n):
            return rnd * per_round[id(s)] + n

        const_in = sem("const_in", 0)
        const_ready = sem("const_ready", 0)
        pre_dve = sem("pre_dve", 0)
        pre_act = sem("pre_act", 0)
        decay_in = sem("decay_in", 0)
        x_loaded = sem("x_loaded", 16)
        xT_ps = sem("xT_ps", 1)
        xT_sb = sem("xT_sb", 1)
        a_ln_mean = sem("a_ln_mean", 2)
        a_ln_cent = sem("a_ln_cent", 2)
        a_ln_sq = sem("a_ln_sq", 2)
        a_ln_var = sem("a_ln_var", 2)
        a_ln_rsqrt = sem("a_ln_rsqrt", 2 * RSQRT_STEPS)
        a_ln_spread = sem("a_ln_spread", 2)
        a_ln_out = sem("a_ln_out", 2)
        a_proj = sem("a_proj", 5)
        a_prod = sem("a_prod", 4)
        a_rot_sum = sem("a_rot_sum", 2)
        a_hi = sem("a_hi", 2)
        a_rest = sem("a_rest", 2)
        a_mid = sem("a_mid", 2)
        a_lo = sem("a_lo", 2)
        a_packed = sem("a_packed", 16 * 4 * len(Q_PARTS))
        a_v = sem("a_v", 1)
        a_s = sem("a_s", len(S_SLOTS))
        a_max = sem("a_max", S_MAXIMA[-1])
        a_maxparts = sem("a_maxparts", 4)
        a_maxT = sem("a_maxT", 1)
        a_maxT_sb = sem("a_maxT_sb", 1)
        a_max_in = sem("a_max_in", 32)
        a_st = sem("a_st", GROUPS * ST_UNITS)
        a_exp = sem("a_exp", GROUPS * ST_UNITS)
        a_pv = sem("a_pv", GROUPS)
        a_o_sb = sem("a_o_sb", GROUPS)
        a_oT = sem("a_oT", GROUPS)
        a_rl = sem("a_rl", GROUPS)
        a_norm = sem("a_norm", GROUPS)
        a_oN_T = sem("a_oN_T", 1)
        a_oA = sem("a_oA", 1)
        a_y = sem("a_y", 1)
        a_x1 = sem("a_x1", 1)
        res_kept = sem("res_kept", 1)
        f_shift = sem("f_shift", 4)
        f_proj = sem("f_proj", 3 * NT)
        f_sq = sem("f_sq", 2 * NT)
        f_ss = sem("f_ss", 2 * NT)
        f_cos = sem("f_cos", 2 * NT)
        f_sin = sem("f_sin", 4 * NT)
        f_rope = sem("f_rope", 2 * NT)
        f_rsqrt = sem("f_rsqrt", RSQRT_STEPS)
        f_unit_v = sem("f_unit_v", NT)
        f_unit_p = sem("f_unit_p", NT)
        f_qkT = sem("f_qkT", 2 * NT)
        f_qkT_sb = sem("f_qkT_sb", 2 * NT)
        f_v = sem("f_v", NT)
        f_v_cross = sem("f_v_cross", 32)
        f_s = sem("f_s", 2 * NT)
        f_max = sem("f_max", 2 * NT)
        f_shifted = sem("f_shifted", 2 * NT)
        f_exp = sem("f_exp", 2 * NT)
        f_pT = sem("f_pT", 2 * NT)
        f_pT_sb = sem("f_pT_sb", 2 * NT)
        f_o = sem("f_o", 2 * NT)
        f_rl = sem("f_rl", 2 * NT)
        f_norm = sem("f_norm", 2 * NT)
        f_oT = sem("f_oT", NT)
        f_oT_sb = sem("f_oT_sb", NT)
        f_wo = sem("f_wo", 1)
        f_mid = sem("f_mid", 1)
        f_ln_mean = sem("f_ln_mean", 1)
        f_ln_cent = sem("f_ln_cent", 1)
        f_ln_sq = sem("f_ln_sq", 1)
        f_ln_var = sem("f_ln_var", 1)
        f_ln_rsqrt = sem("f_ln_rsqrt", RSQRT_STEPS)
        f_ln_spread = sem("f_ln_spread", 1)
        f_ln_out = sem("f_ln_out", 1)
        f_ln_gb = sem("f_ln_gb", 1)
        f_w1 = sem("f_w1", 2 * len(HCH))
        f_gelu = sem("f_gelu", len(HCH))
        f_hid = sem("f_hid", len(HCH))
        f_w2 = sem("f_w2", 1)
        f_next = sem("f_next", 1)
        y_sum = sem("y_sum", 1)
        y_ps = sem("y_ps", 1)
        y_sb = sem("y_sb", 1)
        y_out = sem("y_out", 16)

        def rsqrt(eng, y, s, a, steps, rnd, n0):
            n = n0 + 1
            eng.wait_ge(steps, after(steps, rnd, n))
            eng.tensor_scalar(y.bitcast(I32), s.bitcast(I32), -0.5, float(RSQRT_MAGIC),
                              ALU.mult, ALU.add).then_inc(steps, 1)
            for _ in range(NEWTON):
                n += 1
                eng.wait_ge(steps, after(steps, rnd, n))
                eng.tensor_tensor(a, y, y, ALU.mult).then_inc(steps, 1)
                n += 1
                eng.wait_ge(steps, after(steps, rnd, n))
                eng.scalar_tensor_tensor(a, a, -0.5, s, ALU.mult, ALU.mult).then_inc(steps, 1)
                n += 1
                eng.wait_ge(steps, after(steps, rnd, n))
                eng.scalar_tensor_tensor(y, a, 1.5, y, ALU.add, ALU.mult).then_inc(steps, 1)
            assert n + 1 == n0 + RSQRT_STEPS

        ring = []
        for g in range(GROUPS + 1):
            for n in range(ST_UNITS if g < GROUPS else 0):
                ring.append(("st", ST_UNITS * g + n))
                if n == 4 and g:
                    ring.append(("oT", g - 1))
            if g == GROUPS:
                ring.append(("oT", g - 1))
        ring_at = {what: n for n, what in enumerate(ring)}

        def ring_bank(what):
            return ps[:, ring_at[what] % 2, :]

        MERGED = merged()
        ALONE_A = [("A", k) for k in range(A_TICKS)]
        ALONE_F = [("F", k) for k in range(F_TICKS)]
        N_CONST = 16 * (16 + 6 * LAYERS)
        block = ctx.enter_context(nc.Block())

        @block.sync
        def _(sp):
            loads = [(ident[:], ident_d), (causal_f, causal_d), (band_f, band_d), (sign[:], sign_d),
                     (prod[:, 0, :], posfreq_d), (gate[:, 0:1], pi_gate_d),
                     (dec[:, 0:1], log_xi_d), (dec[:, 1:2], e_gate_d), (prod[0:AH, 1, :], pos_d),
                     (awqk[:], awqk_d), (awv[:], awv_d), (awo[:], awo_d), (rope, rope_d),
                     (qkscale[:], qkscale_d), (b2[:], b2_d), (ln_gb[:], ln_gb_d)]
            for dst, src in loads:
                sp.dma_start(dst, src).then_inc(const_in, 16)
            full = (HID // P) * P
            for l in range(LAYERS):
                sp.dma_start(wqkv[:, l, :], wqkv_d[l]).then_inc(const_in, 16)
                sp.dma_start(wo[:, l], wo_d[l].rearrange("(c p) d -> p c d", p=P)).then_inc(const_in, 16)
                sp.dma_start(w1[:, l, :], w1_d[l]).then_inc(const_in, 16)
                sp.dma_start(w2[:, l, 0:HID // P, :],
                             w2_d[l, 0:full].rearrange("(c p) d -> p c d", p=P)).then_inc(const_in, 16)
                sp.dma_start(w2[0:HID - full, l, HID // P, :], w2_d[l, full:HID]).then_inc(const_in, 16)
                sp.dma_start(b1[:, l], b1_d[l]).then_inc(const_in, 16)
            sp.dma_start(x_in[:], x[0].rearrange("(t p) d -> p t d", p=P)).then_inc(x_loaded, 16)

            sp.wait_ge(pre_dve, 1000)
            for side, (dst, row0) in enumerate(((qP, DECAY_ROW), (kP, DECAY_ROW + 3))):
                for par in range(2):
                    for p3 in range(3):
                        row = 64 * par + row0 + p3
                        sp.dma_start(dst[row:row + 1, :, :],
                                     part[PAIRS * par:PAIRS * par + PAIRS, side, p3, :]).then_inc(decay_in, 16)
            sp.wait_ge(decay_in, 16 * 12)

            def pack(i):
                for side, (dst, order) in enumerate(((qP, Q_PARTS), (kP, K_PARTS))):
                    sp.wait_ge(a_lo, after(a_lo, i, side + 1))
                    sp.wait_ge(a_mid, after(a_mid, i, side + 1))
                    sp.wait_ge(a_hi, after(a_hi, i, side + 1))
                    for par in range(2):
                        for seg, p3 in enumerate(order):
                            row = 64 * par + AD * seg
                            sp.dma_start(dst[row:row + AD, :, :],
                                         part[64 * par:64 * par + 64, side, p3, :]).then_inc(a_packed, 16)

            def pack_max(i):
                sp.wait_ge(a_maxT_sb, after(a_maxT_sb, i, 1))
                for par in range(2):
                    row = 64 * par + MAX_ROW
                    sp.dma_start(qP[row:row + 3, :, :], mT[3 * PAIRS * par:3 * PAIRS * (par + 1), :]).then_inc(a_max_in, 16)

            with sp.Fori(0, SEQS - 1) as i:
                pack(i)
                sp.wait_ge(xT_ps, after(xT_ps, i, 1))
                sp.dma_start(x_in[:], x[i + 1].rearrange("(t p) d -> p t d", p=P)).then_inc(x_loaded, 16)
                pack_max(i)
            pack(SEQS - 1)
            pack_max(SEQS - 1)

        @block.gpsimd
        def _(pool):
            fills = [(qP[:], 1.0), (kP[:], 1.0), (vA[:], 0.0), (mean_w[:], 1.0 / DM), (kT[:], 0.0),
                     (hT[:], 0.0), (v_own[:], 1.0), (v_cross[:], 0.0)]
            for dst, val in fills:
                pool.memset(dst, val).then_inc(const_ready, 1)
            pool.wait_ge(const_ready, 3)
            pool.memset(vA[:, :, :, AD:AD + 1], 1.0).then_inc(const_ready, 1)

            def layers(k, i):
                l, k = divmod(k, F_LAYER)
                lay = i * LAYERS + l
                if l == LAYERS:
                    return
                if 4 <= k < 4 + 2 * NT:
                    u = k - 4
                    pool.wait_ge(f_cos, after(f_cos, lay, u + 1))
                    pool.wait_ge(f_sin, after(f_sin, lay, 2 * u + 2))
                    pool.tensor_tensor(r[:, u, :], t1[:, u % 2, :], t2[:, u % 2, :], ALU.add).then_inc(f_rope, 1)
                if F_RSQRT < k <= F_RSQRT + NT:
                    u = 2 * (k - F_RSQRT) - 1
                    pool.wait_ge(f_rsqrt, after(f_rsqrt, lay, RSQRT_STEPS))
                    pool.wait_ge(f_rope, after(f_rope, lay, u + 1))
                    rv = r[:, u, :].rearrange("p (h d) -> p h d", h=FH)
                    pool.tensor_tensor(rv, rv, ss[:, 1, u, :].unsqueeze(2).broadcast_to([P, FH, FD]),
                                       ALU.mult).then_inc(f_unit_p, 1)

            with pool.Fori(0, SEQS - 1) as i:
                for who, k in ALONE_F:
                    layers(k, i)
            for who, k in ALONE_F:
                layers(k, SEQS - 1)

        @block.scalar
        def _(act):
            act.wait_ge(const_in, N_CONST)
            act.activation(gate[:, 1:2], gate[:, 0:1], ACT.Exp, scale=-1.0).then_inc(pre_act, 1)
            act.activation(dec[:, 2:4], dec[:, 0:2], ACT.Exp, scale=-1.0).then_inc(pre_act, 1)
            act.wait_ge(pre_dve, 100)
            act.activation(a_rot[:, 0, :], a_rot[:, 2, :], ACT.Sin).then_inc(pre_act, 1)
            act.activation(a_rot[:, 1, :], a_rot[:, 3, :], ACT.Sin).then_inc(pre_act, 1)
            act.wait_ge(pre_dve, 1000)
            act.sem_inc(y_sum, 1)
            act.sem_inc(y_sb, 1)
            act.sem_inc(y_out, 16)

            def attention(k, i):
                if k == 1:
                    act.wait_ge(xT_ps, after(xT_ps, i, 1))
                    act.copy(xT[:], ps[:, 0, :]).then_inc(xT_sb, 1)
                if k == 4:
                    act.wait_ge(a_ln_cent, after(a_ln_cent, i, 1))
                    act.activation(sq[:], xn[:], ACT.Square).then_inc(a_ln_sq, 1)
                if k == A_PROJ + 2:
                    act.wait_ge(a_rot_sum, after(a_rot_sum, i, 1))
                    act.copy(part[:, 0, 0, :], rot[:, 0, :]).then_inc(a_hi, 1)
                if k == A_PROJ + 3:
                    act.wait_ge(a_proj, after(a_proj, i, 5))
                    act.copy(vA[:, :, :, 0:AD], ps[:, 2, :].rearrange("p (t h d) -> p t h d", t=NT, h=AH)).then_inc(a_v, 1)
                if k == A_PROJ + 4:
                    act.wait_ge(a_rest, after(a_rest, i, 1))
                    act.copy(part[:, 0, 1, :], rot[:, 0, :]).then_inc(a_mid, 1)
                    act.wait_ge(a_rot_sum, after(a_rot_sum, i, 2))
                    act.copy(part[:, 1, 0, :], rot[:, 1, :]).then_inc(a_hi, 1)
                if k == A_PROJ + 6:
                    act.wait_ge(a_rest, after(a_rest, i, 2))
                    act.copy(part[:, 1, 1, :], rot[:, 1, :]).then_inc(a_mid, 1)
                if k == A_MAXT + 1:
                    act.wait_ge(a_maxT, after(a_maxT, i, 1))
                    act.copy(mT[:], ps[0:6 * PAIRS, 0, :]).then_inc(a_maxT_sb, 1)
                m = k - A_ST
                if 1 <= m <= GROUPS * ST_UNITS:
                    g, n = divmod(m - 1, ST_UNITS)
                    _, col, w = PASS[n // GROUP]
                    act.wait_ge(a_st, after(a_st, i, m))
                    if g:
                        act.wait_ge(a_pv, after(a_pv, i, g))
                    act.activation(pT[:, n % GROUP, col:col + w], ring_bank(("st", m - 1))[:, 0:w],
                                   ACT.Exp).then_inc(a_exp, 1)
                g, n = divmod(m, ST_UNITS)
                if n == 2 and 1 <= g <= GROUPS:
                    act.wait_ge(a_pv, after(a_pv, i, g))
                    if g >= 2:
                        act.wait_ge(a_oT, after(a_oT, i, g - 1))
                    act.copy(oP[:], ps[:, 2, :]).then_inc(a_o_sb, 1)
                if k == A_TAIL + 7:
                    act.wait_ge(a_oN_T, after(a_oN_T, i, 1))
                    act.copy(oA[:], ps[:, 2, :]).then_inc(a_oA, 1)
                if k == A_TAIL + 12:
                    act.wait_ge(a_ln_cent, after(a_ln_cent, i, 2))
                    act.activation(sq[:], xf[:], ACT.Square).then_inc(a_ln_sq, 1)

            def layers(k, i):
                l, k = divmod(k, F_LAYER)
                lay = i * LAYERS + l
                if l == LAYERS:
                    if k == 2:
                        act.wait_ge(y_ps, after(y_ps, i, 1))
                        act.wait_ge(y_out, after(y_out, i, 16))
                        act.copy(ob[:], fbank(0).rearrange("p (t d) -> p t d", t=NT)).then_inc(y_sb, 1)
                        act.wait_ge(y_sb, after(y_sb, i, 2))
                        act.dma_start(out[i].rearrange("(t p) d -> p t d", p=P), ob[:]).then_inc(y_out, 16)
                    return
                if 2 <= k < 2 + 2 * NT:
                    u = k - 2
                    act.wait_ge(f_proj, after(f_proj, lay, u + 1))
                    if u >= 2:
                        act.wait_ge(f_ss, after(f_ss, lay, u - 1))
                    act.activation(sqf[:, u % 2, :], fbank(u), ACT.Square).then_inc(f_sq, 1)
                if 2 + 2 * NT <= k < 2 + 3 * NT:
                    u = k - 2
                    t = u - 2 * NT
                    act.wait_ge(f_proj, after(f_proj, lay, u + 1))
                    act.copy(v_own[:, t, :, 0:FD], fbank(u).rearrange("p (h d) -> p h d", h=FH)).then_inc(f_v, 1)
                if F_QKT < k <= F_QKT + NT:
                    for u in (2 * (k - F_QKT) - 2, 2 * (k - F_QKT) - 1):
                        act.wait_ge(f_qkT, after(f_qkT, lay, u + 1))
                        t = u % NT
                        dst = qT[:, :, P * t:P * t + P] if u < NT else kT[:, :, WIN + P * t:WIN + P * t + P]
                        act.copy(dst, fbank(3 * NT + u).rearrange("p (c q) -> p c q", c=CH)).then_inc(f_qkT_sb, 1)
                if k == F_QKT + 2:
                    act.wait_ge(f_v, after(f_v, lay, NT))
                    act.dma_start(v_cross[WIN:P, :, :, :], v_own[0:WIN, :, :, :]).then_inc(f_v_cross, 16)
                    act.dma_start(v_cross[0:WIN, 1:NT, :, :], v_own[WIN:P, 0:NT - 1, :, :]).then_inc(f_v_cross, 16)
                v = k - F_ATT
                if 1 <= v <= 2 * NT:
                    w = v - 1
                    act.wait_ge(f_shifted, after(f_shifted, lay, w + 1))
                    act.activation(ex[:, w % 2], ex[:, w % 2], ACT.Exp).then_inc(f_exp, 1)
                if 2 <= v < 2 + 2 * NT:
                    w = v - 2
                    act.wait_ge(f_pT, after(f_pT, lay, w + 1))
                    if w >= 2:
                        act.wait_ge(f_o, after(f_o, lay, w - 1))
                    act.copy(pTf[:, w % 2], fbank(2).rearrange("p (c q) -> p c q", c=CH)).then_inc(f_pT_sb, 1)
                if 6 <= v < 6 + 2 * NT and v % 2 == 0:
                    t = (v - 6) // 2
                    act.wait_ge(f_oT, after(f_oT, lay, t + 1))
                    act.copy(oT[:, :, P * t:P * t + P], fbank(4).rearrange("p (c q) -> p c q", c=CH)).then_inc(f_oT_sb, 1)
                if k == F_LN + 2:
                    act.wait_ge(f_ln_cent, after(f_ln_cent, lay, 1))
                    act.activation(sqf[:, 0, :], nT[:], ACT.Square).then_inc(f_ln_sq, 1)
                if k == F_MLP + 2:
                    for j, (_, w) in enumerate(HCH):
                        act.wait_ge(f_w1, after(f_w1, lay, j + 1))
                        act.activation(gel[0:w, j, :], fbank(3 + j)[0:w], ACT.Gelu, bias=b1[0:w, l, 1, j:j + 1]).then_inc(f_gelu, 1)

            for who, k in ALONE_A:
                attention(k, 0)
            with act.Fori(0, SEQS - 1) as i:
                for who, k in MERGED:
                    if who == "A":
                        attention(k, i + 1)
                    else:
                        layers(k, i)
            for who, k in ALONE_F:
                layers(k, SEQS - 1)
            act.wait_ge(y_out, 16 * (SEQS + 1))

        @block.vector
        def _(dve):
            pd = pre_dve
            cnt = [0]

            def link(ins):
                cnt[0] += 1
                ins.then_inc(pd, 1)
                dve.wait_ge(pd, cnt[0])

            dve.wait_ge(const_in, N_CONST)
            dve.wait_ge(const_ready, 9)
            link(dve.tensor_copy(ident_b[:], ident[:]))
            link(dve.tensor_copy(causal[:], causal_f))
            link(dve.tensor_copy(band[:], band_f))
            for l in range(LAYERS):
                for k in range(2):
                    sc = qkscale[:, l, k, :].unsqueeze(1).broadcast_to([P, NT, FD])
                    link(dve.tensor_tensor(f_rot[:, l, 2 * k], rope[:, 2 * k], sc, ALU.mult))
                    for h in range(2):
                        a, b = slice(32 * h, 32 * h + 32), slice(32 - 32 * h, 64 - 32 * h)
                        link(dve.tensor_tensor(f_rot[:, l, 2 * k + 1, :, a], rope[:, 2 * k + 1, :, a],
                                               sc[:, :, b], ALU.mult))
            dve.wait_ge(pre_act, 2)
            link(dve.tensor_scalar(gate[:, 2:3], gate[:, 1:2], 1.0, None, ALU.add))
            link(dve.reciprocal(gate[:, 3:4], gate[:, 2:3]))
            theta = prod[:, 2, :]
            link(dve.tensor_scalar(theta, prod[:, 0, :], gate[:, 3:4], None, ALU.mult))
            TWO_PI = 6.283185307179586
            c1 = 6.28125
            c2 = 0.0019350051879882812
            c3 = TWO_PI - c1 - c2
            big = 12582912.0
            turns = prod[:, 3, :]
            for dst, quarter in ((a_rot[:, 2, :], 0.25), (a_rot[:, 3, :], 0.0)):
                link(dve.tensor_scalar(turns, theta, 1.0 / TWO_PI, quarter, ALU.mult, ALU.add))
                link(dve.tensor_scalar(turns, turns, big, None, ALU.add))
                link(dve.tensor_scalar(turns, turns, big, None, ALU.subtract))
                link(dve.scalar_tensor_tensor(dst, turns, -c1, theta, ALU.mult, ALU.add))
                link(dve.scalar_tensor_tensor(dst, turns, -c2, dst, ALU.mult, ALU.add))
                link(dve.scalar_tensor_tensor(dst, turns, -c3, dst, ALU.mult, ALU.add))
                if quarter:
                    link(dve.tensor_scalar(dst, dst, TWO_PI / 4, None, ALU.add))
                link(dve.tensor_scalar(dst, dst, 3.1415925, -3.1415925, ALU.min, ALU.max))
            assert cnt[0] < 100
            dve.sem_inc(pd, 100 - cnt[0])
            cnt[0] = 100
            link(dve.tensor_scalar(dec[:, 4:5], dec[:, 3:4], 1.0, None, ALU.add))
            link(dve.reciprocal(dec[:, 5:6], dec[:, 4:5]))
            link(dve.tensor_tensor(dec[:, 6:7], dec[:, 5:6], dec[:, 2:3], ALU.mult))
            cpos, rest = prod[0:AH, 2, :], prod[0:AH, 3, :]
            for side, sgn in ((0, -1.0), (1, 1.0)):
                link(dve.tensor_scalar(cpos, prod[0:AH, 1, :], dec[:, 6:7], sgn, ALU.mult, ALU.mult))
                link(dve.tensor_copy(part[0:AH, side, 0, :], cpos))
                link(dve.tensor_tensor(rest, cpos, part[0:AH, side, 0, :], ALU.subtract))
                link(dve.tensor_copy(part[0:AH, side, 1, :], rest))
                link(dve.tensor_tensor(part[0:AH, side, 2, :], rest, part[0:AH, side, 1, :], ALU.subtract))
            dve.wait_ge(pre_act, 4)
            link(dve.tensor_copy(a_rot[:, 2, :], a_rot[:, 0, :]))
            link(dve.tensor_scalar(a_rot[:, 3, :], a_rot[:, 1, :], sign[:, 0:1], None, ALU.mult))
            link(dve.tensor_scalar(a_rot[:, 0:2, :], a_rot[:, 2:4, :], AD ** -0.5, None, ALU.mult))
            dve.sem_inc(pd, 1000 - cnt[0])
            cnt[0] = 1000
            dve.wait_ge(pd, 1000)
            dve.wait_ge(decay_in, 16 * 12)

            def a_products(i, units):
                for u in units:
                    dve.wait_ge(a_proj, after(a_proj, i, u + 1))
                    dve.tensor_tensor(prod[:, u, :], ps[:, (u + 1) % 3, :], a_rot[:, u, :], ALU.mult).then_inc(a_prod, 1)

            def a_rotated(i, side):
                dve.wait_ge(a_prod, after(a_prod, i, 2 * side + 2))
                dve.tensor_tensor(rot[:, side, :], prod[:, 2 * side, :], prod[:, 2 * side + 1, :], ALU.add).then_inc(a_rot_sum, 1)

            def a_remainder(i, side):
                dve.wait_ge(a_hi, after(a_hi, i, side + 1))
                dve.tensor_tensor(rot[:, side, :], rot[:, side, :], part[:, side, 0, :], ALU.subtract).then_inc(a_rest, 1)

            def a_lowest(i, side):
                dve.wait_ge(a_mid, after(a_mid, i, side + 1))
                dve.tensor_tensor(part[:, side, 2, :], rot[:, side, :], part[:, side, 1, :], ALU.subtract).then_inc(a_lo, 1)

            def attention(k, i, first):
                for n, (t0, src, dst) in enumerate(((0, xT, xn), (A_TAIL + 8, x1T, xf))):
                    if k == t0 + 3:
                        dve.wait_ge(a_ln_mean, after(a_ln_mean, i, n + 1))
                        if n and not first:
                            dve.wait_ge(f_mid, after(f_mid, (i - 1) * LAYERS, 1))
                        dve.tensor_tensor(dst[:], src[:], ps[:, 1, :], ALU.subtract).then_inc(a_ln_cent, 1)
                    if k == t0 + 6:
                        dve.wait_ge(a_ln_var, after(a_ln_var, i, n + 1))
                        dve.tensor_scalar(rstd[:, 0, :], ps[:, 1, 0:NT], 1e-5, None, ALU.add).then_inc(a_ln_rsqrt, 1)
                        rsqrt(dve, rstd[:, 1, :], rstd[:, 0, :], rstd[:, 2, :], a_ln_rsqrt, i, n * RSQRT_STEPS)
                    if k == t0 + 8:
                        dve.wait_ge(a_ln_spread, after(a_ln_spread, i, n + 1))
                        dve.wait_ge(a_ln_sq, after(a_ln_sq, i, n + 1))
                        dve.tensor_tensor(dst[:], dst[:], ps[:, 0, :], ALU.mult).then_inc(a_ln_out, 1)
                if k == A_PROJ + 1:
                    a_products(i, (0, 1))
                    a_rotated(i, 0)
                    a_products(i, (2,))
                if k == A_PROJ + 3:
                    a_remainder(i, 0)
                    a_products(i, (3,))
                    a_rotated(i, 1)
                if k == A_PROJ + 5:
                    a_lowest(i, 0)
                    a_remainder(i, 1)
                if k == A_PROJ + 7:
                    a_lowest(i, 1)
                if A_S <= k < A_S + len(S_SLOTS):
                    n = k - A_S
                    bank = ps[:, n % 3, :]
                    h = S_SLOTS[n][0][0]
                    dve.wait_ge(a_s, after(a_s, i, n + 1))
                    if n % SLOTS_PAIR == SLOTS_PAIR - 1:
                        dve.tensor_reduce(negm[:, 1, h % 2, h // 2:h // 2 + 2], bank.rearrange("p (a k) -> p a k", a=2), AX.X,
                                          ALU.max, negate=True).then_inc(a_max, 1)
                    else:
                        for h, t, off in S_SLOTS[n]:
                            dve.tensor_reduce(negm[:, t, h % 2, h // 2:h // 2 + 1], bank[:, off:off + P * (t + 1)], AX.X,
                                              ALU.max, negate=True).then_inc(a_max, 1)
                if k == A_MAXT - 1:
                    dve.wait_ge(a_max, after(a_max, i, S_MAXIMA[-1]))
                    dve.tensor_copy(negm_p[:, :, :, 0, :], negm[:]).then_inc(a_maxparts, 1)
                    dve.wait_ge(a_maxparts, after(a_maxparts, i, 1))
                    dve.tensor_tensor(negm_r[:], negm[:], negm_p[:, :, :, 0, :], ALU.subtract).then_inc(a_maxparts, 1)
                    dve.wait_ge(a_maxparts, after(a_maxparts, i, 2))
                    dve.tensor_copy(negm_p[:, :, :, 1, :], negm_r[:]).then_inc(a_maxparts, 1)
                    dve.wait_ge(a_maxparts, after(a_maxparts, i, 3))
                    dve.tensor_tensor(negm_p[:, :, :, 2, :], negm_r[:], negm_p[:, :, :, 1, :], ALU.subtract).then_inc(a_maxparts, 1)
                g, n = divmod(k - A_ST, ST_UNITS)
                if n == 5 and 1 <= g <= GROUPS:
                    g -= 1
                    dve.wait_ge(a_oT, after(a_oT, i, g + 1))
                    acc = ring_bank(("oT", g)).rearrange("p (t h d) -> p t h d", t=NT, h=GROUP)
                    dve.reciprocal(rl[:, g % 2], acc[:, :, :, AD]).then_inc(a_rl, 1)
                    dve.wait_ge(a_rl, after(a_rl, i, g + 1))
                    dve.tensor_tensor(oN[:, :, GROUP * g:GROUP * (g + 1), :], acc[:, :, :, 0:AD],
                                      rl[:, g % 2].unsqueeze(3).broadcast_to([P, NT, GROUP, AD]), ALU.mult).then_inc(a_norm, 1)
                if k == A_TAIL + 9:
                    dve.wait_ge(a_y, after(a_y, i, 1))
                    if not first:
                        dve.wait_ge(res_kept, after(res_kept, i - 1, 1))
                    dve.tensor_tensor(x1T[:], xT[:], ps[:, 0, :], ALU.add).then_inc(a_x1, 1)

            def shift(src):
                dve.tensor_copy(hT[0:64, :], src[0:64, :]).then_inc(f_shift, 1)
                dve.tensor_copy(hT[64:P, 1:TOK], src[64:P, 0:TOK - 1]).then_inc(f_shift, 1)

            def layers(k, i):
                l, k = divmod(k, F_LAYER)
                lay = i * LAYERS + l
                if l == LAYERS:
                    if k == 0:
                        dve.wait_ge(f_next, after(f_next, lay - 1, 1))
                        dve.wait_ge(res_kept, after(res_kept, i, 1))
                        dve.tensor_tensor(mid[:], cur[:], res[:], ALU.add).then_inc(y_sum, 1)
                    return
                src = xf if l == 0 else cur
                if k == 0:
                    if l == 0:
                        dve.wait_ge(a_ln_out, after(a_ln_out, i, 2))
                    else:
                        dve.wait_ge(f_next, after(f_next, lay - 1, 1))
                    shift(src)
                    if l == 0:
                        dve.wait_ge(a_x1, after(a_x1, i, 1))
                        dve.wait_ge(y_sum, after(y_sum, i, 1))
                        dve.tensor_copy(res[:], x1T[:]).then_inc(res_kept, 1)
                if 3 <= k < 3 + 2 * NT:
                    u = k - 3
                    kind, t = divmod(u, NT)
                    dve.wait_ge(f_sq, after(f_sq, lay, u + 1))
                    dve.tensor_reduce(ss[:, 0, u, :], sqf[:, u % 2, :].rearrange("p (h d) -> p h d", h=FH),
                                      AX.X, ALU.add).then_inc(f_ss, 1)
                    if u >= 2:
                        dve.wait_ge(f_rope, after(f_rope, lay, u - 1))
                    cosb = f_rot[:, l, 2 * kind, t, :].unsqueeze(1).broadcast_to([P, FH, FD])
                    sinb = f_rot[:, l, 2 * kind + 1, t, :].unsqueeze(1).broadcast_to([P, FH, FD])
                    heads = fbank(u).rearrange("p (h d) -> p h d", h=FH)
                    dve.tensor_tensor(t1[:, u % 2, :].rearrange("p (h d) -> p h d", h=FH), heads, cosb,
                                      ALU.mult).then_inc(f_cos, 1)
                    tv = t2[:, u % 2, :].rearrange("p (h d) -> p h d", h=FH)
                    for h in range(2):
                        a, b = slice(32 * h, 32 * h + 32), slice(32 - 32 * h, 64 - 32 * h)
                        dve.tensor_tensor(tv[:, :, a], heads[:, :, b], sinb[:, :, a], ALU.mult).then_inc(f_sin, 1)
                if k == F_RSQRT:
                    dve.wait_ge(f_ss, after(f_ss, lay, 2 * NT))
                    flat = [ss[:, n].rearrange("p u h -> p (u h)") for n in range(3)]
                    dve.tensor_scalar(flat[0], flat[0], 1e-24, None, ALU.max).then_inc(f_rsqrt, 1)
                    rsqrt(dve, flat[1], flat[0], flat[2], f_rsqrt, lay, 0)
                if F_RSQRT < k <= F_RSQRT + NT:
                    u = 2 * (k - F_RSQRT) - 2
                    dve.wait_ge(f_rsqrt, after(f_rsqrt, lay, RSQRT_STEPS))
                    dve.wait_ge(f_rope, after(f_rope, lay, u + 1))
                    rv = r[:, u, :].rearrange("p (h d) -> p h d", h=FH)
                    dve.tensor_tensor(rv, rv, ss[:, 1, u, :].unsqueeze(2).broadcast_to([P, FH, FD]),
                                      ALU.mult).then_inc(f_unit_v, 1)
                v = k - F_ATT
                if 3 <= v < 3 + 2 * NT:
                    w = v - 3
                    t, par = divmod(w, 2)
                    dve.wait_ge(f_o, after(f_o, lay, w + 1))
                    acc = fbank(3)[:, 0:CH * (FD + 1)].rearrange("p (c d) -> p c d", c=CH)
                    dve.reciprocal(rlf[:, w % 2], acc[:, :, FD]).then_inc(f_rl, 1)
                    dve.wait_ge(f_rl, after(f_rl, lay, w + 1))
                    if t >= 2:
                        dve.wait_ge(f_oT, after(f_oT, lay, t - 1))
                    ov = oS[:, t % 2].rearrange("p (c s) d -> p c s d", s=2)
                    dve.tensor_tensor(ov[:, :, par, :], acc[:, :, 0:FD],
                                      rlf[:, w % 2].unsqueeze(2).broadcast_to([P, CH, FD]),
                                      ALU.mult).then_inc(f_norm, 1)
                if 0 <= v < 2 * NT:
                    dve.wait_ge(f_s, after(f_s, lay, v + 1))
                    sc = fbank(v % 2).rearrange("p (c k) -> p c k", c=CH)
                    dve.tensor_reduce(nm[:, v % 2], sc, AX.X, ALU.max, negate=True).then_inc(f_max, 1)
                    dve.wait_ge(f_max, after(f_max, lay, v + 1))
                    if v >= 2:
                        dve.wait_ge(f_pT, after(f_pT, lay, v - 1))
                    dve.tensor_tensor(ex[:, v % 2], sc, nm[:, v % 2].unsqueeze(2).broadcast_to([P, CH, P]),
                                      ALU.add).then_inc(f_shifted, 1)
                if k == F_WO + 1:
                    dve.wait_ge(f_wo, after(f_wo, lay, 1))
                    dve.tensor_tensor(mid[:], src[:], fbank(0), ALU.add).then_inc(f_mid, 1)
                    dve.wait_ge(f_mid, after(f_mid, lay, 1))
                    shift(mid)
                if k == F_LN + 1:
                    dve.wait_ge(f_ln_mean, after(f_ln_mean, lay, 1))
                    dve.tensor_tensor(nT[:], hT[:], fbank(1), ALU.subtract).then_inc(f_ln_cent, 1)
                if k == F_LN + 4:
                    dve.wait_ge(f_ln_var, after(f_ln_var, lay, 1))
                    dve.tensor_scalar(rstd_f[:, 0, :], fbank(1)[:, 0:NT], 1e-5, None, ALU.add).then_inc(f_ln_rsqrt, 1)
                    rsqrt(dve, rstd_f[:, 1, :], rstd_f[:, 0, :], rstd_f[:, 2, :], f_ln_rsqrt, lay, 0)
                if k == F_LN + 6:
                    dve.wait_ge(f_ln_spread, after(f_ln_spread, lay, 1))
                    dve.tensor_tensor(nT[:], nT[:], fbank(2), ALU.mult).then_inc(f_ln_out, 1)
                    dve.wait_ge(f_ln_out, after(f_ln_out, lay, 1))
                    dve.tensor_scalar(nT[:], nT[:], ln_gb[:, l, 0:1], ln_gb[:, l, 1:2], ALU.mult, ALU.add).then_inc(f_ln_gb, 1)
                for j, (_, w) in enumerate(HCH):
                    if k == F_MLP + (3, 3, 4)[j]:
                        dve.wait_ge(f_w1, after(f_w1, lay, len(HCH) + j + 1))
                        dve.wait_ge(f_gelu, after(f_gelu, lay, j + 1))
                        dve.scalar_tensor_tensor(hid[0:w, j, :], fbank(3 + len(HCH) + j)[0:w], b1[0:w, l, 0, j:j + 1],
                                                 gel[0:w, j, :], ALU.add, ALU.mult).then_inc(f_hid, 1)
                if k == F_MLP + 6:
                    dve.wait_ge(f_w2, after(f_w2, lay, 1))
                    dve.scalar_tensor_tensor(cur[:], fbank(4), b2[:, l:l + 1], mid[:], ALU.add, ALU.add).then_inc(f_next, 1)

            for who, k in ALONE_A:
                attention(k, 0, True)
            with dve.Fori(0, SEQS - 1) as i:
                for who, k in MERGED:
                    if who == "A":
                        attention(k, i + 1, False)
                    else:
                        layers(k, i)
            for who, k in ALONE_F:
                layers(k, SEQS - 1)

        @block.tensor
        def _(pe):
            def transpose4(bank, src):
                for t in range(4):
                    last = pe.transpose(bank[:, P * t:P * t + P], src(t), ident[:])
                return last

            def variance(bank, squares):
                for t in range(NT):
                    last = pe.matmul(bank[:, t:t + 1], squares[:, P * t:P * t + P], mean_w[:, 0:1], start=True, stop=True)
                return last

            def spread(bank, y):
                for t in range(NT):
                    last = pe.matmul(bank[:, P * t:P * t + P], y[:, 1, t:t + 1].broadcast_to([P, P]), ident[:],
                                     start=True, stop=True)
                return last

            pe.wait_ge(pre_dve, 1000)
            pe.wait_ge(const_ready, 9)
            pe.wait_ge(decay_in, 16 * 12)

            def a_ring_free(i, what):
                n = ring_at[what]
                if n >= 2:
                    kind, m = ring[n - 2]
                    if kind == "st":
                        pe.wait_ge(a_exp, after(a_exp, i, m + 1))
                    else:
                        pe.wait_ge(a_norm, after(a_norm, i, m + 1))

            def a_values(i, g, j):
                col, w = SECTION[j]
                unit = [n for n, (tiles, _, _) in enumerate(PASS) if j in tiles][0]
                pe.wait_ge(a_exp, after(a_exp, i, ST_UNITS * g + GROUP * (unit + 1)))
                if j == 0 and g:
                    pe.wait_ge(a_o_sb, after(a_o_sb, i, g))
                for hh in range(GROUP):
                    last = pe.matmul(ps[32 * hh:32 * hh + 32, 2, P * j:TOK], vA[:, j, GROUP * g + hh, :],
                                     pT[:, hh, col:col + w], start=(j == 0), stop=(j == 2))
                if j == 2:
                    last.then_inc(a_pv, 1)

            def attention(k, i, first):
                if k == 0:
                    pe.wait_ge(x_loaded, after(x_loaded, i, 16))
                    if not first:
                        pe.wait_ge(a_ln_out, after(a_ln_out, i - 1, 2))
                    transpose4(ps[:, 0, :], lambda t: x_in[:, t, :]).then_inc(xT_ps, 1)
                for n, (t0, src) in enumerate(((0, xT), (A_TAIL + 8, x1T))):
                    if k == t0 + 2:
                        if n:
                            pe.wait_ge(a_x1, after(a_x1, i, 1))
                        else:
                            pe.wait_ge(xT_sb, after(xT_sb, i, 1))
                        pe.matmul(ps[:, 1, :], mean_w[:], src[:], start=True, stop=True).then_inc(a_ln_mean, 1)
                    if k == t0 + 5:
                        pe.wait_ge(a_ln_sq, after(a_ln_sq, i, n + 1))
                        variance(ps[:, 1, :], sq).then_inc(a_ln_var, 1)
                    if k == t0 + A_SPREAD:
                        pe.wait_ge(a_ln_rsqrt, after(a_ln_rsqrt, i, (n + 1) * RSQRT_STEPS))
                        spread(ps[:, 0, :], rstd).then_inc(a_ln_spread, 1)
                if k == A_PROJ:
                    pe.wait_ge(a_ln_out, after(a_ln_out, i, 1))
                    for u in range(3):
                        pe.matmul(ps[:, (u + 1) % 3, :], awqk[:, u, :], xn[:], start=True, stop=True).then_inc(a_proj, 1)
                if k == A_PROJ + 2:
                    pe.wait_ge(a_prod, after(a_prod, i, 2))
                    pe.matmul(ps[:, 1, :], awqk[:, 3, :], xn[:], start=True, stop=True).then_inc(a_proj, 1)
                    for t in range(NT):
                        last = pe.matmul(ps[:, 2, P * t:P * t + P], xn[:, P * t:P * t + P], awv[:], start=True, stop=True)
                    last.then_inc(a_proj, 1)
                if A_S <= k < A_S + len(S_SLOTS):
                    n = k - A_S
                    if n == 0:
                        pe.wait_ge(a_packed, after(a_packed, i, 16 * 4 * len(Q_PARTS)))
                        pe.wait_ge(a_v, after(a_v, i, 1))
                    if n >= 3:
                        pe.wait_ge(a_max, after(a_max, i, S_MAXIMA[n - 3]))
                    bank = ps[:, n % 3, :]
                    for h, t, off in S_SLOTS[n]:
                        rows = slice(64 * (h % 2), 64 * (h % 2) + K_SCORE)
                        pe.matmul(bank[:, off:off + P * (t + 1)], qP[rows, h // 2, P * t:P * t + P],
                                  kP[rows, h // 2, 0:P * (t + 1)], start=True, stop=False, skip_group_check=True)
                        last = pe.matmul(bank[:, off + P * t:off + P * t + P], ident_b[:], causal[:, 0, :],
                                         start=False, stop=True, skip_group_check=True)
                    last.then_inc(a_s, 1)
                if k == A_MAXT:
                    pe.wait_ge(a_maxparts, after(a_maxparts, i, 4))
                    for t in range(NT):
                        last = pe.matmul(ps[0:6 * PAIRS, 0, P * t:P * t + P], negm_p[:, t].rearrange("p a m h -> p (a m h)"),
                                         ident_b[:], start=True, stop=True)
                    last.then_inc(a_maxT, 1)
                m = k - A_ST
                g, n = divmod(m, ST_UNITS)
                if 0 <= m < GROUPS * ST_UNITS:
                    if m == 0:
                        pe.wait_ge(a_max_in, after(a_max_in, i, 32))
                    a_ring_free(i, ("st", m))
                    h = GROUP * g + n % GROUP
                    rows = slice(64 * (h % 2), 64 * (h % 2) + K_SHIFTED)
                    off = 0
                    for c, j in enumerate(PASS[n // GROUP][0]):
                        w = SECTION[j][1]
                        bank = ring_bank(("st", m))
                        pe.matmul(bank[:, off:off + w], kP[rows, h // 2, P * j:P * j + P], qP[rows, h // 2, P * j:TOK],
                                  start=(c == 0), stop=False, skip_group_check=True)
                        last = pe.matmul(bank[:, off:off + P], ident_b[:], causal[:, 1, :], start=False, stop=True,
                                         skip_group_check=True)
                        off += w
                    last.then_inc(a_st, 1)
                if n == 1 and 1 <= g <= GROUPS:
                    a_values(i, g - 1, 2)
                if n == 4 and 1 <= g <= GROUPS:
                    pe.wait_ge(a_o_sb, after(a_o_sb, i, g))
                    a_ring_free(i, ("oT", g - 1))
                    transpose4(ring_bank(("oT", g - 1)), lambda t: oP[:, P * t:P * t + P]).then_inc(a_oT, 1)
                if n in (5, 9, 10) and 0 <= g < GROUPS:
                    a_values(i, g, {5: 0, 9: 1, 10: 3}[n])
                if k == A_TAIL + 6:
                    pe.wait_ge(a_norm, after(a_norm, i, GROUPS))
                    transpose4(ps[:, 2, :], lambda t: oN[:, t].rearrange("p h d -> p (h d)")).then_inc(a_oN_T, 1)
                if k == A_TAIL + 8:
                    pe.wait_ge(a_oA, after(a_oA, i, 1))
                    pe.matmul(ps[:, 0, :], awo[:], oA[:], start=True, stop=True).then_inc(a_y, 1)

            def layers(k, i):
                l, k = divmod(k, F_LAYER)
                lay = i * LAYERS + l
                if l == LAYERS:
                    if k == 1:
                        pe.wait_ge(y_sum, after(y_sum, i, 2))
                        transpose4(fbank(0), lambda t: mid[:, P * t:P * t + P]).then_inc(y_ps, 1)
                    return
                if 1 <= k < 1 + 3 * NT:
                    u = k - 1
                    kind, t = divmod(u, NT)
                    if u == 0:
                        pe.wait_ge(f_shift, after(f_shift, lay, 2))
                        if l == 0:
                            pe.wait_ge(y_sb, after(y_sb, i, 1))
                    if u >= F_BANKS:
                        pe.wait_ge(f_sin, after(f_sin, lay, 2 * (u - F_BANKS) + 2))
                    pe.matmul(fbank(u), hT[:, P * t:P * t + P], wqkv[:, l, CH * P * kind:CH * P * (kind + 1)],
                              start=True, stop=True).then_inc(f_proj, 1)
                if F_QKT <= k < F_QKT + NT:
                    for u in (2 * (k - F_QKT), 2 * (k - F_QKT) + 1):
                        if u == 0:
                            pe.wait_ge(f_sin, after(f_sin, lay, 4 * NT))
                        elif u <= NT:
                            pe.wait_ge(f_v, after(f_v, lay, u))
                        else:
                            pe.wait_ge(f_qkT_sb, after(f_qkT_sb, lay, u - NT))
                        if u % 2:
                            pe.wait_ge(f_unit_p, after(f_unit_p, lay, u // 2 + 1))
                        else:
                            pe.wait_ge(f_unit_v, after(f_unit_v, lay, u // 2 + 1))
                        transpose4(fbank(3 * NT + u), lambda c: r[:, u, P * c:P * c + P]).then_inc(f_qkT, 1)
                v = k - F_ATT
                if 2 <= v < 2 + 2 * NT:
                    w = v - 2
                    pe.wait_ge(f_exp, after(f_exp, lay, w + 1))
                    if w:
                        pe.wait_ge(f_pT_sb, after(f_pT_sb, lay, w))
                    transpose4(fbank(2), lambda c: ex[:, w % 2, c, :]).then_inc(f_pT, 1)
                if 3 <= v < 3 + 2 * NT:
                    w = v - 3
                    t, par = divmod(w, 2)
                    pe.wait_ge(f_pT_sb, after(f_pT_sb, lay, w + 1))
                    if w == 0:
                        pe.wait_ge(f_v_cross, after(f_v_cross, lay, 32))
                    else:
                        pe.wait_ge(f_norm, after(f_norm, lay, w))
                    for c in range(CH):
                        h = 2 * c + par
                        cols = slice((FD + 1) * c, (FD + 1) * (c + 1))
                        pe.matmul(fbank(3)[0:64, cols], pTf[:, w % 2, c, 0:64], v_cross[:, t, h, :],
                                  start=True, stop=True, skip_group_check=True)
                        last = pe.matmul(fbank(3)[64:P, cols], pTf[:, w % 2, c, 64:P], v_own[:, t, h, :],
                                         start=True, stop=True, skip_group_check=True)
                    last.then_inc(f_o, 1)
                if 5 <= v < 5 + 2 * NT and v % 2:
                    t = (v - 5) // 2
                    pe.wait_ge(f_norm, after(f_norm, lay, 2 * t + 2))
                    if t:
                        pe.wait_ge(f_oT_sb, after(f_oT_sb, lay, t))
                    transpose4(fbank(4), lambda c: oS[:, t % 2, 2 * c:2 * c + 2, :].rearrange("p h d -> p (h d)")).then_inc(f_oT, 1)
                if 0 <= v < 2 * NT:
                    t, par = divmod(v, 2)
                    if v == 0:
                        pe.wait_ge(f_qkT_sb, after(f_qkT_sb, lay, 2 * NT))
                    if v >= 2:
                        pe.wait_ge(f_shifted, after(f_shifted, lay, v - 1))
                    bank = fbank(v % 2)
                    rows = slice(64 * par, 64 * par + 64)
                    pe.matmul(bank.rearrange("p (c k) -> p c k", c=CH), ident_b[:],
                              band[:, 0 if t else 1, :].unsqueeze(1).broadcast_to([P, CH, P]),
                              start=True, stop=False, skip_group_check=True)
                    for c in range(CH):
                        q0 = P * t
                        even, odd = bank[0:64, P * c:P * c + P], bank[64:P, P * c:P * c + P]
                        pe.matmul(even, qT[rows, c, q0:q0 + 64], kT[rows, c, q0:q0 + 128],
                                  start=False, stop=True, skip_group_check=True)
                        last = pe.matmul(odd, qT[rows, c, q0 + 64:q0 + 128], kT[rows, c, q0 + 64:q0 + 192],
                                         start=False, stop=True, skip_group_check=True)
                    last.then_inc(f_s, 1)
                if k == F_WO:
                    pe.wait_ge(f_oT_sb, after(f_oT_sb, lay, NT))
                    for c in range(CH):
                        last = pe.matmul(fbank(0), wo[:, l, c, :], oT[:, c, :], start=(c == 0), stop=(c == CH - 1))
                    last.then_inc(f_wo, 1)
                if k == F_LN:
                    pe.wait_ge(f_shift, after(f_shift, lay, 4))
                    pe.matmul(fbank(1), mean_w[:], hT[:], start=True, stop=True).then_inc(f_ln_mean, 1)
                if k == F_LN + 3:
                    pe.wait_ge(f_ln_sq, after(f_ln_sq, lay, 1))
                    variance(fbank(1), sqf[:, 0, :]).then_inc(f_ln_var, 1)
                if k == F_LN + 5:
                    pe.wait_ge(f_ln_rsqrt, after(f_ln_rsqrt, lay, RSQRT_STEPS))
                    spread(fbank(2), rstd_f).then_inc(f_ln_spread, 1)
                for n, j, when in ((0, 0, 0), (0, 1, 0), (0, 2, 0), (1, 0, 1), (1, 1, 1), (1, 2, 3)):
                    if k == F_MLP + when:
                        j0, w = HCH[j]
                        j0 += HID * (1 - n)
                        if (n, j) == (0, 0):
                            pe.wait_ge(f_ln_gb, after(f_ln_gb, lay, 1))
                        if (n, j) == (1, 2):
                            pe.wait_ge(f_gelu, after(f_gelu, lay, 1))
                        pe.matmul(fbank(3 + len(HCH) * n + j)[0:w], w1[:, l, j0:j0 + w], nT[:],
                                  start=True, stop=True).then_inc(f_w1, 1)
                if k == F_MLP + 5:
                    pe.wait_ge(f_hid, after(f_hid, lay, len(HCH)))
                    for j, (_, w) in enumerate(HCH):
                        last = pe.matmul(fbank(4), w2[0:w, l, j, :], hid[0:w, j, :], start=(j == 0), stop=(j == len(HCH) - 1))
                    last.then_inc(f_w2, 1)

            for who, k in ALONE_A:
                attention(k, 0, True)
            with pe.Fori(0, SEQS - 1) as i:
                for who, k in MERGED:
                    if who == "A":
                        attention(k, i + 1, False)
                    else:
                        layers(k, i)
            for who, k in ALONE_F:
                layers(k, SEQS - 1)


def kernel(L0_attn_x, L0_attn_Wqkv, L0_attn_Wo, L0_attn_log_xi, L0_attn_pi_gate_logit,
           L0_attn_e_gate_logit, L0_ffn_wqkv, L0_ffn_q_scale, L0_ffn_k_scale, L0_ffn_wo,
           L0_ffn_ln_g, L0_ffn_ln_b, L0_ffn_w1, L0_ffn_b1, L0_ffn_w2, L0_ffn_b2):
    import math

    import numpy as np
    import concourse.bacc as bacc
    from concourse.bass_utils import run_bass_kernel_spmd

    f32 = np.float32
    rows = np.arange(P)
    par, dim, pair = rows // 64, (rows % 64) // PAIRS, rows % PAIRS
    head = 2 * pair + par
    order = np.array([2 * p + a for a in range(2) for p in range(PAIRS)])

    neg = f32(-1e30)
    q_, k_ = np.arange(P)[:, None], np.arange(P)[None, :]
    causal = np.stack([np.where(k_ <= q_, f32(0), neg), np.where(k_ >= q_, f32(0), neg)], 1).astype(f32)
    a, b = np.arange(WIN)[:, None], np.arange(WIN)[None, :]
    own, before = np.where(b <= a, f32(0), neg), np.where(b >= a, f32(0), neg)
    none = np.full((WIN, WIN), neg)
    band = np.stack([np.block([[before, own], [before, own]]), np.block([[none, own], [before, own]])], 1).astype(f32)
    kfrac = np.arange(0, AD, 2, dtype=f32) / f32(AD)
    inv = (f32(math.pi) ** (f32(1.0) - kfrac)).astype(f32)
    pos = np.arange(TOK, dtype=f32)
    posfreq = (pos[None, :] * inv[dim // 2][:, None]).astype(f32)
    sign = np.where(dim % 2 == 0, f32(-1), f32(1)).astype(f32)[:, None]
    half = np.arange(0, FD, 2, dtype=f32)
    inv_freq = (f32(1.0) / (f32(10000.0) ** (half / f32(FD)))).astype(f32)
    freqs = (pos[:, None] * inv_freq[None, :]).astype(f32)
    freqs = np.concatenate([freqs, freqs], -1).astype(np.float64)
    base = (half + f32(0.4 * FD)) / f32(1.4 * FD)
    power = (pos - f32(TOK // 2)) / f32(WIN // 2)
    scale = (base[None, :] ** power[:, None]).astype(f32)
    scale = np.concatenate([scale, scale], -1).astype(np.float64)
    rsign = np.where(np.arange(FD) < FD // 2, -1.0, 1.0)
    cos, sin = np.cos(freqs), np.sin(freqs) * rsign
    rope = np.stack([8.0 * cos * scale, 8.0 * sin * scale, cos / scale, sin / scale]).astype(f32)
    rope = rope.reshape(4, NT, P, FD).transpose(2, 0, 1, 3)

    W = np.asarray(L0_attn_Wqkv)
    at = head * AD + dim
    swapped = head * AD + (dim ^ 1)
    awqk = np.stack([W[at].T, W[swapped].T, W[DM + at].T, W[DM + swapped].T], 1)
    b1 = np.zeros((LAYERS, P, 2, len(HCH)), f32)
    for j, (j0, w) in enumerate(HCH):
        for s in range(2):
            b1[:, :w, s, j] = np.asarray(L0_ffn_b1)[:, HID * s + j0:HID * s + j0 + w]
    qk = np.stack([np.asarray(L0_ffn_q_scale), np.asarray(L0_ffn_k_scale)], 1)
    arrays = {
        "x": np.asarray(L0_attn_x),
        "ident": np.eye(P, dtype=f32), "causal": causal, "band": band, "posfreq": posfreq,
        "pos": np.broadcast_to(pos, (AH, TOK)), "sign": sign, "rope": rope,
        "awqk": awqk, "awv": W[2 * DM:].T, "awo": np.asarray(L0_attn_Wo).T,
        "pi_gate": np.asarray(L0_attn_pi_gate_logit)[head][:, None],
        "log_xi": np.asarray(L0_attn_log_xi)[order][:, None],
        "e_gate": np.asarray(L0_attn_e_gate_logit)[order][:, None],
        "wqkv": np.asarray(L0_ffn_wqkv), "wo": np.asarray(L0_ffn_wo), "w1": np.asarray(L0_ffn_w1),
        "w2": np.asarray(L0_ffn_w2), "qkscale": np.broadcast_to(qk[None], (P,) + qk.shape),
        "ln_gb": np.stack([np.asarray(L0_ffn_ln_g).T, np.asarray(L0_ffn_ln_b).T], 2), "b1": b1,
        "b2": np.asarray(L0_ffn_b2).T,
    }
    arrays = {f"in_{k}": np.ascontiguousarray(v) for k, v in arrays.items()}
    nc = bacc.Bacc("TRN2", target_bir_lowering=False, num_devices=1)
    d = {k[3:]: nc.dram_tensor(k, v.shape, mybir.dt.from_np(v.dtype), kind="ExternalInput").ap()
         for k, v in arrays.items()}
    out = nc.dram_tensor("out", (SEQS, TOK, DM), F32, kind="ExternalOutput").ap()
    build(nc, d["x"],
          [d[k] for k in ("ident", "causal", "band", "posfreq", "pos", "sign", "rope")],
          [d[k] for k in ("awqk", "awv", "awo")], [d[k] for k in ("pi_gate", "log_xi", "e_gate")],
          [d[k] for k in ("wqkv", "wo", "w1", "w2")],
          [d[k] for k in ("qkscale", "ln_gb", "b1", "b2")], out)
    r = run_bass_kernel_spmd(nc, [arrays], core_ids=[0])
    return r.results[0]["out"]
```

```python
from contextlib import ExitStack

import concourse.bass as bass
from concourse import mybir

F32 = mybir.dt.float32
BF16 = mybir.dt.bfloat16
I32 = mybir.dt.int32
ALU = mybir.AluOpType
ACT = mybir.ActivationFunctionType
AX = mybir.AxisListType

P = 128
SEQS, TOK, DM = 8, 512, 128
NT = TOK // P
AH, AD = 16, 8
PAIRS = AH // 2
LAYERS, FH, FD = 2, 8, 64
CH = FH // 2
WIN = 64
HID = int(DM * 4 * 2 / 3)
HCH = [(j * P, min(P, HID - j * P)) for j in range((HID + P - 1) // P)]
Q_PARTS, K_PARTS = (0, 0, 1, 1, 0, 2), (0, 1, 0, 1, 2, 0)
DECAY_ROW = len(Q_PARTS) * AD
MAX_ROW = 120
RSQRT_MAGIC = 0x5F3759DF
NEWTON = 3
RSQRT_STEPS = 2 + 3 * NEWTON
SECTION = {0: (0, 512), 1: (512, 384), 3: (896, 128), 2: (1024, 256)}
PT_COLS = 1280
PASS = [((0,), 0, 512), ((1, 3), 512, 512), ((2,), 1024, 256)]
GROUP = 4
GROUPS = AH // GROUP
ST_UNITS = len(PASS) * GROUP

A_SPREAD = 7
A_PROJ = 9
A_S = A_PROJ + 13
S_SLOTS = [slot for h in (0, 1, 4, 5, 8, 9, 12, 13)
           for slot in (((h, 3, 0),), ((h, 2, 0), (h, 0, 384)), ((h + 2, 3, 0),),
                        ((h + 2, 2, 0), (h + 2, 0, 384)), ((h, 1, 0), (h + 2, 1, 256)))]
SLOTS_PAIR = len(S_SLOTS) // PAIRS
S_MAXIMA = [7 * (n // SLOTS_PAIR) + (1, 3, 4, 6, 7)[n % SLOTS_PAIR] for n in range(len(S_SLOTS))]
A_MAXT = A_S + len(S_SLOTS) + 1
A_ST = A_MAXT + 5
A_TAIL = A_ST + GROUPS * ST_UNITS
A_TICKS = A_TAIL + 17
F_RSQRT = (7, 11)
F_UNIT = (8, 8, 9, 9, 11, 12, 12, 13)
UNITS_DVE, UNITS_POOL = (4, 6), (0, 1, 2, 3, 5, 7)
F_QKT, F_ATT = 13, 17
F_WO = F_ATT + 13
F_LN = F_WO + 2
F_MLP = F_LN + 7
F_LAYER = F_MLP + 7
F_TICKS = LAYERS * F_LAYER + 3
A_FRONT = A_PROJ + 6
A_BEFORE = (
    0, 1, 0, 2, 0, 1, 0, 2, 0, 1, 1, 0, 0, 0, 2, 3, 5, 2, 0, 2, 0, 2, 1, 1, 2, 4, 6, 2, 4,
    3, 0, 3, 1, 3, 0, 1, 3, 1, 1, 2, 0, 0, 0, 0, 2, 3, 0, 0, 0, 2, 1, 0, 3, 0, 4, 2, 0, 1,
    1, 1, 1, 0, 1, 1, 1, 3, 2, 2, 1, 1, 2, 2, 1, 2, 1, 1, 3, 1, 5, 0, 2, 0, 1, 1, 3, 2, 3,
    1, 1, 0, 2, 0, 1, 3, 0, 0)

def merged():
    a = [("A", 2 if k < A_FRONT else 1, k) for k in (*range(A_FRONT, A_TICKS), *range(A_FRONT))]
    assert sum(A_BEFORE) == A_TICKS and len(A_BEFORE) == F_TICKS + 1
    out = []
    for k, n in enumerate(A_BEFORE):
        out += a[:n] + [("F", 0, k)] * (k < F_TICKS)
        a = a[n:]
    return out


def build(nc, x, consts, a_w, a_vec, f_w, f_vec, out):
    (ident_d, causal_d, band_d, posfreq_d, pos_d, sign_d, rope_d) = consts
    (awqk_d, awv_d, awo_d) = a_w
    (pi_gate_d, log_xi_d, e_gate_d) = a_vec
    (wqkv_d, wo_d, w1_d, w2_d) = f_w
    (qkscale_d, ln_gb_d, b1_d, b2_d) = f_vec

    with ExitStack() as ctx:
        def sb(name, shape, dt=F32):
            return ctx.enter_context(nc.sbuf_tensor(name, shape, dt))

        ident = sb("ident", [P, P])
        ident_b = sb("ident_b", [P, P], BF16)
        causal = sb("causal", [P, 2, P], BF16)
        band = sb("band", [P, 2, P], BF16)
        mean_w = sb("mean_w", [P, P])
        awqk = sb("awqk", [P, 4, P])
        awv = sb("awv", [P, P])
        awo = sb("awo", [P, P])
        wqkv = sb("wqkv", [P, LAYERS, 3 * CH * P])
        wo = sb("wo", [P, LAYERS, CH, P])
        w1 = sb("w1", [P, LAYERS, 2 * HID])
        w2 = sb("w2", [P, LAYERS, len(HCH), P])
        ln_gb = sb("ln_gb", [P, LAYERS, 2])
        b1 = sb("b1", [P, LAYERS, 2, len(HCH)])
        b2 = sb("b2", [P, LAYERS])
        a_rot = sb("a_rot", [P, 4, TOK])
        f_rot = sb("f_rot", [P, LAYERS, 4, NT, FD])
        qkscale = sb("qkscale", [P, LAYERS, 2, FD])
        gate = sb("gate", [P, 4])
        sign = sb("sign", [P, 1])
        dec = sb("dec", [AH, 8])

        x_in = sb("x_in", [P, NT, DM])
        xT = sb("xT", [P, TOK])
        sq = sb("sq", [P, TOK])
        rstd = sb("rstd", [P, 3, NT])
        xn = sb("xn", [P, TOK])
        part = sb("part", [P, 2, 3, TOK], BF16)
        qP = sb("qP", [P, 2, PAIRS, TOK], BF16)
        kP = sb("kP", [P, PAIRS, TOK], BF16)
        negm = sb("negm", [P, NT, 2, PAIRS])
        negm_r = sb("negm_r", [P, NT, 2, PAIRS])
        negm_p = sb("negm_p", [P, NT, 2, 3, PAIRS], BF16)
        mT = sb("mT", [2 * 3 * PAIRS, TOK], BF16)
        vA = sb("vA", [P, NT, AH, 32])
        pT = sb("pT", [P, GROUP, PT_COLS])
        pT_flat = pT[:].rearrange("p g c -> p (g c)")
        prod = pT_flat[:, 0:4 * TOK].rearrange("p (u t) -> p u t", u=4)
        rot = pT_flat[:, 4 * TOK:6 * TOK].rearrange("p (a t) -> p a t", a=2)
        oP = sb("oP", [P, TOK])
        rl = sb("rl", [P, 2, NT, GROUP])
        oN = sb("oN", [P, NT, AH, AD])
        oA = sb("oA", [P, TOK])
        x1T = sb("x1T", [P, TOK])
        xf = sb("xf", [P, TOK])

        res = sb("res", [P, TOK])
        cur = sb("cur", [P, TOK])
        hT = sb("hT", [P, TOK])
        rstd_f = sb("rstd_f", [P, 3, NT])
        sqf = sb("sqf", [P, 2, CH * P])
        t1 = sb("t1", [P, 2, CH * P])
        t2 = sb("t2", [P, 2, CH * P])
        ss = sb("ss", [P, 3, 2 * NT, FH])
        r = sb("r", [P, 2 * NT, CH * P])
        ex = t1[:].rearrange("p b (c k) -> p b c k", c=CH)
        pTf = t2[:].rearrange("p b (c k) -> p b c k", c=CH)
        oS = sqf[:].rearrange("p b (h d) -> p b h d", h=FH)
        oT = r[:, 0:CH, :]
        gel = r[:, 0:len(HCH), :]
        hid = r[:, len(HCH):2 * len(HCH), :]
        rope = r[:, 0:2, :].rearrange("p a (b t d) -> p (a b) t d", t=NT, d=FD)
        causal_f = r[:, 2, 0:2 * P].rearrange("p (a k) -> p a k", a=2)
        band_f = r[:, 3, 0:2 * P].rearrange("p (a k) -> p a k", a=2)
        qT = sb("qT", [P, 2, CH, TOK])
        kT = sb("kT", [P, CH, WIN + TOK])
        v_own = sb("v_own", [P, NT, FH, FD + 1])
        v_cross = sb("v_cross", [P, NT, FH, FD + 1])
        nm = sb("nm", [P, 2, CH])
        rlf = sb("rlf", [P, 2, CH])
        mid = sb("mid", [P, TOK])
        nT = sb("nT", [P, TOK])
        ob = sb("ob", [P, NT, DM])

        ps = ctx.enter_context(nc.psum_tensor("ps", [P, 8, 512], F32))
        F_BANKS = 5

        def fbank(n):
            return ps[:, 3 + n % F_BANKS, :]

        per_round = {}

        def sem(name, per):
            s = ctx.enter_context(nc.semaphore(name))
            per_round[id(s)] = per
            return s

        def after(s, rnd, n):
            return rnd * per_round[id(s)] + n

        const_in = sem("const_in", 0)
        const_ready = sem("const_ready", 0)
        pre_dve = sem("pre_dve", 0)
        pre_act = sem("pre_act", 0)
        mat_in = sem("mat_in", 0)
        layer_in = sem("layer_in", 0)
        layer_tables = sem("layer_tables", 0)
        decay_in = sem("decay_in", 0)
        x_loaded = sem("x_loaded", 16)
        xT_ps = sem("xT_ps", 1)
        xT_sb = sem("xT_sb", 1)
        a_ln_mean = sem("a_ln_mean", 2)
        a_ln_cent = sem("a_ln_cent", 2)
        a_ln_sq = sem("a_ln_sq", 2)
        a_ln_var = sem("a_ln_var", 2)
        a_ln_rsqrt = sem("a_ln_rsqrt", 2 * RSQRT_STEPS)
        a_ln_spread = sem("a_ln_spread", 2)
        a_ln_out = sem("a_ln_out", 2)
        a_proj = sem("a_proj", 5)
        a_prod = sem("a_prod", 4)
        a_rot_sum = sem("a_rot_sum", 2)
        a_hi = sem("a_hi", 2)
        a_rest = sem("a_rest", 2)
        a_mid = sem("a_mid", 2)
        a_lo = sem("a_lo", 2)
        a_packed = sem("a_packed", 16 * 4 * len(Q_PARTS))
        a_v = sem("a_v", 1)
        a_s = sem("a_s", len(S_SLOTS))
        a_max = sem("a_max", S_MAXIMA[-1])
        a_maxparts = sem("a_maxparts", 4)
        a_maxT = sem("a_maxT", 1)
        a_maxT_sb = sem("a_maxT_sb", 1)
        a_max_in = sem("a_max_in", 32)
        a_st = sem("a_st", GROUPS * ST_UNITS)
        a_exp = sem("a_exp", GROUPS * ST_UNITS)
        a_pv = sem("a_pv", GROUPS)
        a_o_sb = sem("a_o_sb", GROUPS)
        a_oT = sem("a_oT", GROUPS)
        a_rl = sem("a_rl", GROUPS)
        a_norm = sem("a_norm", GROUPS)
        a_oN_T = sem("a_oN_T", 1)
        a_oA = sem("a_oA", 1)
        a_y = sem("a_y", 1)
        a_x1 = sem("a_x1", 1)
        x_kept = sem("x_kept", 2)
        f_shift = sem("f_shift", 4)
        f_proj = sem("f_proj", 3 * NT)
        f_sq = sem("f_sq", 2 * NT)
        f_ss = sem("f_ss", 2 * NT)
        f_cos = sem("f_cos", 2 * NT)
        f_sin = sem("f_sin", 4 * NT)
        f_rope = sem("f_rope", 2 * NT)
        f_rsqrt = sem("f_rsqrt", 2 * RSQRT_STEPS)
        f_unit_v = sem("f_unit_v", len(UNITS_DVE))
        f_unit_p = sem("f_unit_p", len(UNITS_POOL))
        f_qkT = sem("f_qkT", 2 * NT)
        f_qkT_sb = sem("f_qkT_sb", 2 * NT)
        f_v = sem("f_v", NT)
        f_v_cross = sem("f_v_cross", 32)
        f_s = sem("f_s", 2 * NT)
        f_max = sem("f_max", 2 * NT)
        f_shifted = sem("f_shifted", 2 * NT)
        f_exp = sem("f_exp", 2 * NT)
        f_pT = sem("f_pT", 2 * NT)
        f_pT_sb = sem("f_pT_sb", 2 * NT)
        f_o = sem("f_o", 2 * NT)
        f_rl = sem("f_rl", 2 * NT)
        f_norm = sem("f_norm", 2 * NT)
        f_oT = sem("f_oT", NT)
        f_oT_sb = sem("f_oT_sb", NT)
        f_wo = sem("f_wo", 1)
        f_mid = sem("f_mid", 1)
        f_ln_mean = sem("f_ln_mean", 1)
        f_ln_cent = sem("f_ln_cent", 1)
        f_ln_sq = sem("f_ln_sq", 1)
        f_ln_var = sem("f_ln_var", 1)
        f_ln_rsqrt = sem("f_ln_rsqrt", RSQRT_STEPS)
        f_ln_spread = sem("f_ln_spread", 1)
        f_ln_out = sem("f_ln_out", 1)
        f_ln_gb = sem("f_ln_gb", 1)
        f_w1 = sem("f_w1", 2 * len(HCH))
        f_gelu = sem("f_gelu", len(HCH))
        f_hid = sem("f_hid", len(HCH))
        f_w2 = sem("f_w2", 1)
        f_next = sem("f_next", 1)
        y_sum = sem("y_sum", 1)
        y_ps = sem("y_ps", 1)
        y_sb = sem("y_sb", 1)
        y_out = sem("y_out", 16)

        def rsqrt(eng, y, s, a, steps, rnd, n0):
            n = n0 + 1
            eng.wait_ge(steps, after(steps, rnd, n))
            eng.tensor_scalar(y.bitcast(I32), s.bitcast(I32), -0.5, float(RSQRT_MAGIC),
                              ALU.mult, ALU.add).then_inc(steps, 1)
            for _ in range(NEWTON):
                n += 1
                eng.wait_ge(steps, after(steps, rnd, n))
                eng.tensor_tensor(a, y, y, ALU.mult).then_inc(steps, 1)
                n += 1
                eng.wait_ge(steps, after(steps, rnd, n))
                eng.scalar_tensor_tensor(a, a, -0.5, s, ALU.mult, ALU.mult).then_inc(steps, 1)
                n += 1
                eng.wait_ge(steps, after(steps, rnd, n))
                eng.scalar_tensor_tensor(y, a, 1.5, y, ALU.add, ALU.mult).then_inc(steps, 1)
            assert n + 1 == n0 + RSQRT_STEPS

        ring = []
        for g in range(GROUPS + 1):
            for n in range(ST_UNITS if g < GROUPS else 0):
                ring.append(("st", ST_UNITS * g + n))
                if n == 4 and g:
                    ring.append(("oT", g - 1))
            if g == GROUPS:
                ring.append(("oT", g - 1))
        ring_at = {what: n for n, what in enumerate(ring)}

        def ring_bank(what):
            return ps[:, ring_at[what] % 2, :]

        MERGED = merged()
        N_CONST, N_MAT, N_LAYER = 16 * 6, 16 * 5, 16 * (5 + 6 * LAYERS)
        N_FILLS, N_DECAY = 11, 16 * 17
        ANGLES_DONE, DECAY_DONE, N_TABLES = 100, 200, 1 + 6 * LAYERS
        block = ctx.enter_context(nc.Block())

        @block.sync
        def _(sp):
            sp.dma_start(gate[:, 0:1], pi_gate_d).then_inc(const_in, 16)
            sp.dma_start(dec[:, 0:1], log_xi_d).then_inc(const_in, 16)
            sp.dma_start(dec[:, 1:2], e_gate_d).then_inc(const_in, 16)
            sp.dma_start(prod[:, 0, :], posfreq_d).then_inc(const_in, 16)
            sp.dma_start(prod[0:AH, 1, :], pos_d).then_inc(const_in, 16)
            sp.dma_start(sign[:], sign_d).then_inc(const_in, 16)
            sp.dma_start(ident[:], ident_d).then_inc(mat_in, 16)
            sp.dma_start(x_in[:], x[0].rearrange("(t p) d -> p t d", p=P)).then_inc(x_loaded, 16)
            sp.dma_start(awqk[:], awqk_d).then_inc(mat_in, 16)
            sp.dma_start(awv[:], awv_d).then_inc(mat_in, 16)
            sp.dma_start(causal_f, causal_d).then_inc(mat_in, 16)
            sp.dma_start(awo[:], awo_d).then_inc(mat_in, 16)
            for dst, src in ((band_f, band_d), (rope, rope_d), (qkscale[:], qkscale_d), (b2[:], b2_d),
                             (ln_gb[:], ln_gb_d)):
                sp.dma_start(dst, src).then_inc(layer_in, 16)
            full = (HID // P) * P
            for l in range(LAYERS):
                sp.dma_start(wqkv[:, l, :], wqkv_d[l]).then_inc(layer_in, 16)
                sp.dma_start(wo[:, l], wo_d[l].rearrange("(c p) d -> p c d", p=P)).then_inc(layer_in, 16)
                sp.dma_start(w1[:, l, :], w1_d[l]).then_inc(layer_in, 16)
                sp.dma_start(w2[:, l, 0:HID // P, :],
                             w2_d[l, 0:full].rearrange("(c p) d -> p c d", p=P)).then_inc(layer_in, 16)
                sp.dma_start(w2[0:HID - full, l, HID // P, :], w2_d[l, full:HID]).then_inc(layer_in, 16)
                sp.dma_start(b1[:, l], b1_d[l]).then_inc(layer_in, 16)

            sp.wait_ge(const_ready, N_FILLS)
            sp.wait_ge(pre_dve, DECAY_DONE)
            for par in range(2):
                for p3 in range(3):
                    row, heads = 64 * par + DECAY_ROW + p3, slice(PAIRS * par, PAIRS * par + PAIRS)
                    sp.dma_start(qP[row:row + 1, par, :, :], part[heads, 0, p3, :]).then_inc(decay_in, 16)
                    sp.dma_start(kP[row + 3:row + 4, :, :], part[heads, 1, p3, :]).then_inc(decay_in, 16)
                row, ones = 64 * par + DECAY_ROW, mT[0:3 * PAIRS, :]
                sp.dma_start(qP[row + 3:row + 6, par, :, :], ones).then_inc(decay_in, 16)
                sp.dma_start(kP[row:row + 3, :, :], ones).then_inc(decay_in, 16)
            sp.dma_start(kP[MAX_ROW:MAX_ROW + 3, :, :], mT[0:3 * PAIRS, :]).then_inc(decay_in, 16)
            sp.wait_ge(decay_in, N_DECAY)

            def pack(i):
                for side, order in enumerate((Q_PARTS, K_PARTS)):
                    sp.wait_ge(a_lo, after(a_lo, i, side + 1))
                    sp.wait_ge(a_mid, after(a_mid, i, side + 1))
                    sp.wait_ge(a_hi, after(a_hi, i, side + 1))
                    for par in range(2):
                        for seg, p3 in enumerate(order):
                            row = 64 * par + AD * seg
                            dst = kP[row:row + AD, :, :] if side else qP[row:row + AD, par, :, :]
                            sp.dma_start(dst, part[64 * par:64 * par + 64, side, p3, :]).then_inc(a_packed, 16)

            def pack_max(i):
                sp.wait_ge(a_maxT_sb, after(a_maxT_sb, i, 1))
                for par in range(2):
                    sp.dma_start(qP[MAX_ROW:MAX_ROW + 3, par, :, :], mT[3 * PAIRS * par:3 * PAIRS * (par + 1), :]).then_inc(a_max_in, 16)

            with sp.Fori(0, SEQS - 1) as i:
                pack(i)
                sp.wait_ge(xT_ps, after(xT_ps, i, 1))
                sp.dma_start(x_in[:], x[i + 1].rearrange("(t p) d -> p t d", p=P)).then_inc(x_loaded, 16)
                pack_max(i)
            pack(SEQS - 1)
            pack_max(SEQS - 1)

        @block.gpsimd
        def _(pool):
            pool.memset(mean_w[:], 1.0 / DM).then_inc(const_ready, 1)
            pool.memset(vA[:], 0.0).then_inc(const_ready, 1)
            pool.wait_ge(const_ready, 2)
            pool.memset(vA[:, :, :, AD:AD + 1], 1.0).then_inc(const_ready, 1)
            for dst, val in ((mT[:], 1.0), (qP[:], 0.0), (kP[:], 0.0), (qT[:], 0.0), (kT[:], 0.0), (hT[:], 0.0),
                             (v_own[:], 1.0), (v_cross[:], 0.0)):
                pool.memset(dst, val).then_inc(const_ready, 1)

            def layers(k, i):
                l, k = divmod(k, F_LAYER)
                lay = i * LAYERS + l
                if l == LAYERS:
                    if k == 0:
                        pool.wait_ge(f_next, after(f_next, lay - 1, 1))
                        pool.wait_ge(x_kept, after(x_kept, i, 2))
                        pool.tensor_tensor(mid[:], cur[:], res[:], ALU.add).then_inc(y_sum, 1)
                    return
                if 4 <= k < 4 + 2 * NT:
                    u = k - 4
                    pool.wait_ge(f_cos, after(f_cos, lay, u + 1))
                    pool.wait_ge(f_sin, after(f_sin, lay, 2 * u + 2))
                    pool.tensor_tensor(r[:, u, :], t1[:, u % 2, :], t2[:, u % 2, :], ALU.add).then_inc(f_rope, 1)
                for u in (n for n in UNITS_POOL if k == F_UNIT[n]):
                    pool.wait_ge(f_rsqrt, after(f_rsqrt, lay, RSQRT_STEPS * (u // NT + 1)))
                    pool.wait_ge(f_rope, after(f_rope, lay, u + 1))
                    rv = r[:, u, :].rearrange("p (h d) -> p h d", h=FH)
                    pool.tensor_tensor(rv, rv, ss[:, 1, u, :].unsqueeze(2).broadcast_to([P, FH, FD]),
                                       ALU.mult).then_inc(f_unit_p, 1)

            with pool.Fori(0, SEQS) as i:
                for k in range(F_TICKS):
                    layers(k, i)

        @block.scalar
        def _(act):
            act.wait_ge(const_in, N_CONST)
            act.activation(gate[:, 1:2], gate[:, 0:1], ACT.Exp, scale=-1.0).then_inc(pre_act, 1)
            act.activation(dec[:, 2:4], dec[:, 0:2], ACT.Exp, scale=-1.0).then_inc(pre_act, 1)
            act.wait_ge(pre_dve, ANGLES_DONE)
            act.activation(a_rot[:, 0, :], a_rot[:, 2, :], ACT.Sin).then_inc(pre_act, 1)
            act.activation(a_rot[:, 1, :], a_rot[:, 3, :], ACT.Sin).then_inc(pre_act, 1)
            act.sem_inc(y_sum, 1)
            act.sem_inc(y_sb, 1)
            act.sem_inc(y_out, 16)

            def attention(k, i, first):
                if k == 1:
                    act.wait_ge(xT_ps, after(xT_ps, i, 1))
                    act.copy(xT[:], ps[:, 0, :]).then_inc(xT_sb, 1)
                if k == 4:
                    act.wait_ge(a_ln_cent, after(a_ln_cent, i, 1))
                    act.activation(sq[:], xn[:], ACT.Square).then_inc(a_ln_sq, 1)
                if k == A_PROJ + 2:
                    act.wait_ge(a_rot_sum, after(a_rot_sum, i, 1))
                    act.copy(part[:, 0, 0, :], rot[:, 0, :]).then_inc(a_hi, 1)
                if k == A_PROJ + 3:
                    if first:
                        act.wait_ge(const_ready, 3)
                    act.wait_ge(a_proj, after(a_proj, i, 5))
                    act.copy(vA[:, :, :, 0:AD], ps[:, 2, :].rearrange("p (t h d) -> p t h d", t=NT, h=AH)).then_inc(a_v, 1)
                if k == A_PROJ + 4:
                    act.wait_ge(a_rest, after(a_rest, i, 1))
                    act.copy(part[:, 0, 1, :], rot[:, 0, :]).then_inc(a_mid, 1)
                    act.wait_ge(a_rot_sum, after(a_rot_sum, i, 2))
                    act.copy(part[:, 1, 0, :], rot[:, 1, :]).then_inc(a_hi, 1)
                if k == A_PROJ + 6:
                    act.wait_ge(a_rest, after(a_rest, i, 2))
                    act.copy(part[:, 1, 1, :], rot[:, 1, :]).then_inc(a_mid, 1)
                if k == A_MAXT + 1:
                    act.wait_ge(a_maxT, after(a_maxT, i, 1))
                    act.copy(mT[:], ps[0:6 * PAIRS, 0, :]).then_inc(a_maxT_sb, 1)
                m = k - A_ST
                if 1 <= m <= GROUPS * ST_UNITS:
                    g, n = divmod(m - 1, ST_UNITS)
                    _, col, w = PASS[n // GROUP]
                    act.wait_ge(a_st, after(a_st, i, m))
                    if g:
                        act.wait_ge(a_pv, after(a_pv, i, g))
                    act.activation(pT[:, n % GROUP, col:col + w], ring_bank(("st", m - 1))[:, 0:w],
                                   ACT.Exp).then_inc(a_exp, 1)
                g, n = divmod(m, ST_UNITS)
                if n == 2 and 1 <= g <= GROUPS:
                    act.wait_ge(a_pv, after(a_pv, i, g))
                    if g >= 2:
                        act.wait_ge(a_oT, after(a_oT, i, g - 1))
                    act.copy(oP[:], ps[:, 2, :]).then_inc(a_o_sb, 1)
                if k == A_TAIL + 7:
                    act.wait_ge(a_oN_T, after(a_oN_T, i, 1))
                    act.copy(oA[:], ps[:, 2, :]).then_inc(a_oA, 1)
                if k == A_TAIL + 12:
                    act.wait_ge(a_ln_cent, after(a_ln_cent, i, 2))
                    act.activation(sq[:], xf[:], ACT.Square).then_inc(a_ln_sq, 1)

            def layers(k, i):
                l, k = divmod(k, F_LAYER)
                lay = i * LAYERS + l
                if l == LAYERS:
                    if k == 2:
                        act.wait_ge(y_ps, after(y_ps, i, 1))
                        act.wait_ge(y_out, after(y_out, i, 16))
                        act.copy(ob[:], fbank(0).rearrange("p (t d) -> p t d", t=NT)).then_inc(y_sb, 1)
                        act.wait_ge(y_sb, after(y_sb, i, 2))
                        act.dma_start(out[i].rearrange("(t p) d -> p t d", p=P), ob[:]).then_inc(y_out, 16)
                    return
                if 2 <= k < 2 + 2 * NT:
                    u = k - 2
                    act.wait_ge(f_proj, after(f_proj, lay, u + 1))
                    if u >= 2:
                        act.wait_ge(f_ss, after(f_ss, lay, u - 1))
                    act.activation(sqf[:, u % 2, :], fbank(u), ACT.Square).then_inc(f_sq, 1)
                if 2 + 2 * NT <= k < 2 + 3 * NT:
                    u = k - 2
                    t = u - 2 * NT
                    act.wait_ge(f_proj, after(f_proj, lay, u + 1))
                    act.copy(v_own[:, t, :, 0:FD], fbank(u).rearrange("p (h d) -> p h d", h=FH)).then_inc(f_v, 1)
                if F_QKT < k <= F_QKT + NT:
                    for u in (2 * (k - F_QKT) - 2, 2 * (k - F_QKT) - 1):
                        act.wait_ge(f_qkT, after(f_qkT, lay, u + 1))
                        t = u % NT
                        bank = fbank(3 * NT + u).rearrange("p (c q) -> p c q", c=CH)
                        if u < NT:
                            act.copy(qT[0:64, 0, :, P * t:P * t + P], bank[0:64])
                            act.copy(qT[64:P, 1, :, P * t:P * t + P], bank[64:P]).then_inc(f_qkT_sb, 1)
                        else:
                            act.copy(kT[:, :, WIN + P * t:WIN + P * t + P], bank).then_inc(f_qkT_sb, 1)
                if k == F_QKT + 2:
                    act.wait_ge(f_v, after(f_v, lay, NT))
                    act.dma_start(v_cross[WIN:P, :, :, :], v_own[0:WIN, :, :, :]).then_inc(f_v_cross, 16)
                    act.dma_start(v_cross[0:WIN, 1:NT, :, :], v_own[WIN:P, 0:NT - 1, :, :]).then_inc(f_v_cross, 16)
                v = k - F_ATT
                if 1 <= v <= 2 * NT:
                    w = v - 1
                    act.wait_ge(f_shifted, after(f_shifted, lay, w + 1))
                    act.activation(ex[:, w % 2], ex[:, w % 2], ACT.Exp).then_inc(f_exp, 1)
                if 2 <= v < 2 + 2 * NT:
                    w = v - 2
                    act.wait_ge(f_pT, after(f_pT, lay, w + 1))
                    if w >= 2:
                        act.wait_ge(f_o, after(f_o, lay, w - 1))
                    act.copy(pTf[:, w % 2], fbank(2).rearrange("p (c q) -> p c q", c=CH)).then_inc(f_pT_sb, 1)
                if 6 <= v < 6 + 2 * NT and v % 2 == 0:
                    t = (v - 6) // 2
                    act.wait_ge(f_oT, after(f_oT, lay, t + 1))
                    act.copy(oT[:, :, P * t:P * t + P], fbank(4).rearrange("p (c q) -> p c q", c=CH)).then_inc(f_oT_sb, 1)
                if k == F_LN + 2:
                    act.wait_ge(f_ln_cent, after(f_ln_cent, lay, 1))
                    act.activation(sqf[:, 0, :], nT[:], ACT.Square).then_inc(f_ln_sq, 1)
                if k == F_MLP + 2:
                    for j, (_, w) in enumerate(HCH):
                        act.wait_ge(f_w1, after(f_w1, lay, j + 1))
                        act.activation(gel[0:w, j, :], fbank(3 + j)[0:w], ACT.Gelu, bias=b1[0:w, l, 1, j:j + 1]).then_inc(f_gelu, 1)

            for k in range(A_TICKS):
                attention(k, 0, True)
            for k in range(A_FRONT):
                attention(k, 1, False)
            act.wait_ge(layer_in, N_LAYER)
            act.wait_ge(const_ready, N_FILLS)
            with act.Fori(0, SEQS - 2) as i:
                for stage, ahead, k in MERGED:
                    if stage == "A":
                        attention(k, i + ahead, False)
                    else:
                        layers(k, i)
            for stage, ahead, k in MERGED:
                if stage == "F":
                    layers(k, SEQS - 2)
                elif ahead == 1:
                    attention(k, SEQS - 1, False)
            for k in range(F_TICKS):
                layers(k, SEQS - 1)
            act.wait_ge(y_out, 16 * (SEQS + 1))

        @block.vector
        def _(dve):
            pd = pre_dve
            cnt = [0]

            def link(ins):
                cnt[0] += 1
                ins.then_inc(pd, 1)
                dve.wait_ge(pd, cnt[0])

            dve.wait_ge(const_in, N_CONST)
            dve.wait_ge(pre_act, 2)
            link(dve.tensor_scalar(gate[:, 2:3], gate[:, 1:2], 1.0, None, ALU.add))
            link(dve.reciprocal(gate[:, 3:4], gate[:, 2:3]))
            theta = prod[:, 2, :]
            link(dve.tensor_scalar(theta, prod[:, 0, :], gate[:, 3:4], None, ALU.mult))
            TWO_PI = 6.283185307179586
            c1 = 6.28125
            c2 = 0.0019350051879882812
            c3 = TWO_PI - c1 - c2
            big = 12582912.0
            turns = prod[:, 3, :]
            for dst, quarter in ((a_rot[:, 2, :], 0.25), (a_rot[:, 3, :], 0.0)):
                link(dve.tensor_scalar(turns, theta, 1.0 / TWO_PI, quarter, ALU.mult, ALU.add))
                link(dve.tensor_scalar(turns, turns, big, None, ALU.add))
                link(dve.tensor_scalar(turns, turns, big, None, ALU.subtract))
                link(dve.scalar_tensor_tensor(dst, turns, -c1, theta, ALU.mult, ALU.add))
                link(dve.scalar_tensor_tensor(dst, turns, -c2, dst, ALU.mult, ALU.add))
                link(dve.scalar_tensor_tensor(dst, turns, -c3, dst, ALU.mult, ALU.add))
                if quarter:
                    link(dve.tensor_scalar(dst, dst, TWO_PI / 4, None, ALU.add))
                link(dve.tensor_scalar(dst, dst, 3.1415925, -3.1415925, ALU.min, ALU.max))
            assert cnt[0] < ANGLES_DONE
            dve.sem_inc(pd, ANGLES_DONE - cnt[0])
            cnt[0] = ANGLES_DONE
            link(dve.tensor_scalar(dec[:, 4:5], dec[:, 3:4], 1.0, None, ALU.add))
            link(dve.reciprocal(dec[:, 5:6], dec[:, 4:5]))
            link(dve.tensor_tensor(dec[:, 6:7], dec[:, 5:6], dec[:, 2:3], ALU.mult))
            cpos, rest = prod[0:AH, 2, :], prod[0:AH, 3, :]
            for side, sgn in ((0, -1.0), (1, 1.0)):
                link(dve.tensor_scalar(cpos, prod[0:AH, 1, :], dec[:, 6:7], sgn, ALU.mult, ALU.mult))
                link(dve.tensor_copy(part[0:AH, side, 0, :], cpos))
                link(dve.tensor_tensor(rest, cpos, part[0:AH, side, 0, :], ALU.subtract))
                link(dve.tensor_copy(part[0:AH, side, 1, :], rest))
                link(dve.tensor_tensor(part[0:AH, side, 2, :], rest, part[0:AH, side, 1, :], ALU.subtract))
            dve.wait_ge(pre_act, 4)
            link(dve.tensor_copy(a_rot[:, 2, :], a_rot[:, 0, :]))
            link(dve.tensor_scalar(a_rot[:, 3, :], a_rot[:, 1, :], sign[:, 0:1], None, ALU.mult))
            link(dve.tensor_scalar(a_rot[:, 0:2, :], a_rot[:, 2:4, :], AD ** -0.5, None, ALU.mult))
            dve.wait_ge(mat_in, N_MAT)
            link(dve.tensor_copy(ident_b[:], ident[:]))
            link(dve.tensor_copy(causal[:], causal_f))
            dve.sem_inc(pd, DECAY_DONE - cnt[0])

            def layer_constants():
                dve.wait_ge(layer_in, N_LAYER)
                dve.wait_ge(const_ready, N_FILLS)
                dve.tensor_copy(band[:], band_f).then_inc(layer_tables, 1)
                for l in range(LAYERS):
                    for k in range(2):
                        sc = qkscale[:, l, k, :].unsqueeze(1).broadcast_to([P, NT, FD])
                        dve.tensor_tensor(f_rot[:, l, 2 * k], rope[:, 2 * k], sc, ALU.mult).then_inc(layer_tables, 1)
                        for h in range(2):
                            a, b = slice(32 * h, 32 * h + 32), slice(32 - 32 * h, 64 - 32 * h)
                            dve.tensor_tensor(f_rot[:, l, 2 * k + 1, :, a], rope[:, 2 * k + 1, :, a],
                                              sc[:, :, b], ALU.mult).then_inc(layer_tables, 1)
                dve.wait_ge(layer_tables, N_TABLES)

            def a_products(i, units):
                for u in units:
                    dve.wait_ge(a_proj, after(a_proj, i, u + 1))
                    dve.tensor_tensor(prod[:, u, :], ps[:, (u + 1) % 3, :], a_rot[:, u, :], ALU.mult).then_inc(a_prod, 1)

            def a_rotated(i, side):
                dve.wait_ge(a_prod, after(a_prod, i, 2 * side + 2))
                dve.tensor_tensor(rot[:, side, :], prod[:, 2 * side, :], prod[:, 2 * side + 1, :], ALU.add).then_inc(a_rot_sum, 1)

            def a_remainder(i, side):
                dve.wait_ge(a_hi, after(a_hi, i, side + 1))
                dve.tensor_tensor(rot[:, side, :], rot[:, side, :], part[:, side, 0, :], ALU.subtract).then_inc(a_rest, 1)

            def a_lowest(i, side):
                dve.wait_ge(a_mid, after(a_mid, i, side + 1))
                dve.tensor_tensor(part[:, side, 2, :], rot[:, side, :], part[:, side, 1, :], ALU.subtract).then_inc(a_lo, 1)

            def attention(k, i, first):
                for n, (t0, src, dst) in enumerate(((0, xT, xn), (A_TAIL + 8, x1T, xf))):
                    if k == t0 + 3:
                        dve.wait_ge(a_ln_mean, after(a_ln_mean, i, n + 1))
                        if n and not first:
                            dve.wait_ge(x_kept, after(x_kept, i - 1, 2))
                        dve.tensor_tensor(dst[:], src[:], ps[:, 1, :], ALU.subtract).then_inc(a_ln_cent, 1)
                    if k == t0 + 6:
                        dve.wait_ge(a_ln_var, after(a_ln_var, i, n + 1))
                        dve.tensor_scalar(rstd[:, 0, :], ps[:, 1, 0:NT], 1e-5, None, ALU.add).then_inc(a_ln_rsqrt, 1)
                        rsqrt(dve, rstd[:, 1, :], rstd[:, 0, :], rstd[:, 2, :], a_ln_rsqrt, i, n * RSQRT_STEPS)
                    if k == t0 + 8:
                        dve.wait_ge(a_ln_spread, after(a_ln_spread, i, n + 1))
                        dve.wait_ge(a_ln_sq, after(a_ln_sq, i, n + 1))
                        dve.tensor_tensor(dst[:], dst[:], ps[:, 0, :], ALU.mult).then_inc(a_ln_out, 1)
                if k == A_PROJ + 1:
                    if first:
                        dve.wait_ge(decay_in, N_DECAY)
                    a_products(i, (0, 1))
                    a_rotated(i, 0)
                    a_products(i, (2,))
                if k == A_PROJ + 3:
                    a_remainder(i, 0)
                    a_products(i, (3,))
                    a_rotated(i, 1)
                if k == A_PROJ + 5:
                    a_lowest(i, 0)
                    a_remainder(i, 1)
                if k == A_PROJ + 7:
                    a_lowest(i, 1)
                    if first:
                        layer_constants()
                if A_S <= k < A_S + len(S_SLOTS):
                    n = k - A_S
                    bank = ps[:, n % 3, :]
                    h = S_SLOTS[n][0][0]
                    dve.wait_ge(a_s, after(a_s, i, n + 1))
                    if n % SLOTS_PAIR == SLOTS_PAIR - 1:
                        dve.tensor_reduce(negm[:, 1, h % 2, h // 2:h // 2 + 2], bank.rearrange("p (a k) -> p a k", a=2), AX.X,
                                          ALU.max, negate=True).then_inc(a_max, 1)
                    else:
                        for h, t, off in S_SLOTS[n]:
                            dve.tensor_reduce(negm[:, t, h % 2, h // 2:h // 2 + 1], bank[:, off:off + P * (t + 1)], AX.X,
                                              ALU.max, negate=True).then_inc(a_max, 1)
                if k == A_MAXT - 1:
                    dve.wait_ge(a_max, after(a_max, i, S_MAXIMA[-1]))
                    dve.tensor_copy(negm_p[:, :, :, 0, :], negm[:]).then_inc(a_maxparts, 1)
                    dve.wait_ge(a_maxparts, after(a_maxparts, i, 1))
                    dve.tensor_tensor(negm_r[:], negm[:], negm_p[:, :, :, 0, :], ALU.subtract).then_inc(a_maxparts, 1)
                    dve.wait_ge(a_maxparts, after(a_maxparts, i, 2))
                    dve.tensor_copy(negm_p[:, :, :, 1, :], negm_r[:]).then_inc(a_maxparts, 1)
                    dve.wait_ge(a_maxparts, after(a_maxparts, i, 3))
                    dve.tensor_tensor(negm_p[:, :, :, 2, :], negm_r[:], negm_p[:, :, :, 1, :], ALU.subtract).then_inc(a_maxparts, 1)
                g, n = divmod(k - A_ST, ST_UNITS)
                if n == 5 and 1 <= g <= GROUPS:
                    g -= 1
                    dve.wait_ge(a_oT, after(a_oT, i, g + 1))
                    acc = ring_bank(("oT", g)).rearrange("p (t h d) -> p t h d", t=NT, h=GROUP)
                    dve.reciprocal(rl[:, g % 2], acc[:, :, :, AD]).then_inc(a_rl, 1)
                    dve.wait_ge(a_rl, after(a_rl, i, g + 1))
                    dve.tensor_tensor(oN[:, :, GROUP * g:GROUP * (g + 1), :], acc[:, :, :, 0:AD],
                                      rl[:, g % 2].unsqueeze(3).broadcast_to([P, NT, GROUP, AD]), ALU.mult).then_inc(a_norm, 1)
                if k == A_TAIL + 9:
                    dve.wait_ge(a_y, after(a_y, i, 1))
                    if not first:
                        dve.wait_ge(x_kept, after(x_kept, i - 1, 2))
                    dve.tensor_tensor(x1T[:], xT[:], ps[:, 0, :], ALU.add).then_inc(a_x1, 1)

            def shift(src):
                dve.tensor_copy(hT[0:64, :], src[0:64, :]).then_inc(f_shift, 1)
                dve.tensor_copy(hT[64:P, 1:TOK], src[64:P, 0:TOK - 1]).then_inc(f_shift, 1)

            def layers(k, i):
                l, k = divmod(k, F_LAYER)
                lay = i * LAYERS + l
                if l == LAYERS:
                    return
                if k == 0:
                    if l == 0:
                        dve.wait_ge(a_ln_out, after(a_ln_out, i, 2))
                    else:
                        dve.wait_ge(f_next, after(f_next, lay - 1, 1))
                    shift(xf if l == 0 else cur)
                    if l == 0:
                        dve.wait_ge(a_x1, after(a_x1, i, 1))
                        dve.wait_ge(y_sum, after(y_sum, i, 1))
                        dve.tensor_copy(res[:], x1T[:]).then_inc(x_kept, 1)
                        dve.tensor_copy(cur[:], xf[:]).then_inc(x_kept, 1)
                if 3 <= k < 3 + 2 * NT:
                    u = k - 3
                    kind, t = divmod(u, NT)
                    dve.wait_ge(f_sq, after(f_sq, lay, u + 1))
                    dve.tensor_reduce(ss[:, 0, u, :], sqf[:, u % 2, :].rearrange("p (h d) -> p h d", h=FH),
                                      AX.X, ALU.add).then_inc(f_ss, 1)
                    if u >= 2:
                        dve.wait_ge(f_rope, after(f_rope, lay, u - 1))
                    cosb = f_rot[:, l, 2 * kind, t, :].unsqueeze(1).broadcast_to([P, FH, FD])
                    sinb = f_rot[:, l, 2 * kind + 1, t, :].unsqueeze(1).broadcast_to([P, FH, FD])
                    heads = fbank(u).rearrange("p (h d) -> p h d", h=FH)
                    dve.tensor_tensor(t1[:, u % 2, :].rearrange("p (h d) -> p h d", h=FH), heads, cosb,
                                      ALU.mult).then_inc(f_cos, 1)
                    tv = t2[:, u % 2, :].rearrange("p (h d) -> p h d", h=FH)
                    for h in range(2):
                        a, b = slice(32 * h, 32 * h + 32), slice(32 - 32 * h, 64 - 32 * h)
                        dve.tensor_tensor(tv[:, :, a], heads[:, :, b], sinb[:, :, a], ALU.mult).then_inc(f_sin, 1)
                if k in F_RSQRT:
                    kind = F_RSQRT.index(k)
                    dve.wait_ge(f_ss, after(f_ss, lay, NT * (kind + 1)))
                    flat = [ss[:, n, NT * kind:NT * (kind + 1)].rearrange("p u h -> p (u h)") for n in range(3)]
                    dve.tensor_scalar(flat[0], flat[0], 1e-24, None, ALU.max).then_inc(f_rsqrt, 1)
                    rsqrt(dve, flat[1], flat[0], flat[2], f_rsqrt, lay, RSQRT_STEPS * kind)
                for u in (n for n in UNITS_DVE if k == F_UNIT[n]):
                    dve.wait_ge(f_rsqrt, after(f_rsqrt, lay, RSQRT_STEPS * (u // NT + 1)))
                    dve.wait_ge(f_rope, after(f_rope, lay, u + 1))
                    rv = r[:, u, :].rearrange("p (h d) -> p h d", h=FH)
                    dve.tensor_tensor(rv, rv, ss[:, 1, u, :].unsqueeze(2).broadcast_to([P, FH, FD]),
                                      ALU.mult).then_inc(f_unit_v, 1)
                v = k - F_ATT
                if 3 <= v < 3 + 2 * NT:
                    w = v - 3
                    t, par = divmod(w, 2)
                    dve.wait_ge(f_o, after(f_o, lay, w + 1))
                    acc = fbank(3)[:, 0:CH * (FD + 1)].rearrange("p (c d) -> p c d", c=CH)
                    dve.reciprocal(rlf[:, w % 2], acc[:, :, FD]).then_inc(f_rl, 1)
                    dve.wait_ge(f_rl, after(f_rl, lay, w + 1))
                    if t >= 2:
                        dve.wait_ge(f_oT, after(f_oT, lay, t - 1))
                    ov = oS[:, t % 2].rearrange("p (c s) d -> p c s d", s=2)
                    dve.tensor_tensor(ov[:, :, par, :], acc[:, :, 0:FD],
                                      rlf[:, w % 2].unsqueeze(2).broadcast_to([P, CH, FD]),
                                      ALU.mult).then_inc(f_norm, 1)
                if 0 <= v < 2 * NT:
                    dve.wait_ge(f_s, after(f_s, lay, v + 1))
                    sc = fbank(v % 2).rearrange("p (c k) -> p c k", c=CH)
                    dve.tensor_reduce(nm[:, v % 2], sc, AX.X, ALU.max, negate=True).then_inc(f_max, 1)
                    dve.wait_ge(f_max, after(f_max, lay, v + 1))
                    if v == 0:
                        dve.wait_ge(f_rope, after(f_rope, lay, 2 * NT))
                    if v >= 2:
                        dve.wait_ge(f_pT, after(f_pT, lay, v - 1))
                    dve.tensor_tensor(ex[:, v % 2], sc, nm[:, v % 2].unsqueeze(2).broadcast_to([P, CH, P]),
                                      ALU.add).then_inc(f_shifted, 1)
                if k == F_WO + 1:
                    dve.wait_ge(f_wo, after(f_wo, lay, 1))
                    if l == 0:
                        dve.wait_ge(x_kept, after(x_kept, i, 2))
                    dve.tensor_tensor(mid[:], cur[:], fbank(0), ALU.add).then_inc(f_mid, 1)
                    dve.wait_ge(f_mid, after(f_mid, lay, 1))
                    shift(mid)
                if k == F_LN + 1:
                    dve.wait_ge(f_ln_mean, after(f_ln_mean, lay, 1))
                    dve.tensor_tensor(nT[:], hT[:], fbank(1), ALU.subtract).then_inc(f_ln_cent, 1)
                if k == F_LN + 4:
                    dve.wait_ge(f_ln_var, after(f_ln_var, lay, 1))
                    dve.tensor_scalar(rstd_f[:, 0, :], fbank(1)[:, 0:NT], 1e-5, None, ALU.add).then_inc(f_ln_rsqrt, 1)
                    rsqrt(dve, rstd_f[:, 1, :], rstd_f[:, 0, :], rstd_f[:, 2, :], f_ln_rsqrt, lay, 0)
                if k == F_LN + 6:
                    dve.wait_ge(f_ln_spread, after(f_ln_spread, lay, 1))
                    dve.tensor_tensor(nT[:], nT[:], fbank(2), ALU.mult).then_inc(f_ln_out, 1)
                    dve.wait_ge(f_ln_out, after(f_ln_out, lay, 1))
                    dve.tensor_scalar(nT[:], nT[:], ln_gb[:, l, 0:1], ln_gb[:, l, 1:2], ALU.mult, ALU.add).then_inc(f_ln_gb, 1)
                for j, (_, w) in enumerate(HCH):
                    if k == F_MLP + (3, 3, 4)[j]:
                        dve.wait_ge(f_w1, after(f_w1, lay, len(HCH) + j + 1))
                        dve.wait_ge(f_gelu, after(f_gelu, lay, j + 1))
                        dve.scalar_tensor_tensor(hid[0:w, j, :], fbank(3 + len(HCH) + j)[0:w], b1[0:w, l, 0, j:j + 1],
                                                 gel[0:w, j, :], ALU.add, ALU.mult).then_inc(f_hid, 1)
                if k == F_MLP + 6:
                    dve.wait_ge(f_w2, after(f_w2, lay, 1))
                    dve.scalar_tensor_tensor(cur[:], fbank(4), b2[:, l:l + 1], mid[:], ALU.add, ALU.add).then_inc(f_next, 1)

            for k in range(A_TICKS):
                attention(k, 0, True)
            for k in range(A_FRONT):
                attention(k, 1, False)
            with dve.Fori(0, SEQS - 2) as i:
                for stage, ahead, k in MERGED:
                    if stage == "A":
                        attention(k, i + ahead, False)
                    else:
                        layers(k, i)
            for stage, ahead, k in MERGED:
                if stage == "F":
                    layers(k, SEQS - 2)
                elif ahead == 1:
                    attention(k, SEQS - 1, False)
            for k in range(F_TICKS):
                layers(k, SEQS - 1)

        @block.tensor
        def _(pe):
            def transpose4(bank, src):
                for t in range(4):
                    last = pe.transpose(bank[:, P * t:P * t + P], src(t), ident[:])
                return last

            def variance(bank, squares):
                for t in range(NT):
                    last = pe.matmul(bank[:, t:t + 1], squares[:, P * t:P * t + P], mean_w[:, 0:1], start=True, stop=True)
                return last

            def spread(bank, y):
                for t in range(NT):
                    last = pe.matmul(bank[:, P * t:P * t + P], y[:, 1, t:t + 1].broadcast_to([P, P]), ident[:],
                                     start=True, stop=True)
                return last

            pe.wait_ge(mat_in, N_MAT)
            pe.wait_ge(const_ready, 1)

            def a_ring_free(i, what):
                n = ring_at[what]
                if n >= 2:
                    kind, m = ring[n - 2]
                    if kind == "st":
                        pe.wait_ge(a_exp, after(a_exp, i, m + 1))
                    else:
                        pe.wait_ge(a_norm, after(a_norm, i, m + 1))

            def a_values(i, g, j):
                col, w = SECTION[j]
                unit = [n for n, (tiles, _, _) in enumerate(PASS) if j in tiles][0]
                pe.wait_ge(a_exp, after(a_exp, i, ST_UNITS * g + GROUP * (unit + 1)))
                if j == 0 and g:
                    pe.wait_ge(a_o_sb, after(a_o_sb, i, g))
                for hh in range(GROUP):
                    last = pe.matmul(ps[32 * hh:32 * hh + 32, 2, P * j:TOK], vA[:, j, GROUP * g + hh, :],
                                     pT[:, hh, col:col + w], start=(j == 0), stop=(j == 2))
                if j == 2:
                    last.then_inc(a_pv, 1)

            def attention(k, i, first):
                if k == 0:
                    pe.wait_ge(x_loaded, after(x_loaded, i, 16))
                    if not first:
                        pe.wait_ge(a_ln_out, after(a_ln_out, i - 1, 2))
                    transpose4(ps[:, 0, :], lambda t: x_in[:, t, :]).then_inc(xT_ps, 1)
                for n, (t0, src) in enumerate(((0, xT), (A_TAIL + 8, x1T))):
                    if k == t0 + 2:
                        if n:
                            pe.wait_ge(a_x1, after(a_x1, i, 1))
                        else:
                            pe.wait_ge(xT_sb, after(xT_sb, i, 1))
                        pe.matmul(ps[:, 1, :], mean_w[:], src[:], start=True, stop=True).then_inc(a_ln_mean, 1)
                    if k == t0 + 5:
                        pe.wait_ge(a_ln_sq, after(a_ln_sq, i, n + 1))
                        variance(ps[:, 1, :], sq).then_inc(a_ln_var, 1)
                    if k == t0 + A_SPREAD:
                        pe.wait_ge(a_ln_rsqrt, after(a_ln_rsqrt, i, (n + 1) * RSQRT_STEPS))
                        spread(ps[:, 0, :], rstd).then_inc(a_ln_spread, 1)
                if k == A_PROJ:
                    pe.wait_ge(a_ln_out, after(a_ln_out, i, 1))
                    for u in range(3):
                        pe.matmul(ps[:, (u + 1) % 3, :], awqk[:, u, :], xn[:], start=True, stop=True).then_inc(a_proj, 1)
                if k == A_PROJ + 2:
                    pe.wait_ge(a_prod, after(a_prod, i, 2))
                    pe.matmul(ps[:, 1, :], awqk[:, 3, :], xn[:], start=True, stop=True).then_inc(a_proj, 1)
                    for t in range(NT):
                        last = pe.matmul(ps[:, 2, P * t:P * t + P], xn[:, P * t:P * t + P], awv[:], start=True, stop=True)
                    last.then_inc(a_proj, 1)
                if A_S <= k < A_S + len(S_SLOTS):
                    n = k - A_S
                    if n == 0:
                        if first:
                            pe.wait_ge(pre_dve, DECAY_DONE)
                            pe.wait_ge(decay_in, N_DECAY)
                            pe.wait_ge(const_ready, N_FILLS)
                        pe.wait_ge(a_packed, after(a_packed, i, 16 * 4 * len(Q_PARTS)))
                        pe.wait_ge(a_v, after(a_v, i, 1))
                    if n >= 3:
                        pe.wait_ge(a_max, after(a_max, i, S_MAXIMA[n - 3]))
                    bank = ps[:, n % 3, :]
                    for h, t, off in S_SLOTS[n]:
                        pe.matmul(bank[:, off:off + P * (t + 1)], qP[0:MAX_ROW, h % 2, h // 2, P * t:P * t + P],
                                  kP[0:MAX_ROW, h // 2, 0:P * (t + 1)], start=True, stop=False, skip_group_check=True)
                        last = pe.matmul(bank[:, off + P * t:off + P * t + P], ident_b[:], causal[:, 0, :],
                                         start=False, stop=True, skip_group_check=True)
                    last.then_inc(a_s, 1)
                if k == A_MAXT:
                    pe.wait_ge(a_maxparts, after(a_maxparts, i, 4))
                    for t in range(NT):
                        last = pe.matmul(ps[0:6 * PAIRS, 0, P * t:P * t + P], negm_p[:, t].rearrange("p a m h -> p (a m h)"),
                                         ident_b[:], start=True, stop=True)
                    last.then_inc(a_maxT, 1)
                m = k - A_ST
                g, n = divmod(m, ST_UNITS)
                if 0 <= m < GROUPS * ST_UNITS:
                    if m == 0:
                        pe.wait_ge(a_max_in, after(a_max_in, i, 32))
                    a_ring_free(i, ("st", m))
                    h = GROUP * g + n % GROUP
                    off = 0
                    for c, j in enumerate(PASS[n // GROUP][0]):
                        w = SECTION[j][1]
                        bank = ring_bank(("st", m))
                        pe.matmul(bank[:, off:off + w], kP[:, h // 2, P * j:P * j + P], qP[:, h % 2, h // 2, P * j:TOK],
                                  start=(c == 0), stop=False, skip_group_check=True)
                        last = pe.matmul(bank[:, off:off + P], ident_b[:], causal[:, 1, :], start=False, stop=True,
                                         skip_group_check=True)
                        off += w
                    last.then_inc(a_st, 1)
                if n == 1 and 1 <= g <= GROUPS:
                    a_values(i, g - 1, 2)
                if n == 4 and 1 <= g <= GROUPS:
                    pe.wait_ge(a_o_sb, after(a_o_sb, i, g))
                    a_ring_free(i, ("oT", g - 1))
                    transpose4(ring_bank(("oT", g - 1)), lambda t: oP[:, P * t:P * t + P]).then_inc(a_oT, 1)
                if n in (5, 9, 10) and 0 <= g < GROUPS:
                    a_values(i, g, {5: 0, 9: 1, 10: 3}[n])
                if k == A_TAIL + 6:
                    pe.wait_ge(a_norm, after(a_norm, i, GROUPS))
                    transpose4(ps[:, 2, :], lambda t: oN[:, t].rearrange("p h d -> p (h d)")).then_inc(a_oN_T, 1)
                if k == A_TAIL + 8:
                    pe.wait_ge(a_oA, after(a_oA, i, 1))
                    pe.matmul(ps[:, 0, :], awo[:], oA[:], start=True, stop=True).then_inc(a_y, 1)

            def layers(k, i):
                l, k = divmod(k, F_LAYER)
                lay = i * LAYERS + l
                if l == LAYERS:
                    if k == 1:
                        pe.wait_ge(y_sum, after(y_sum, i, 2))
                        transpose4(fbank(0), lambda t: mid[:, P * t:P * t + P]).then_inc(y_ps, 1)
                    return
                if 1 <= k < 1 + 3 * NT:
                    u = k - 1
                    kind, t = divmod(u, NT)
                    if u == 0:
                        pe.wait_ge(f_shift, after(f_shift, lay, 2))
                        if l == 0:
                            pe.wait_ge(y_sb, after(y_sb, i, 1))
                    if u >= F_BANKS:
                        pe.wait_ge(f_sin, after(f_sin, lay, 2 * (u - F_BANKS) + 2))
                    pe.matmul(fbank(u), hT[:, P * t:P * t + P], wqkv[:, l, CH * P * kind:CH * P * (kind + 1)],
                              start=True, stop=True).then_inc(f_proj, 1)
                if F_QKT <= k < F_QKT + NT:
                    for u in (2 * (k - F_QKT), 2 * (k - F_QKT) + 1):
                        if u == 0:
                            pe.wait_ge(f_sin, after(f_sin, lay, 4 * NT))
                        elif u <= NT:
                            pe.wait_ge(f_v, after(f_v, lay, u))
                        else:
                            pe.wait_ge(f_qkT_sb, after(f_qkT_sb, lay, u - NT))
                        if u in UNITS_DVE:
                            pe.wait_ge(f_unit_v, after(f_unit_v, lay, UNITS_DVE.index(u) + 1))
                        else:
                            pe.wait_ge(f_unit_p, after(f_unit_p, lay, UNITS_POOL.index(u) + 1))
                        transpose4(fbank(3 * NT + u), lambda c: r[:, u, P * c:P * c + P]).then_inc(f_qkT, 1)
                v = k - F_ATT
                if 2 <= v < 2 + 2 * NT:
                    w = v - 2
                    pe.wait_ge(f_exp, after(f_exp, lay, w + 1))
                    if w:
                        pe.wait_ge(f_pT_sb, after(f_pT_sb, lay, w))
                    else:
                        pe.wait_ge(f_qkT_sb, after(f_qkT_sb, lay, 2 * NT - 2))
                    transpose4(fbank(2), lambda c: ex[:, w % 2, c, :]).then_inc(f_pT, 1)
                if 3 <= v < 3 + 2 * NT:
                    w = v - 3
                    t, par = divmod(w, 2)
                    pe.wait_ge(f_pT_sb, after(f_pT_sb, lay, w + 1))
                    if w == 0:
                        pe.wait_ge(f_v_cross, after(f_v_cross, lay, 32))
                        pe.wait_ge(f_qkT_sb, after(f_qkT_sb, lay, 2 * NT - 1))
                    else:
                        pe.wait_ge(f_norm, after(f_norm, lay, w))
                    for c in range(CH):
                        h = 2 * c + par
                        cols = slice((FD + 1) * c, (FD + 1) * (c + 1))
                        pe.matmul(fbank(3)[0:64, cols], pTf[:, w % 2, c, 0:64], v_cross[:, t, h, :],
                                  start=True, stop=True, skip_group_check=True)
                        last = pe.matmul(fbank(3)[64:P, cols], pTf[:, w % 2, c, 64:P], v_own[:, t, h, :],
                                         start=True, stop=True, skip_group_check=True)
                    last.then_inc(f_o, 1)
                if 5 <= v < 5 + 2 * NT and v % 2:
                    t = (v - 5) // 2
                    pe.wait_ge(f_norm, after(f_norm, lay, 2 * t + 2))
                    if t:
                        pe.wait_ge(f_oT_sb, after(f_oT_sb, lay, t))
                    else:
                        pe.wait_ge(f_qkT_sb, after(f_qkT_sb, lay, 2 * NT))
                    transpose4(fbank(4), lambda c: oS[:, t % 2, 2 * c:2 * c + 2, :].rearrange("p h d -> p (h d)")).then_inc(f_oT, 1)
                if 0 <= v < 2 * NT:
                    t, par = divmod(v, 2)
                    if par == 0:
                        pe.wait_ge(f_qkT_sb, after(f_qkT_sb, lay, NT + 1 + t))
                    if v >= 2:
                        pe.wait_ge(f_shifted, after(f_shifted, lay, v - 1))
                    bank = fbank(v % 2)
                    pe.matmul(bank.rearrange("p (c k) -> p c k", c=CH), ident_b[:],
                              band[:, 0 if t else 1, :].unsqueeze(1).broadcast_to([P, CH, P]),
                              start=True, stop=False, skip_group_check=True)
                    for c in range(CH):
                        q0 = P * t
                        even, odd = bank[0:64, P * c:P * c + P], bank[64:P, P * c:P * c + P]
                        pe.matmul(even, qT[:, par, c, q0:q0 + 64], kT[:, c, q0:q0 + 128],
                                  start=False, stop=True, skip_group_check=True)
                        last = pe.matmul(odd, qT[:, par, c, q0 + 64:q0 + 128], kT[:, c, q0 + 64:q0 + 192],
                                         start=False, stop=True, skip_group_check=True)
                    last.then_inc(f_s, 1)
                if k == F_WO:
                    pe.wait_ge(f_oT_sb, after(f_oT_sb, lay, NT))
                    for c in range(CH):
                        last = pe.matmul(fbank(0), wo[:, l, c, :], oT[:, c, :], start=(c == 0), stop=(c == CH - 1))
                    last.then_inc(f_wo, 1)
                if k == F_LN:
                    pe.wait_ge(f_shift, after(f_shift, lay, 4))
                    pe.matmul(fbank(1), mean_w[:], hT[:], start=True, stop=True).then_inc(f_ln_mean, 1)
                if k == F_LN + 3:
                    pe.wait_ge(f_ln_sq, after(f_ln_sq, lay, 1))
                    variance(fbank(1), sqf[:, 0, :]).then_inc(f_ln_var, 1)
                if k == F_LN + 5:
                    pe.wait_ge(f_ln_rsqrt, after(f_ln_rsqrt, lay, RSQRT_STEPS))
                    spread(fbank(2), rstd_f).then_inc(f_ln_spread, 1)
                for n, j, when in ((0, 0, 0), (0, 1, 0), (0, 2, 0), (1, 0, 1), (1, 1, 1), (1, 2, 3)):
                    if k == F_MLP + when:
                        j0, w = HCH[j]
                        j0 += HID * (1 - n)
                        if (n, j) == (0, 0):
                            pe.wait_ge(f_ln_gb, after(f_ln_gb, lay, 1))
                        if (n, j) == (1, 2):
                            pe.wait_ge(f_gelu, after(f_gelu, lay, 1))
                        pe.matmul(fbank(3 + len(HCH) * n + j)[0:w], w1[:, l, j0:j0 + w], nT[:],
                                  start=True, stop=True).then_inc(f_w1, 1)
                if k == F_MLP + 5:
                    pe.wait_ge(f_hid, after(f_hid, lay, len(HCH)))
                    for j, (_, w) in enumerate(HCH):
                        last = pe.matmul(fbank(4), w2[0:w, l, j, :], hid[0:w, j, :], start=(j == 0), stop=(j == len(HCH) - 1))
                    last.then_inc(f_w2, 1)

            for k in range(A_TICKS):
                attention(k, 0, True)
            for k in range(A_FRONT):
                attention(k, 1, False)
            pe.wait_ge(layer_in, N_LAYER)
            pe.wait_ge(layer_tables, N_TABLES)
            with pe.Fori(0, SEQS - 2) as i:
                for stage, ahead, k in MERGED:
                    if stage == "A":
                        attention(k, i + ahead, False)
                    else:
                        layers(k, i)
            for stage, ahead, k in MERGED:
                if stage == "F":
                    layers(k, SEQS - 2)
                elif ahead == 1:
                    attention(k, SEQS - 1, False)
            for k in range(F_TICKS):
                layers(k, SEQS - 1)

def kernel(L0_attn_x, L0_attn_Wqkv, L0_attn_Wo, L0_attn_log_xi, L0_attn_pi_gate_logit,
           L0_attn_e_gate_logit, L0_ffn_wqkv, L0_ffn_q_scale, L0_ffn_k_scale, L0_ffn_wo,
           L0_ffn_ln_g, L0_ffn_ln_b, L0_ffn_w1, L0_ffn_b1, L0_ffn_w2, L0_ffn_b2):
    import math

    import numpy as np
    import concourse.bacc as bacc
    from concourse.bass_utils import run_bass_kernel_spmd

    f32 = np.float32
    rows = np.arange(P)
    par, dim, pair = rows // 64, (rows % 64) // PAIRS, rows % PAIRS
    head = 2 * pair + par
    order = np.array([2 * p + a for a in range(2) for p in range(PAIRS)])

    neg = f32(-1e30)
    q_, k_ = np.arange(P)[:, None], np.arange(P)[None, :]
    causal = np.stack([np.where(k_ <= q_, f32(0), neg), np.where(k_ >= q_, f32(0), neg)], 1).astype(f32)
    a, b = np.arange(WIN)[:, None], np.arange(WIN)[None, :]
    own, before = np.where(b <= a, f32(0), neg), np.where(b >= a, f32(0), neg)
    none = np.full((WIN, WIN), neg)
    band = np.stack([np.block([[before, own], [before, own]]), np.block([[none, own], [before, own]])], 1).astype(f32)
    kfrac = np.arange(0, AD, 2, dtype=f32) / f32(AD)
    inv = (f32(math.pi) ** (f32(1.0) - kfrac)).astype(f32)
    pos = np.arange(TOK, dtype=f32)
    posfreq = (pos[None, :] * inv[dim // 2][:, None]).astype(f32)
    sign = np.where(dim % 2 == 0, f32(-1), f32(1)).astype(f32)[:, None]
    half = np.arange(0, FD, 2, dtype=f32)
    inv_freq = (f32(1.0) / (f32(10000.0) ** (half / f32(FD)))).astype(f32)
    freqs = (pos[:, None] * inv_freq[None, :]).astype(f32)
    freqs = np.concatenate([freqs, freqs], -1).astype(np.float64)
    base = (half + f32(0.4 * FD)) / f32(1.4 * FD)
    power = (pos - f32(TOK // 2)) / f32(WIN // 2)
    scale = (base[None, :] ** power[:, None]).astype(f32)
    scale = np.concatenate([scale, scale], -1).astype(np.float64)
    rsign = np.where(np.arange(FD) < FD // 2, -1.0, 1.0)
    cos, sin = np.cos(freqs), np.sin(freqs) * rsign
    rope = np.stack([8.0 * cos * scale, 8.0 * sin * scale, cos / scale, sin / scale]).astype(f32)
    rope = rope.reshape(4, NT, P, FD).transpose(2, 0, 1, 3)

    W = np.asarray(L0_attn_Wqkv)
    at = head * AD + dim
    swapped = head * AD + (dim ^ 1)
    awqk = np.stack([W[at].T, W[swapped].T, W[DM + at].T, W[DM + swapped].T], 1)
    b1 = np.zeros((LAYERS, P, 2, len(HCH)), f32)
    for j, (j0, w) in enumerate(HCH):
        for s in range(2):
            b1[:, :w, s, j] = np.asarray(L0_ffn_b1)[:, HID * s + j0:HID * s + j0 + w]
    qk = np.stack([np.asarray(L0_ffn_q_scale), np.asarray(L0_ffn_k_scale)], 1)
    arrays = {
        "x": np.asarray(L0_attn_x),
        "ident": np.eye(P, dtype=f32), "causal": causal, "band": band, "posfreq": posfreq,
        "pos": np.broadcast_to(pos, (AH, TOK)), "sign": sign, "rope": rope,
        "awqk": awqk, "awv": W[2 * DM:].T, "awo": np.asarray(L0_attn_Wo).T,
        "pi_gate": np.asarray(L0_attn_pi_gate_logit)[head][:, None],
        "log_xi": np.asarray(L0_attn_log_xi)[order][:, None],
        "e_gate": np.asarray(L0_attn_e_gate_logit)[order][:, None],
        "wqkv": np.asarray(L0_ffn_wqkv), "wo": np.asarray(L0_ffn_wo), "w1": np.asarray(L0_ffn_w1),
        "w2": np.asarray(L0_ffn_w2), "qkscale": np.broadcast_to(qk[None], (P,) + qk.shape),
        "ln_gb": np.stack([np.asarray(L0_ffn_ln_g).T, np.asarray(L0_ffn_ln_b).T], 2), "b1": b1,
        "b2": np.asarray(L0_ffn_b2).T,
    }
    arrays = {f"in_{k}": np.ascontiguousarray(v) for k, v in arrays.items()}
    nc = bacc.Bacc("TRN2", target_bir_lowering=False, num_devices=1)
    d = {k[3:]: nc.dram_tensor(k, v.shape, mybir.dt.from_np(v.dtype), kind="ExternalInput").ap()
         for k, v in arrays.items()}
    out = nc.dram_tensor("out", (SEQS, TOK, DM), F32, kind="ExternalOutput").ap()
    build(nc, d["x"],
          [d[k] for k in ("ident", "causal", "band", "posfreq", "pos", "sign", "rope")],
          [d[k] for k in ("awqk", "awv", "awo")], [d[k] for k in ("pi_gate", "log_xi", "e_gate")],
          [d[k] for k in ("wqkv", "wo", "w1", "w2")],
          [d[k] for k in ("qkscale", "ln_gb", "b1", "b2")], out)
    r = run_bass_kernel_spmd(nc, [arrays], core_ids=[0])
    return r.results[0]["out"]
```
